# Optimizing a Trainium2 kernel written in Bass

```python
import numpy as np
import jax
import jax.numpy as jnp

def _softmax(x, axis=-1):
    return jax.nn.softmax(x, axis=axis)

def _gelu(x):
    return jax.nn.gelu(x, approximate=True)

def _silu(x):
    return jax.nn.silu(x)

def _sigmoid(x):
    return jax.nn.sigmoid(x)

def _layernorm(x, axis=-1, eps=1e-05):
    m = jnp.mean(x, axis=axis, keepdims=True)
    v = jnp.var(x, axis=axis, keepdims=True)
    return (x - m) / jnp.sqrt(v + eps)

def _scatter_add(tgt, idx, src, axis=0):
    return tgt.at[idx].add(src)

def _segment_sum(src, seg, n):
    return jax.ops.segment_sum(src, seg, n)
kernel_name = 'mk_gps_d1_gnn_r16_05cc9f'

def setup_inputs(seed: int=0):
    np.random.seed(seed)
    _w = jnp.asarray

    def _rec_inputs():
        import jax
        import jax.numpy as jnp
        _gk = jax.random.key(seed)
        x = -6.415e-05 + 1 * jax.random.normal(jax.random.fold_in(_gk, 1), (625, 1024), jnp.float32)
        _s = jax.random.randint(jax.random.fold_in(_gk, 2), (10000,), 0, 625, jnp.int32)
        _d = jax.random.randint(jax.random.fold_in(_gk, 3), (10000,), 0, 625, jnp.int32)
        _loop = jnp.arange(625, dtype=jnp.int32)
        src = jnp.concatenate([_s, _d, _loop])
        dst = jnp.concatenate([_d, _s, _loop])
        _o = jnp.argsort(dst, stable=True)
        src = src[_o]
        dst = dst[_o]
        return (x, src, dst)
    x, src, dst = _rec_inputs()

    def _L0_gnn_setup():
        import jax, jax.numpy as jnp
        import numpy as np
        NEG_SLOPE = 0.1
        EPS = 1e-05
        key = jax.random.key(seed)
        k1, k2, k3, k4, k5 = jax.random.split(key, 5)
        N, E, DIN, DOUT = (625, 10000, 1024, 1024)
        x = jax.random.normal(k1, (N, DIN), dtype=jnp.float32)
        W = jax.random.normal(k2, (DIN, DOUT), dtype=jnp.float32) * 0.02
        a = jax.random.normal(k3, (1, 2 * DOUT), dtype=jnp.float32) * 0.02
        src = jax.random.randint(k4, (E,), 0, N, dtype=jnp.int64)
        dst = jax.random.randint(k5, (E,), 0, N, dtype=jnp.int64)
        return {'x': x, 'W': W, 'a': a, 'src': src, 'dst': dst}
    _L0_gnn_all = _L0_gnn_setup()
    _L0_gnn_in = {k: v for k, v in _L0_gnn_all.items() if k in ('W', 'a')}
    del _L0_gnn_all

    def _L0_mix_setup():
        import jax, jax.numpy as jnp
        import numpy as np
        B, N, D, H = (4, 256, 1024, 16)
        HD = D // H

        def _kernel(x):
            return jax.nn.elu(x) + 1.0
        key = jax.random.key(seed)
        k1, k2, k3, k4 = jax.random.split(key, 4)
        x = jax.random.normal(k1, (B, N, D), dtype=jnp.float32)
        w_qkv = jax.random.normal(k2, (3 * D, D), dtype=jnp.float32) * (1.0 / np.sqrt(D))
        w_out = jax.random.normal(k3, (D, D), dtype=jnp.float32) * (1.0 / np.sqrt(D))
        b_out = jax.random.normal(k4, (D,), dtype=jnp.float32) * 0.01
        return {'x': x, 'w_qkv': w_qkv, 'w_out': w_out, 'b_out': b_out}
    _L0_mix_all = _L0_mix_setup()
    _L0_mix_in = {k: v for k, v in _L0_mix_all.items() if k in ('w_qkv', 'w_out', 'b_out')}
    del _L0_mix_all

    def _L0_ffn_setup():
        import jax, jax.numpy as jnp
        import numpy as np
        B, S, H = (4, 128, 1024)
        E, K = (8, 2)
        I_R, I_S = (4 * H, 8 * H)
        CAP_FACTOR = 1.25
        SCALE = 1.0
        key = jax.random.key(seed)
        ks = jax.random.split(key, 9)
        std = 0.02
        return {'x': jax.random.normal(ks[0], (B, S, H), jnp.float32), 'router_w': std * jax.random.normal(ks[1], (E, H), jnp.float32), 'rg': std * jax.random.normal(ks[2], (E, H, I_R), jnp.float32), 'ru': std * jax.random.normal(ks[3], (E, H, I_R), jnp.float32), 'rd': std * jax.random.normal(ks[4], (E, I_R, H), jnp.float32), 'sg': std * jax.random.normal(ks[5], (H, I_S), jnp.float32), 'su': std * jax.random.normal(ks[6], (H, I_S), jnp.float32), 'sd': std * jax.random.normal(ks[7], (I_S, H), jnp.float32)}
    _L0_ffn_all = _L0_ffn_setup()
    _L0_ffn_in = {k: v for k, v in _L0_ffn_all.items() if k in ('router_w', 'rg', 'ru', 'rd', 'sg', 'su', 'sd')}
    del _L0_ffn_all
    return {'x': x, 'src': src, 'dst': dst, 'L0_gnn_W': _L0_gnn_in['W'], 'L0_gnn_a': _L0_gnn_in['a'], 'L0_mix_w_qkv': _L0_mix_in['w_qkv'], 'L0_mix_w_out': _L0_mix_in['w_out'], 'L0_mix_b_out': _L0_mix_in['b_out'], 'L0_ffn_router_w': _L0_ffn_in['router_w'], 'L0_ffn_rg': _L0_ffn_in['rg'], 'L0_ffn_ru': _L0_ffn_in['ru'], 'L0_ffn_rd': _L0_ffn_in['rd'], 'L0_ffn_sg': _L0_ffn_in['sg'], 'L0_ffn_su': _L0_ffn_in['su'], 'L0_ffn_sd': _L0_ffn_in['sd']}

def reference(x, src, dst, L0_gnn_W, L0_gnn_a, L0_mix_w_qkv, L0_mix_w_out, L0_mix_b_out, L0_ffn_router_w, L0_ffn_rg, L0_ffn_ru, L0_ffn_rd, L0_ffn_sg, L0_ffn_su, L0_ffn_sd):
    import jax
    import jax.numpy as jnp

    def _L0_gnn_ref(x, W, a, src, dst):
        import jax, jax.numpy as jnp
        import numpy as np
        NEG_SLOPE = 0.1
        EPS = 1e-05
        N = x.shape[0]
        d = W.shape[1]
        h = x @ W
        a_l, a_r = (a[0, :d], a[0, d:])
        al = h @ a_l
        ar = h @ a_r
        e = jnp.exp(-jax.nn.leaky_relu(al[src] + ar[dst], negative_slope=NEG_SLOPE))
        rowsum = jax.ops.segment_sum(e, src, num_segments=N)
        h_prime = jax.ops.segment_sum(e[:, None] * h[dst], src, num_segments=N)
        h_prime = h_prime / (rowsum[:, None] + EPS)
        return jax.nn.elu(h_prime)

    def _L0_mix_ref(x, w_qkv, w_out, b_out):
        import jax, jax.numpy as jnp
        import numpy as np
        B, N, D, H = (4, 256, 1024, 16)
        HD = D // H

        def _kernel(x):
            return jax.nn.elu(x) + 1.0
        b, n, d = x.shape
        qkv = x @ w_qkv.T
        qkv = qkv.reshape(b, n, 3, H, HD)
        q, k, v = (qkv[:, :, 0], qkv[:, :, 1], qkv[:, :, 2])
        q = _kernel(q)
        k = _kernel(k)
        kv = jnp.einsum('bnhd,bnhm->bhdm', k, v)
        z = 1.0 / (jnp.einsum('bnhd,bhd->bnh', q, k.sum(axis=1)) + 1e-06)
        out = jnp.einsum('bnhd,bhdm,bnh->bnhm', q, kv, z)
        out = out.reshape(b, n, d)
        return out @ w_out.T + b_out

    def _L0_ffn_ref(x, router_w, rg, ru, rd, sg, su, sd):
        import jax, jax.numpy as jnp
        import numpy as np
        B, S, H = (4, 128, 1024)
        E, K = (8, 2)
        I_R, I_S = (4 * H, 8 * H)
        CAP_FACTOR = 1.25
        SCALE = 1.0
        b, s, h = x.shape
        T = b * s
        capacity = max(int(CAP_FACTOR * T / E), 1)
        xf = x.reshape(T, h)
        eps = jnp.finfo(x.dtype).eps
        xn = xf * jax.lax.rsqrt(jnp.mean(xf * xf, axis=-1, keepdims=True) + eps)
        logits = xn @ router_w.T
        probs = jax.nn.softmax(logits, axis=-1)
        topk_p, topk_i = jax.lax.top_k(probs, K)
        rw = topk_p / jnp.sum(topk_p, axis=-1, keepdims=True)
        one_hot = jax.nn.one_hot(topk_i, E, dtype=x.dtype)
        mask = one_hot.sum(1)
        wdense = (one_hot * rw[..., None]).sum(1)
        sel = mask.T.astype(bool)
        order = jnp.argsort(~sel, axis=1, stable=True)
        dispatch = order[:, :capacity]
        count = sel.sum(axis=1)
        valid = (jnp.arange(capacity)[None, :] < count[:, None]).astype(x.dtype)
        xg = xf[dispatch]
        gate = jax.nn.silu(jnp.einsum('ech,ehi->eci', xg, rg))
        up = jnp.einsum('ech,ehi->eci', xg, ru)
        eout = jnp.einsum('eci,eih->ech', gate * up, rd)
        w = jnp.take_along_axis(wdense.T, dispatch, axis=1)
        contrib = eout * (w * valid)[..., None]
        routed = jnp.zeros_like(xf).at[dispatch.reshape(-1)].add(contrib.reshape(-1, h))
        shared = jax.nn.silu(x @ sg) * (x @ su) @ sd
        return shared + SCALE * routed.reshape(b, s, h)
    xn = _layernorm(x, axis=-1)
    x = x + _L0_gnn_ref(xn, L0_gnn_W, L0_gnn_a, src, dst) + _L0_mix_ref(xn[None], L0_mix_w_qkv, L0_mix_w_out, L0_mix_b_out)[0]
    x = x + _L0_ffn_ref(_layernorm(x, axis=-1)[None], L0_ffn_router_w, L0_ffn_rg, L0_ffn_ru, L0_ffn_rd, L0_ffn_sg, L0_ffn_su, L0_ffn_sd)[0]
    return x

_drawn_inputs = setup_inputs


def setup_inputs(seed=0):
    import zlib

    import numpy as np

    out = dict(_drawn_inputs(seed))
    spreads = {}
    factors = {'L0_mix_b_out': 2.704}
    for name, (base, spread) in spreads.items():
        noise = np.random.default_rng([zlib.crc32(name.encode()), seed]).standard_normal(out[name].shape)
        drawn = base * np.exp(spread * noise) if base else spread * noise
        out[name] = jnp.asarray(drawn.astype(out[name].dtype))
    for name, factor in factors.items():
        out[name] = (out[name] * factor).astype(out[name].dtype)
    return out
```

```python
from contextlib import ExitStack

import numpy as np

import concourse.bass as bass
from concourse import mybir

F32 = mybir.dt.float32
F32R = mybir.dt.float32r
BF16 = mybir.dt.bfloat16
F16 = mybir.dt.float16
I32 = mybir.dt.int32
U32 = mybir.dt.uint32
ALU = mybir.AluOpType
ACT = mybir.ActivationFunctionType
AXX = mybir.AxisListType.X

P = 128
N = 625
TP = 125
NT = N // TP
D = 1024
KT = D // P
HALF = 512
E = 8
CAP = int(1.25 * N / E)
IR = 4 * D
IS = 8 * D
NE = 20625
EC = NE // TP
EG = 28
NG = 6
ECP = EG * NG
DIGIT = 4096.0
SC = (N + 1) // 2
NP2 = 626
HALVES = ((0, 314), (314, 312))
HEADS = 16
HD = 64
PAIRS = HEADS // 2
EPS = 1e-5
RMS_EPS = float(np.finfo(np.float32).eps)
FMAX = float(np.finfo(np.float32).max)
SLOPE = 0.1
Q = 4
U = 30
RING = 10
RAW = 3
BLK = 15
STEPS = E * Q
USED0 = RING + 1
ONE = 1
UNITS_GATE = (0, 12)
UNIT_S = 8
UNIT_SD = 20
UNIT_RD = 22
A_END = (8, 20)
S_END = (10, 12)
GATE, UP, X0, R0 = 0, 1, 2, 6
T_BANK = (R0, GATE)


def unit_source(u):
    def rows(half):
        return lambda t: t[:, half * 1024:(half + 1) * 1024]

    def columns(j):
        return lambda t: t[:].rearrange("p (k n) -> p k n", k=KT)[:, :, j * P:(j + 1) * P]

    if u < UNIT_S:
        return u // 2, rows(u % 2)
    if u < UNITS_GATE[1]:
        return 4 + u % 2, columns((u - UNIT_S) // 2)
    return u // 2, rows(u % 2)


def unit_view(t, u):
    if UNIT_S <= u < UNITS_GATE[1]:
        return t[:].rearrange("p (k n) -> p k n", k=KT)
    return t[:]


SOURCE = [unit_source(u) for u in range(U)]
LAST_UNIT = [max(u for u in range(U) if SOURCE[u][0] == b) for b in range(BLK)]


def build(nc, x, src, dst, W, a, w_qkv, w_out, b_out, router_w, rg, ru, rd, sg, su, sd, out):
    ctx = ExitStack()
    sems = {}

    def sem(name):
        if name not in sems:
            sems[name] = ctx.enter_context(nc.semaphore(name))
        return sems[name]

    cursor = [16512]

    def place(name, shape, dt, at=None):
        size = int(np.prod(shape[1:])) * mybir.dt.size(dt)
        size = (size + 31) // 32 * 32
        off = cursor[0] if at is None else at
        if at is None:
            cursor[0] += size
        return nc.alloc_sbuf_tensor_at(name, shape, dt, offset=off)

    def here():
        return cursor[0]

    resid = place("resid", [TP, NT, D], F32)
    ident = place("ident", [P, P], F32)
    ones = place("ones", [P, P], F32)
    tri = place("tri", [P, P], F32)
    pos_u = place("pos_u", [TP, 2, 8], U32)
    wts = place("wts", [TP, 2, 8], F32)
    tok_u = place("tok_u", [CAP, E], U32)
    raw_at = here()
    raw = [place(f"raw{r}", [P, 2048], F32) for r in range(RAW)]
    shared_at = here()
    yT_hi = place("yT_hi", [P, KT, NP2], F32R)
    yT_lo = place("yT_lo", [P, KT, NP2], F32R)
    conv_at = here()
    c_hi = [place(f"c_hi{s}", [P, 1024], F32R) for s in range(RING)]
    c_lo = [place(f"c_lo{s}", [P, 1024], F32R) for s in range(RING)]
    xgT_hi = place("xgT_hi", [P, KT * CAP], F32R)
    xgT_lo = place("xgT_lo", [P, KT * CAP], F32R)
    sh_hi = place("sh_hi", [P, 2, NP2], F32R)
    sh_lo = place("sh_lo", [P, 2, NP2], F32R)
    s_silu = [place(f"s_silu{i}", [P, 314], F32) for i in range(2)]
    s_h = [place(f"s_h{i}", [P, 314], F32) for i in range(2)]
    r_silu = place("r_silu", [CAP, HALF], F32)
    r_h = [place(f"r_h{i}", [CAP, HALF], F32) for i in range(2)]
    hT_hi = place("hT_hi", [P, 8 * CAP], F32R)
    hT_lo = place("hT_lo", [P, 8 * CAP], F32R)
    eout = place("eout", [CAP, D], F32)
    eout_st = place("eout_st", [CAP, D], F32)
    assert here() <= 229344, here()
    cursor[0] = raw_at
    a_bc = place("a_bc", [TP, 2 * D], F32)
    zt = [place(f"zt{i}", [TP, N], F32) for i in range(2)]
    ez = [place(f"ez{i}", [TP, N], F32) for i in range(2)]
    albc = place("albc", [TP, N], F32)
    assert here() <= shared_at, (here(), shared_at)
    wl = [place(f"wl{i}", [P, 4 * D], F32, at=shared_at + i * 16384) for i in range(2)]
    small_at = shared_at + 2 * 16384
    cursor[0] = small_at
    mv = place("mv", [TP, NT, 2], F32)
    st6 = place("st6", [TP, 2, 6], F32)
    rstd = place("rstd", [TP, NT], F32)
    al = place("al", [TP, NT, 2], F32)
    rinv = place("rinv", [TP, NT], F32)
    diag = place("diag", [TP, NT, TP], F32)
    rw_in = place("rw_in", [E, D], F32)
    assert here() <= conv_at
    cursor[0] = conv_at
    xnT = place("xnT", [P, KT, NP2], F32)
    wT_at = here()
    wT = place("wT", [P, KT, HALF], F32)
    h_at = here()
    h = place("h", [TP, NT, D], F32)
    k_at = here()
    kk = place("kk", [TP, NT, D], F32)
    v_at = here()
    vv = place("vv", [TP, NT, D], F32)
    C = place("C", [TP, NT, SC, 2], F32)
    b_bc = place("b_bc", [TP, D], F32)
    KV = place("KV", [P, PAIRS, P], F32)
    KS = place("KS", [P, PAIRS, P], F32)
    late_at = here()
    late_end = 229344
    rwT_hi = place("rwT_hi", [P, KT, E], F32R)
    rwT_lo = place("rwT_lo", [P, KT, E], F32R)
    rr = {n: place("rr_" + n, [TP, 8], F32) for n in
          ("ms", "r", "mx", "sum", "den", "k1", "k2", "p1", "p2", "tok")}
    iota8 = place("iota8", [TP, E], F32)
    iotaslot = place("iotaslot", [TP, E], F32)
    iotacap = place("iotacap", [TP, CAP], F32)
    assert here() <= late_end, here()
    scr = place("scr", [TP, D], F32, at=k_at)
    xn = place("xn", [TP, NT, D], F32, at=h_at)
    outT = place("outT", [P, KT, NP2], F32, at=h_at)
    sq = place("sq", [TP, D], F32, at=h_at)
    y = place("y", [TP, NT, D], F32, at=k_at)
    cursor[0] = k_at
    oh_d = [place(f"oh_d{i}", [TP, 640], BF16) for i in range(4)]
    oh_s = [place(f"oh_s{i}", [TP, 320], BF16) for i in range(4)]
    iota_h = place("iota_h", [TP, 640], F16)
    src_i = place("src_i", [TP, ECP], I32)
    dst_i = place("dst_i", [TP, ECP], I32)
    src_f = place("src_f", [TP, ECP], F32)
    dst_f = place("dst_f", [TP, ECP], F32)
    dig_f = place("dig_f", [TP, ECP], F32)
    tmp_i = place("tmp_i", [TP, ECP], I32)
    assert here() <= v_at
    v_int = place("v_int", [TP, NT, SC], I32, at=v_at)
    v_lo = place("v_lo", [TP, NT, SC], I32, at=v_at + 6272)
    v_hi = place("v_hi", [TP, NT, SC], I32, at=v_at + 2 * 6272)
    cursor[0] = raw_at
    fm = [place(f"fm{i}", [P, HALF], F32) for i in range(2)]
    fe = [place(f"fe{i}", [P, HALF], F32) for i in range(2)]
    qT = [place(f"qT{i}", [P, NP2], F32) for i in range(2)]
    dn = [place(f"dn{i}", [P, 320], F32) for i in range(2)]
    dr = [place(f"dr{i}", [P, 320], F32) for i in range(2)]
    gscr = [place(f"gscr{i}", [TP, HALF], F32) for i in range(2)]
    assert here() <= shared_at
    cursor[0] = v_at
    S = place("S", [TP, NT, E, CAP], F32)
    xg = [place(f"xg{i}", [CAP, D], F32) for i in range(4)]
    assert here() <= late_at
    cursor[0] = conv_at
    st_hi = [place(f"st_hi{i}", [P, KT * CAP], F32R) for i in range(2)]
    st_lo = [place(f"st_lo{i}", [P, KT * CAP], F32R) for i in range(2)]
    rt = {n: place("rt_" + n, [TP, NT, E], F32) for n in
          ("lg", "pr", "v8", "if8", "oh1", "oh2", "mask", "rank", "keep", "slot", "t1", "t2")}
    i8 = place("rt_i8", [TP, NT, E], U32)
    assert here() <= wT_at
    cursor[0] = conv_at
    g = [[place(f"g{c}_{t}", [TP, D], F32) for t in range(NT)] for c in range(2)]

    PS = [ctx.enter_context(nc.psum_tensor(f"ps{b}", [P, HALF], F32)) for b in range(8)]

    y_rows = nc.dram_tensor("y_rows", [N, D], F32).ap()
    xgT_hi_d = nc.dram_tensor("xgT_hi_d", [E, P, KT * CAP], F32).ap()
    xgT_lo_d = nc.dram_tensor("xgT_lo_d", [E, P, KT * CAP], F32).ap()
    eout_d = nc.dram_tensor("eout_d", [(E + 1) * CAP, D], F32).ap()

    x_t = x.rearrange("(t p) d -> t p d", p=TP)
    out_t = out.rearrange("(t p) d -> t p d", p=TP)
    y_rows_t = y_rows.rearrange("(t p) d -> t p d", p=TP)
    rg_v = rg.rearrange("e (k p) (q n) -> e q p k n", p=P, n=HALF)
    ru_v = ru.rearrange("e (k p) (q n) -> e q p k n", p=P, n=HALF)
    rd_v = rd.rearrange("e (q k p) n -> e q p k n", k=8, p=P)
    sg_v = sg.rearrange("(k p) (i n) -> i p k n", p=P, n=256)
    su_v = su.rearrange("(k p) (i n) -> i p k n", p=P, n=256)
    sd_v = sd.rearrange("(i k p) n -> i p k n", k=2, p=P)
    W_v = W.rearrange("(k p) (c n) -> c p k n", p=P, n=HALF)
    wq_v = w_qkv.rearrange("(c s p) k -> c p s k", s=4, p=P)
    wo_v = w_out.rearrange("(c s p) k -> c p s k", s=4, p=P)
    loads = [W_v[0], W_v[1], wq_v[2], wq_v[3], wq_v[4], wq_v[5], wq_v[0], wq_v[1], wo_v[0], wo_v[1]]
    GROUPS = len(loads) - 2
    TB = (5, 6, 7)

    block = ctx.enter_context(nc.Block())

    @block.sync
    def _(sp):
        sp.dma_start(src_i[:, 0:EC], src.rearrange("(p c) -> p c", p=TP)).then_inc(sem("src_in"), 16)
        sp.dma_start(dst_i[:, 0:EC], dst.rearrange("(p c) -> p c", p=TP)).then_inc(sem("dst_in"), 16)
        for n, v in enumerate(loads):
            if n in (2, 3):
                sp.wait_ge(sem("h_ps"), (n - 1) * NT)
            elif n >= 4:
                sp.wait_ge(sem("wT_ps"), (n - 3) * KT)
            d = wl[n % 2][:].rearrange("p (k n) -> p k n", k=v.shape[1])
            sp.dma_start(d, v).then_inc(sem(f"wl_in{n % 2}"), 16)
        for t in range(NT):
            sp.wait_ge(sem("y_done"), t + 1)
            sp.dma_start(y_rows_t[t], y[:, t, :]).then_inc(sem("y_stored"), 16)
        sp.wait_ge(sem("num_used"), 2 * PAIRS)
        for e in range(E):
            sp.wait_ge(sem("st_lo_done"), 2 * (e + 1))
            sp.dma_start(xgT_hi_d[e], st_hi[e % 2][:].bitcast(F32)).then_inc(sem(f"st_stored{e % 2}"), 16)
            sp.dma_start(xgT_lo_d[e], st_lo[e % 2][:].bitcast(F32)).then_inc(sem(f"st_stored{e % 2}"), 16)
        with sp.Fori(0, E) as e:
            with sp.Fori(0, Q) as q:
                it = sp.snap(e * Q + q)
                blocks = [rg_v[e, q * 2][:, 0:4, :], rg_v[e, q * 2][:, 4:8, :],
                          ru_v[e, q * 2][:, 0:4, :], ru_v[e, q * 2][:, 4:8, :],
                          sg_v[it], su_v[it],
                          rg_v[e, q * 2 + 1][:, 0:4, :], rg_v[e, q * 2 + 1][:, 4:8, :],
                          ru_v[e, q * 2 + 1][:, 0:4, :], ru_v[e, q * 2 + 1][:, 4:8, :],
                          sd_v[it]] + [rd_v[e, q][:, 2 * r:2 * r + 2, :] for r in range(4)]
                for b, v in enumerate(blocks):
                    if b >= RAW:
                        sp.wait_ge(sem("lo_done"), it * U + (U + LAST_UNIT[b - RAW] + 1))
                    else:
                        sp.wait_ge(sem("lo_done"), it * U + (LAST_UNIT[b - RAW + BLK] + 1))
                    sp.dma_start(raw[b % RAW][:].rearrange("p (k n) -> p k n", k=v.shape[1]),
                                 v).then_inc(sem(f"raw_in{b % RAW}"), 16)
        for t in range(NT):
            sp.wait_ge(sem("out_done"), t + 1)
            sp.dma_start(out_t[t], resid[:, t, :]).then_inc(sem("out_stored"), 16)
        sp.wait_ge(sem("out_stored"), 16 * NT)

    @block.gpsimd
    def _(pool):
        chain = [0]

        def link(ins):
            chain[0] += 1
            ins.then_inc(sem("pool_chain"), 1)
            pool.wait_ge(sem("pool_chain"), chain[0])

        for t in range(NT):
            pool.dma_start(resid[:, t, :], x_t[t]).then_inc(sem(f"x_in{t}"), 16)
        pool.dma_start(a_bc[:], a[0, :].partition_broadcast(TP)).then_inc(sem("a_in"), 16)
        pool.dma_start(b_bc[:], b_out.partition_broadcast(TP)).then_inc(sem("b_in"), 16)
        pool.dma_start(rw_in[:], router_w).then_inc(sem("rw_in"), 16)
        link(nc.gpsimd.iota(iota_h[:], [[1, 640]], base=0, channel_multiplier=0,
                            allow_small_or_imprecise_dtypes=True))
        link(nc.gpsimd.memset(src_i[:, EC:ECP], -2))
        nc.gpsimd.memset(dst_i[:, EC:ECP], -2).then_inc(sem("iota_done"), 1)
        link(nc.gpsimd.memset(ones[:], 1.0))
        link(nc.gpsimd.affine_select(out=ident[:], in_=ones[:], pattern=[[-1, P]], compare_op=ALU.is_equal,
                                     fill=0.0, base=0, channel_multiplier=1))
        link(nc.gpsimd.affine_select(out=tri[:], in_=ones[:], pattern=[[1, P]], compare_op=ALU.is_gt,
                                     fill=0.0, base=0, channel_multiplier=-1))
        link(nc.gpsimd.memset(C[:], 0.0))
        link(nc.gpsimd.memset(KV[:], 0.0))
        link(nc.gpsimd.memset(KS[:], 0.0))
        link(nc.gpsimd.iota(iota8[:], [[1, E]], base=0, channel_multiplier=0, allow_small_or_imprecise_dtypes=True))
        link(nc.gpsimd.iota(iotaslot[:], [[CAP, E]], base=CAP, channel_multiplier=0,
                            allow_small_or_imprecise_dtypes=True))
        link(nc.gpsimd.iota(iotacap[:], [[1, CAP]], base=0, channel_multiplier=0,
                            allow_small_or_imprecise_dtypes=True))
        nc.gpsimd.iota(rr["tok"][:], [[TP, 8]], base=0, channel_multiplier=1,
                       allow_small_or_imprecise_dtypes=True).then_inc(sem("const_done"), 1)
        Ci = C[:].bitcast(I32)
        with pool.Fori(0, NG) as gr:
            pool.wait_ge(sem("digits"), gr * 2 + 2)
            nc.gpsimd.tensor_tensor(Ci[:, :, :, 0], Ci[:, :, :, 0], v_lo[:], ALU.add).then_inc(sem("counted"), 1)
            nc.gpsimd.tensor_tensor(Ci[:, :, :, 1], Ci[:, :, :, 1], v_hi[:], ALU.add).then_inc(sem("counted"), 1)
        pool.wait_ge(sem("b_in"), 16)
        pool.wait_ge(sem("xn_done"), NT)
        for t in range(NT):
            nc.gpsimd.tensor_tensor(resid[:, t, :], resid[:, t, :], b_bc[:], ALU.add).then_inc(sem("biased"), 1)
        pool.wait_ge(sem("y_stored"), 16 * NT)
        pool.wait_ge(sem("tok_done"), 1)
        for e in range(E):
            if e >= 4:
                pool.wait_ge(sem("xgT_ps"), 2 * (e - 3))
            nc.gpsimd.indirect_dma_start(
                out=xg[e % 4][:], out_offset=None, in_=y_rows,
                in_offset=bass.IndirectOffsetOnAxis(ap=tok_u[:, e:e + 1], axis=0)).then_inc(sem(f"xg_in{e % 4}"), 16)
        for i in range(2):
            pool.wait_ge(sem(f"st_stored{i}"), 16 * E)
        link(nc.gpsimd.memset(eout[:], 0.0))
        nc.gpsimd.memset(eout_st[:], 0.0).then_inc(sem("eout_clear"), 1)
        with pool.Fori(0, E) as e:
            pool.wait_ge(sem("unit_used"), e * (Q * U) + (A_END[1] - U + USED0))
            pool.dma_start(xgT_hi[:].bitcast(F32), xgT_hi_d[e]).then_inc(sem("xgT_in"), 16)
            pool.dma_start(xgT_lo[:].bitcast(F32), xgT_lo_d[e]).then_inc(sem("xgT_in"), 16)
            pool.wait_ge(sem("rd_added"), e * (2 * Q) + 2)
            pool.sem_inc(sem("turns"), 1)
            nc.gpsimd.tensor_copy(eout_st[:], eout[:]).then_inc(sem("eout_copied"), 1)
            pool.wait_ge(sem("eout_copied"), e + 1)
            pool.sem_inc(sem("turns"), 1)
            nc.gpsimd.memset(eout[:], 0.0).then_inc(sem("eout_clear"), 1)
            pool.dma_start(eout_d[bass.ds(e * CAP, CAP), :], eout_st[:]).then_inc(sem("eout_stored"), 16)
            pool.wait_ge(sem("eout_stored"), e * 16 + 16)
        pool.wait_ge(sem("rd_added"), 2 * Q * E + 2)
        pool.dma_start(eout_d[E * CAP:(E + 1) * CAP, :], eout[:]).then_inc(sem("eout_stored"), 16)
        pool.wait_ge(sem("eout_stored"), 16 * (E + 1))
        pool.wait_ge(sem("sd_added"), 2 * NT * Q * E + ONE)
        for t in range(NT):
            for c in range(2):
                nc.gpsimd.indirect_dma_start(
                    out=g[c][t][:], out_offset=None, in_=eout_d,
                    in_offset=bass.IndirectOffsetOnAxis(ap=pos_u[:, c, t:t + 1], axis=0)).then_inc(
                        sem(f"g_in{c}_{t}"), 16)

    @block.scalar
    def _(act):
        def count_copies(gr):
            for dt in range(NT):
                act.wait_ge(sem("count_done"), gr * NT + dt + 1)
                if dt == 0 and not (isinstance(gr, int) and gr == 0):
                    act.wait_ge(sem("digits"), gr * 2)
                nc.scalar.copy(v_int[:, dt, :], PS[dt][0:TP, 0:SC]).then_inc(sem("count_out"), 1)

        def layernorm_std(n):
            act.wait_ge(sem("var_done"), n)
            nc.scalar.activation(rstd[:], mv[:, :, 1], ACT.Sqrt).then_inc(sem("std_done"), 1)

        layernorm_std(1)
        count_copies(0)
        with act.Fori(1, NG) as gr:
            count_copies(gr)
        for j in range(2 * NT):
            t, half = divmod(j, 2)
            act.wait_ge(sem("xnT_ps"), j + 1)
            nc.scalar.copy(xnT[:, 4 * half:4 * half + 4, t * TP:(t + 1) * TP],
                           PS[TB[j % 3]][:, 0:4 * TP].rearrange("p (k n) -> p k n", k=4)).then_inc(sem("xnT_out"), 1)
        act.wait_ge(sem("rwT_ps"), 1)
        nc.scalar.copy(rwT_hi[:], PS[7][:, 0:KT * E].rearrange("p (k n) -> p k n", k=KT)).then_inc(sem("rwT_hi"), 1)
        for j in range(2 * NT):
            half, t = divmod(j, NT)
            act.wait_ge(sem("h_ps"), j + 1)
            nc.scalar.copy(h[:, t, half * HALF:(half + 1) * HALF], PS[t][0:TP, :]).then_inc(sem("h_out"), 1)

        def wT_copies(gp):
            for k in range(KT):
                act.wait_ge(sem("wT_ps"), gp * KT + k + 1)
                if k == 0 and gp >= 1:
                    name, n = (("kv_ps", NT * gp) if gp <= 4 else ("q_ps", 8 * (gp - 4)) if gp <= 6 else
                               ("o_ps", NT))
                    act.wait_ge(sem(name), n)
                nc.scalar.copy(wT[:, k, :], PS[TB[k % 3]][:, :]).then_inc(sem("wT_out"), 1)

        def feature_exp(n, parts, cols):
            act.wait_ge(sem("fm_done"), n + 1)
            if n >= 2:
                act.wait_ge(sem("fe_used"), n - 1)
            nc.scalar.activation(fe[n % 2][0:parts, 0:cols], fm[n % 2][0:parts, 0:cols],
                                 ACT.Exp).then_inc(sem("fe_done"), 1)

        wT_copies(0)
        for dt in range(NT):
            act.wait_ge(sem("z_done"), dt + 1)
            if dt >= 2:
                act.wait_ge(sem("ez_used"), dt - 1)
            nc.scalar.activation(ez[dt % 2][:], zt[dt % 2][:], ACT.Exp, scale=-1.0).then_inc(sem("ez_done"), 1)
        for t in range(NT):
            feature_exp(t, TP, HALF)
        wT_copies(1)
        for t in range(NT):
            feature_exp(NT + t, TP, HALF)
        for gp in (2, 3):
            wT_copies(gp)
            for t in range(NT):
                act.wait_ge(sem("kv_ps"), gp * NT + t + 1)
                nc.scalar.copy(vv[:, t, (gp - 2) * HALF:(gp - 1) * HALF], PS[t][0:TP, :]).then_inc(sem("v_out"), 1)
        nf = 2 * NT
        for j in range(2 * NT):
            feature_exp(nf + j, TP, HALF)
        nf += 2 * NT
        for gp in (4, 5):
            wT_copies(gp)
            for j in range(4):
                for hf in range(2):
                    feature_exp(nf, P, (313, 312)[hf])
                    nf += 1
        for gp in (6, 7):
            wT_copies(gp)
        layernorm_std(2)
        for t in range(NT):
            act.wait_ge(sem("y_done"), t + 1)
            if t:
                act.wait_ge(sem("ms_done"), t)
            nc.scalar.activation(sq[:], y[:, t, :], ACT.Square,
                                 accum_out=rr["ms"][:, t:t + 1]).then_inc(sem("ms_done"), 1)
            for half in range(2):
                j = 2 * t + half
                act.wait_ge(sem("yT_ps"), j + 1)
                nc.scalar.copy(yT_hi[:, 4 * half:4 * half + 4, t * TP:(t + 1) * TP],
                               PS[TB[j % 3]][:, 0:4 * TP].rearrange("p (k n) -> p k n", k=4)).then_inc(sem("yT_hi"), 1)
        act.wait_ge(sem("rms_done"), 1)
        nc.scalar.activation(rr["r"][:, 0:NT], rr["ms"][:, 0:NT], ACT.Sqrt).then_inc(sem("rms_sqrt"), 1)
        act.wait_ge(sem("lg_done"), 1)
        nc.scalar.activation(rt["pr"][:], rt["lg"][:], ACT.Exp).then_inc(sem("pr_done"), 1)
        for e in range(E):
            if e >= 2:
                act.wait_ge(sem(f"st_stored{e % 2}"), 2 * 16 * (e // 2))
            for half in range(2):
                act.wait_ge(sem("xgT_ps"), 2 * e + half + 1)
                nc.scalar.copy(st_hi[e % 2][:, half * 4 * CAP:(half + 1) * 4 * CAP],
                               PS[(2 * e + half) % 4][:, 0:4 * CAP]).then_inc(sem("st_hi_done"), 1)
        for i in range(2):
            act.wait_ge(sem(f"st_stored{i}"), 16 * E)

        with act.Fori(0, E) as e:
            with act.Fori(0, Q) as q:
                it = act.snap(e * Q + q)

                def hi(u):
                    r, part = SOURCE[u]
                    act.wait_ge(sem(f"raw_in{r % RAW}"), (it * (BLK // RAW) + r // RAW + 1) * 16)
                    act.wait_ge(sem("unit_used"), it * U + (u + 1 - RING + USED0))
                    nc.scalar.copy(unit_view(c_hi[u % RING], u), part(raw[r % RAW])).then_inc(sem("hi_done"), 1)

                def silu_routed(b):
                    act.wait_ge(sem("unit_used"), it * U + (A_END[b] + USED0))
                    act.wait_ge(sem("h_done"), it * 2 + b + ONE)
                    nc.scalar.activation(r_silu[:], PS[GATE][0:CAP, :], ACT.Silu).then_inc(sem("silu_done"), 1)

                def silu_shared(n):
                    if n % 2 == 0:
                        act.wait_ge(sem("s_half"), it * 2 + (n // 2 + 1))
                    else:
                        act.wait_ge(sem("unit_used"), it * U + (S_END[n // 2] + USED0))
                    act.wait_ge(sem("sh_mult"), it * 4 + max(n - 1, 0) + ONE)
                    w = HALVES[n % 2][1]
                    nc.scalar.activation(s_silu[n % 2][:, 0:w], PS[X0 + 2 * (n % 2)][:, 0:w],
                                         ACT.Silu).then_inc(sem("silu_done"), 1)

                def turned_hi(b):
                    act.wait_ge(sem("t_done"), it * 2 + b + 1)
                    nc.scalar.copy(hT_hi[:, b * 4 * CAP:(b + 1) * 4 * CAP],
                                   PS[T_BANK[b]][:, 0:4 * CAP]).then_inc(sem("thi_done"), 1)

                for u in range(18):
                    hi(u)
                silu_routed(0)
                silu_shared(0)
                silu_shared(1)
                hi(18)
                hi(19)
                silu_shared(2)
                silu_shared(3)
                hi(20)
                hi(21)
                turned_hi(0)
                for u in range(22, 30):
                    hi(u)
                silu_routed(1)
                turned_hi(1)

    @block.vector
    def _(dve):
        chain = [0]

        def link(ins):
            chain[0] += 1
            ins.then_inc(sem("dve_chain"), 1)
            dve.wait_ge(sem("dve_chain"), chain[0])

        V = nc.vector
        dve.wait_ge(sem("src_in"), 16)
        dve.wait_ge(sem("dst_in"), 16)
        dve.wait_ge(sem("iota_done"), 1)
        V.tensor_copy(dst_f[:], dst_i[:]).then_inc(sem("idx"), 1)
        link(V.tensor_scalar(tmp_i[:], src_i[:], 1, None, ALU.arith_shift_right))
        link(V.tensor_copy(src_f[:], tmp_i[:]))
        link(V.tensor_scalar(tmp_i[:], src_i[:], 1, None, ALU.bitwise_and))
        link(V.tensor_copy(dig_f[:], tmp_i[:]))
        link(V.tensor_scalar(dig_f[:], dig_f[:], DIGIT - 1.0, 1.0, ALU.mult, ALU.add))
        dve.wait_ge(sem("idx"), 1)

        def one_hots(gr):
            for c in range(EG):
                col = gr * EG + c
                if c >= 4:
                    dve.wait_ge(sem("onehot_used"), gr * (EG - 1) + (c - 3))
                V.tensor_scalar(oh_d[c % 4][:, 0:626], iota_h[:, 0:626], dst_f[:, bass.ds(col, 1)], None,
                                ALU.is_equal).then_inc(sem("onehot"), 1)
                V.tensor_scalar(oh_s[c % 4][:, 0:314], iota_h[:, 0:314], src_f[:, bass.ds(col, 1)],
                                dig_f[:, bass.ds(col, 1)], ALU.is_equal, ALU.mult).then_inc(sem("onehot"), 1)

        def digits(gr):
            dve.wait_ge(sem("count_out"), gr * NT + NT)
            if not (isinstance(gr, int) and gr == 0):
                dve.wait_ge(sem("counted"), gr * 2)
            V.tensor_scalar(v_lo[:], v_int[:], int(DIGIT) - 1, None, ALU.bitwise_and).then_inc(sem("digits"), 1)
            V.tensor_scalar(v_hi[:], v_int[:], 12, None, ALU.arith_shift_right).then_inc(sem("digits"), 1)

        def layernorm(n, dest, done, ready):
            for t in range(NT):
                ready(t)
                for half in range(2):
                    V.bn_stats(st6[:, half, :], resid[:, t, half * HALF:(half + 1) * HALF]).then_inc(sem("bn"), 1)
                bn[0] += 2
                dve.wait_ge(sem("bn"), bn[0])
                link(V.bn_aggr(mv[:, t, :], st6[:]))
            V.tensor_scalar(mv[:, :, 1], mv[:, :, 1], EPS, None, ALU.add).then_inc(sem("var_done"), 1)
            dve.wait_ge(sem("std_done"), n)
            link(V.reciprocal(rstd[:], rstd[:]))
            for t in range(NT):
                V.tensor_scalar(dest[:, t, :], resid[:, t, :], mv[:, t, 0:1], rstd[:, t:t + 1],
                                ALU.subtract, ALU.mult).then_inc(sem(done), 1)

        bn = [0]
        one_hots(0)
        layernorm(1, xn, "xn_done", lambda t: dve.wait_ge(sem(f"x_in{t}"), 16))
        digits(0)
        with dve.Fori(1, NG) as gr:
            one_hots(gr)
            digits(gr)
        dve.wait_ge(sem("rwT_hi"), 1)
        V.tensor_tensor(rwT_lo[:], PS[7][:, 0:KT * E].rearrange("p (k n) -> p k n", k=KT),
                        rwT_hi[:].bitcast(F32), ALU.subtract).then_inc(sem("rwT_lo"), 1)
        dve.wait_ge(sem("a_in"), 16)
        for t in range(NT):
            dve.wait_ge(sem("h_out"), NT + t + 1)
            for c in range(2):
                link(V.tensor_tensor_reduce(out=scr[:], in0=h[:, t, :], in1=a_bc[:, c * D:(c + 1) * D], scale=1.0,
                                            scalar=0.0, op0=ALU.mult, op1=ALU.add, accum_out=al[:, t, c:c + 1]))
            V.tensor_scalar(diag[:, t, :], ident[0:TP, 0:TP], al[:, t, 0:1], None,
                            ALU.mult).then_inc(sem("diag_done"), 1)

        def feature_min(n, ps, parts, cols, scale=None):
            if n >= 2:
                dve.wait_ge(sem("fe_done"), n - 1)
            if scale is None:
                V.tensor_scalar(fm[n % 2][0:parts, 0:cols], ps, 0.0, None, ALU.min).then_inc(sem("fm_done"), 1)
            else:
                V.tensor_scalar(fm[n % 2][0:parts, 0:cols], ps, scale, 0.0, ALU.mult,
                                ALU.min).then_inc(sem("fm_done"), 1)

        dve.wait_ge(sem("albc_ps"), 1)
        V.tensor_copy(albc[:, 0:4 * TP], PS[5][0:TP, 0:4 * TP]).then_inc(sem("albc_out"), 1)
        V.tensor_copy(albc[:, 4 * TP:N], PS[6][0:TP, 0:TP]).then_inc(sem("albc_out"), 1)
        dve.wait_ge(sem("albc_out"), 2)
        dve.wait_ge(sem("counted"), 2 * NG)
        Cf = C[:].rearrange("p t c two -> p t (c two)")

        Ci = C[:].bitcast(I32).rearrange("p t c two -> p t (c two)")

        def edge_weights(dt):
            dve.wait_ge(sem("ez_done"), dt + 1)
            V.scalar_tensor_tensor(out=Cf[:, dt, 0:N], in0=ez[dt % 2][:], scalar=FMAX, in1=Ci[:, dt, 0:N],
                                   op0=ALU.min, op1=ALU.mult).then_inc(sem("ez_used"), 1)

        for dt in range(NT):
            if dt >= 2:
                edge_weights(dt - 2)
            link(V.tensor_scalar(zt[dt % 2][:], albc[:], al[:, dt, 1:2], None, ALU.add))
            V.scalar_tensor_tensor(out=zt[dt % 2][:], in0=zt[dt % 2][:], scalar=SLOPE, in1=zt[dt % 2][:],
                                   op0=ALU.mult, op1=ALU.max).then_inc(sem("z_done"), 1)
        edge_weights(NT - 2)
        edge_weights(NT - 1)
        dve.wait_ge(sem("ez_used"), NT)
        nf = 0
        for gp in range(2):
            for t in range(NT):
                dve.wait_ge(sem("kv_ps"), gp * NT + t + 1)
                feature_min(nf, PS[t][0:TP, :], TP, HALF)
                dve.wait_ge(sem("fe_done"), nf + 1)
                V.scalar_tensor_tensor(out=kk[:, t, gp * HALF:(gp + 1) * HALF], in0=PS[t][0:TP, :], scalar=0.0,
                                       in1=fe[nf % 2][0:TP, :], op0=ALU.max, op1=ALU.add).then_inc(sem("fe_used"), 1)
                nf += 1
        for j in range(PAIRS):
            dve.wait_ge(sem("KV_ps"), j + 1)
            ps = PS[j % 4]
            for o in (0, HD):
                V.tensor_copy(KV[o:o + HD, j, o:o + HD], ps[o:o + HD, o:o + HD]).then_inc(sem("KV_out"), 1)
                V.tensor_copy(KS[o:o + HD, j, o:o + HD], ps[o:o + HD, P:P + HD]).then_inc(sem("KV_out"), 1)
        dve.wait_ge(sem("rowsum_ps"), 1)
        link(V.tensor_scalar(rinv[:], PS[4][0:TP, 0:NT], EPS, None, ALU.add))
        link(V.reciprocal(rinv[:], rinv[:]))
        dve.wait_ge(sem("biased"), NT)
        for j in range(2 * NT):
            t, half = divmod(j, 2)
            dve.wait_ge(sem("agg_ps"), j + 1)
            ps = PS[j % 4][0:TP, :]
            feature_min(nf, ps, TP, HALF, scale=rinv[:, t:t + 1])
            r = resid[:, t, half * HALF:(half + 1) * HALF]
            link(V.tensor_scalar(gscr[j % 2][:], ps, rinv[:, t:t + 1], 0.0, ALU.mult, ALU.max))
            V.tensor_tensor(r, r, gscr[j % 2][:], ALU.add).then_inc(sem("agg_out"), 1)
            dve.wait_ge(sem("agg_out"), j + 1)
            dve.wait_ge(sem("fe_done"), nf + 1)
            V.scalar_tensor_tensor(out=r, in0=fe[nf % 2][0:TP, :], scalar=-1.0, in1=r, op0=ALU.add,
                                   op1=ALU.add).then_inc(sem("fe_used"), 1)
            nf += 1
        for j in range(PAIRS):
            for hf, (o, w) in enumerate(((0, 313), (313, 312))):
                dve.wait_ge(sem("q_ps"), 2 * j + hf + 1)
                ps = PS[hf][:, 0:w]
                feature_min(nf, ps, P, w)
                if j >= 2:
                    dve.wait_ge(sem("num_ps"), 2 * (j - 1))
                dve.wait_ge(sem("fe_done"), nf + 1)
                V.scalar_tensor_tensor(out=qT[j % 2][:, o:o + w], in0=ps, scalar=0.0, in1=fe[nf % 2][:, 0:w],
                                       op0=ALU.max, op1=ALU.add).then_inc(sem("fe_used"), 1)
                nf += 1
            for hf, (o, w) in enumerate(((0, 313), (313, 312))):
                dve.wait_ge(sem("num_ps"), 2 * j + hf + 1)
                link(V.tensor_scalar(dn[hf][:, 0:w], PS[(3, 1)[hf]][:, 0:w], 1e-6, None, ALU.add))
                link(V.reciprocal(dr[hf][:, 0:w], dn[hf][:, 0:w]))
                V.tensor_tensor(outT[:, j, o:o + w], PS[(2, 4)[hf]][:, 0:w], dr[hf][:, 0:w],
                                ALU.mult).then_inc(sem("num_used"), 1)
        for gp in range(2):
            for t in range(NT):
                dve.wait_ge(sem("o_ps"), gp * NT + t + 1)
                r = resid[:, t, gp * HALF:(gp + 1) * HALF]
                V.tensor_tensor(r, PS[t][0:TP, :], r, ALU.add).then_inc(sem("o_out"), 1)
        dve.wait_ge(sem("o_out"), 2 * NT)
        V.memset(yT_hi[:, :, N:NP2].bitcast(F32), 0.0).then_inc(sem("pad"), 1)
        V.memset(yT_lo[:, :, N:NP2].bitcast(F32), 0.0).then_inc(sem("pad"), 1)
        layernorm(2, y, "y_done", lambda t: None)
        dve.wait_ge(sem("y_done"), NT)
        for j in range(2 * NT):
            t, half = divmod(j, 2)
            s = (slice(None), slice(4 * half, 4 * half + 4), slice(t * TP, (t + 1) * TP))
            dve.wait_ge(sem("yT_hi"), j + 1)
            V.tensor_tensor(yT_lo[s], PS[TB[j % 3]][:, 0:4 * TP].rearrange("p (k n) -> p k n", k=4),
                            yT_hi[s].bitcast(F32), ALU.subtract).then_inc(sem("yT_lo"), 1)
        T = rt
        bc = [TP, NT, E]

        def wide(v):
            return v[:, 0:NT].unsqueeze(2).to_broadcast(bc)

        dve.wait_ge(sem("ms_done"), NT)
        V.tensor_scalar(rr["ms"][:, 0:NT], rr["ms"][:, 0:NT], 1.0 / D, RMS_EPS, ALU.mult,
                        ALU.add).then_inc(sem("rms_done"), 1)
        dve.wait_ge(sem("rms_sqrt"), 1)
        link(V.reciprocal(rr["r"][:, 0:NT], rr["r"][:, 0:NT]))
        dve.wait_ge(sem("lg_ps"), 1)
        link(V.tensor_tensor(T["lg"][:], PS[4][0:TP, 0:NT * E].rearrange("p (t e) -> p t e", t=NT), wide(rr["r"]),
                             ALU.mult))
        link(V.tensor_reduce(rr["mx"][:, 0:NT], T["lg"][:], AXX, ALU.max))
        V.tensor_tensor(T["lg"][:], T["lg"][:], wide(rr["mx"]), ALU.subtract).then_inc(sem("lg_done"), 1)
        dve.wait_ge(sem("pr_done"), 1)
        link(V.tensor_reduce(rr["sum"][:, 0:NT], T["pr"][:], AXX, ALU.add))
        link(V.reciprocal(rr["sum"][:, 0:NT], rr["sum"][:, 0:NT]))
        link(V.tensor_tensor(T["pr"][:], T["pr"][:], wide(rr["sum"]), ALU.mult))
        dve.wait_ge(sem("const_done"), 1)
        for t in range(NT):
            link(V.max(T["v8"][:, t, :], T["pr"][:, t, :]))
            link(V.max_index(i8[:, t, :], T["v8"][:, t, :], T["pr"][:, t, :]))
        link(V.tensor_copy(T["if8"][:], i8[:]))
        for t in range(NT):
            link(V.tensor_scalar(T["oh1"][:, t, :], iota8[:], T["if8"][:, t, 0:1], None, ALU.is_equal))
            link(V.tensor_scalar(T["oh2"][:, t, :], iota8[:], T["if8"][:, t, 1:2], None, ALU.is_equal))
        V.tensor_tensor(T["mask"][:], T["oh1"][:], T["oh2"][:], ALU.add).then_inc(sem("mask_done"), 1)
        link(V.tensor_tensor(rr["den"][:, 0:NT], T["v8"][:, :, 0], T["v8"][:, :, 1], ALU.add))
        link(V.reciprocal(rr["den"][:, 0:NT], rr["den"][:, 0:NT]))
        dve.wait_ge(sem("rank_ps"), 1)
        dve.wait_ge(sem("mask_done"), 1)
        link(V.tensor_copy(T["rank"][:], PS[5][0:TP, 0:NT * E].rearrange("p (t e) -> p t e", t=NT)))
        for t in range(NT):
            for e in range(E):
                V.tensor_scalar(S[:, t, e, :], iotacap[:], T["rank"][:, t, e:e + 1], T["mask"][:, t, e:e + 1],
                                ALU.is_equal, ALU.mult).then_inc(sem("S_done"), 1)
        link(V.tensor_scalar(T["keep"][:], T["rank"][:], float(CAP), None, ALU.is_lt))
        link(V.tensor_scalar(T["slot"][:], T["rank"][:], float(CAP - 1), None, ALU.min))
        link(V.tensor_tensor(T["slot"][:], T["slot"][:], iotaslot[:].unsqueeze(1).to_broadcast(bc), ALU.add))
        for c, (oh, kv_, ps_) in enumerate((("oh1", "k1", "p1"), ("oh2", "k2", "p2"))):
            link(V.tensor_tensor(T["t1"][:], T[oh][:], T["keep"][:], ALU.mult))
            link(V.tensor_reduce(rr[kv_][:, 0:NT], T["t1"][:], AXX, ALU.add))
            link(V.tensor_tensor(T["t2"][:], T[oh][:], T["slot"][:], ALU.mult))
            link(V.tensor_reduce(rr[ps_][:, 0:NT], T["t2"][:], AXX, ALU.add))
            link(V.tensor_copy(pos_u[:, c, 0:NT], rr[ps_][:, 0:NT]))
            link(V.tensor_tensor(rr[kv_][:, 0:NT], rr[kv_][:, 0:NT], rr["den"][:, 0:NT], ALU.mult))
            link(V.tensor_tensor(wts[:, c, 0:NT], rr[kv_][:, 0:NT], T["v8"][:, :, c], ALU.mult))
        dve.wait_ge(sem("tok_ps"), 1)
        V.tensor_copy(tok_u[:], PS[6][0:CAP, 0:E]).then_inc(sem("tok_done"), 1)
        for e in range(E):
            for half in range(2):
                s = slice(half * 4 * CAP, (half + 1) * 4 * CAP)
                dve.wait_ge(sem("st_hi_done"), 2 * e + half + 1)
                V.tensor_tensor(st_lo[e % 2][:, s], PS[(2 * e + half) % 4][:, 0:4 * CAP],
                                st_hi[e % 2][:, s].bitcast(F32), ALU.subtract).then_inc(sem("st_lo_done"), 1)
        for i in range(2):
            dve.wait_ge(sem(f"st_stored{i}"), 16 * E)
        V.memset(PS[R0][0:CAP, :], 0.0).then_inc(sem("rd_clear"), 1)
        V.memset(PS[R0 + 1][0:CAP, :], 0.0).then_inc(sem("rd_clear"), 1)
        dve.wait_ge(sem("rd_clear"), 2)

        def routed_add(step, cleared):
            dve.wait_ge(sem("unit_used"), step * U + USED0)
            dve.wait_ge(sem("eout_clear"), cleared)
            for half in range(2):
                r = eout[:, half * HALF:(half + 1) * HALF]
                V.tensor_tensor(r, PS[R0 + half][0:CAP, :], r, ALU.add).then_inc(sem("rd_added"), 1)

        dve.sem_inc(sem("lo_done"), U)
        for name in ("h_done", "sh_mult", "tlo_done", "sd_added"):
            dve.sem_inc(sem(name), ONE)

        with dve.Fori(0, E) as e:
            with dve.Fori(0, Q) as q:
                it = dve.snap(e * Q + q)

                def lo(u):
                    r, part = SOURCE[u]
                    dve.wait_ge(sem("hi_done"), it * U + u + 1)
                    V.tensor_tensor(unit_view(c_lo[u % RING], u), part(raw[r % RAW]),
                                    unit_view(c_hi[u % RING], u).bitcast(F32),
                                    ALU.subtract).then_inc(sem("lo_done"), 1)

                def routed_inner(b):
                    dve.wait_ge(sem("silu_done"), it * 6 + (0, 5)[b] + 1)
                    V.tensor_tensor(r_h[b][:], PS[UP][0:CAP, :], r_silu[:], ALU.mult).then_inc(sem("h_done"), 1)

                def shared_inner(n):
                    j, hf = divmod(n, 2)
                    o, w = HALVES[hf]
                    dve.wait_ge(sem("silu_done"), it * 6 + n + 2)
                    V.tensor_tensor(s_h[hf][:, 0:w], PS[X0 + 1 + 2 * hf][:, 0:w], s_silu[hf][:, 0:w],
                                    ALU.mult).then_inc(sem("sh_mult"), 1)
                    dve.wait_ge(sem("sh_mult"), it * 4 + n + 1 + ONE)
                    V.tensor_copy(sh_hi[:, j, o:o + w], s_h[hf][:, 0:w]).then_inc(sem("sh_hi_done"), 1)
                    dve.wait_ge(sem("sh_hi_done"), it * 4 + n + 1)
                    V.tensor_tensor(sh_lo[:, j, o:o + w], s_h[hf][:, 0:w], sh_hi[:, j, o:o + w].bitcast(F32),
                                    ALU.subtract).then_inc(sem("sh_ready"), 1)

                def turned_lo(b):
                    s = slice(b * 4 * CAP, (b + 1) * 4 * CAP)
                    dve.wait_ge(sem("thi_done"), it * 2 + b + 1)
                    V.tensor_tensor(hT_lo[:, s], PS[T_BANK[b]][:, 0:4 * CAP], hT_hi[:, s].bitcast(F32),
                                    ALU.subtract).then_inc(sem("tlo_done"), 1)

                for u in range(10):
                    lo(u)
                routed_add(it, ((it + (Q - 1)) >> 2) + 1)
                for u in range(10, 18):
                    lo(u)
                routed_inner(0)
                shared_inner(0)
                shared_inner(1)
                lo(18)
                lo(19)
                shared_inner(2)
                shared_inner(3)
                lo(20)
                lo(21)
                turned_lo(0)
                for u in range(22, 30):
                    lo(u)
                routed_inner(1)
                for n in range(2 * NT):
                    t, half = divmod(n, 2)
                    r = resid[:, t, half * HALF:(half + 1) * HALF]
                    dve.wait_ge(sem("sd_done"), it * (2 * NT) + n + 1)
                    V.tensor_tensor(r, PS[X0 + n % 4][0:TP, :], r, ALU.add).then_inc(sem("sd_added"), 1)
                turned_lo(1)
        routed_add(STEPS, E + 1)
        dve.wait_ge(sem("sd_added"), 2 * NT * Q * E + ONE)
        for t in range(NT):
            for c in range(2):
                dve.wait_ge(sem(f"g_in{c}_{t}"), 16)
                ins = V.scalar_tensor_tensor(out=resid[:, t, :], in0=g[c][t][:], scalar=wts[:, c, t:t + 1],
                                             in1=resid[:, t, :], op0=ALU.mult, op1=ALU.add)
                if c == 0:
                    link(ins)
            ins.then_inc(sem("out_done"), 1)

    @block.tensor
    def _(pe):
        MM = nc.tensor.matmul
        TR = nc.tensor.transpose

        def count_group(gr):
            if not (isinstance(gr, int) and gr == 0):
                pe.wait_ge(sem("count_out"), gr * NT)
            for c in range(EG):
                pe.wait_ge(sem("onehot"), gr * (2 * EG) + 2 * c + 2)
                for dt in range(NT):
                    m = MM(PS[dt][0:TP, 0:SC], oh_d[c % 4][:, dt * TP:(dt + 1) * TP], oh_s[c % 4][:, 0:SC],
                           start=(c == 0), stop=(c == EG - 1))
                    if c == EG - 1:
                        m.then_inc(sem("count_done"), 1)
                    elif dt == NT - 1:
                        m.then_inc(sem("onehot_used"), 1)
        count_group(0)
        with pe.Fori(1, NG) as gr:
            count_group(gr)

        pe.wait_ge(sem("const_done"), 1)
        for j in range(2 * NT):
            t, half = divmod(j, 2)
            pe.wait_ge(sem("xn_done"), t + 1)
            if j >= 3:
                pe.wait_ge(sem("xnT_out"), j - 2)
            for k in range(4):
                c = (4 * half + k) * P
                m = TR(PS[TB[j % 3]][:, k * TP:(k + 1) * TP], xn[:, t, c:c + P], ident[0:TP, 0:TP])
            m.then_inc(sem("xnT_ps"), 1)
        pe.wait_ge(sem("rw_in"), 16)
        pe.wait_ge(sem("xnT_out"), 2 * NT)
        for k in range(KT):
            m = TR(PS[7][:, k * E:(k + 1) * E], rw_in[:, k * P:(k + 1) * P], ident[0:E, 0:E])
        m.then_inc(sem("rwT_ps"), 1)
        pe.wait_ge(sem("count_out"), NG * NT)
        for half in range(2):
            pe.wait_ge(sem(f"wl_in{half}"), 16)
            w = wl[half][:].rearrange("p (k n) -> p k n", k=KT)
            for t in range(NT):
                if half:
                    pe.wait_ge(sem("h_out"), t + 1)
                for k in range(KT):
                    m = MM(PS[t][0:TP, :], xnT[:, k, t * TP:(t + 1) * TP], w[:, k, :],
                           start=(k == 0), stop=(k == KT - 1))
                m.then_inc(sem("h_ps"), 1)

        def turn(gp):
            n = gp + 2
            pe.wait_ge(sem(f"wl_in{n % 2}"), 16 * (n // 2 + 1))
            w = wl[n % 2][:].rearrange("p (s k) -> p s k", s=4)
            if gp == 0:
                pe.wait_ge(sem("rwT_lo"), 1)
            if gp == 1:
                pe.wait_ge(sem("albc_out"), 2)
            for k in range(KT):
                if gp * KT + k >= 3:
                    pe.wait_ge(sem("wT_out"), gp * KT + k - 2)
                for i in range(4):
                    m = TR(PS[TB[k % 3]][:, i * P:(i + 1) * P], w[:, i, k * P:(k + 1) * P], ident[:])
                m.then_inc(sem("wT_ps"), 1)

        def project(t, lhs, done):
            for k in range(KT):
                m = MM(PS[t][0:TP, :], lhs[:, k, t * TP:(t + 1) * TP], wT[:, k, :],
                       start=(k == 0), stop=(k == KT - 1))
            m.then_inc(sem(done), 1)

        for gp in range(4):
            turn(gp)
            pe.wait_ge(sem("wT_out"), (gp + 1) * KT)
            for t in range(NT):
                if gp == 0:
                    pe.wait_ge(sem("h_out"), NT + t + 1)
                elif gp <= 2:
                    pe.wait_ge(sem("fe_used"), (gp - 1) * NT + t + 1)
                else:
                    pe.wait_ge(sem("v_out"), t + 1)
                project(t, xnT, "kv_ps")
                if gp == 0 and t == 2:
                    pe.wait_ge(sem("diag_done"), NT)
                    for s in range(NT):
                        ps = PS[5][0:TP, s * TP:(s + 1) * TP] if s < 4 else PS[6][0:TP, 0:TP]
                        m = MM(ps, ones[0:TP, 0:TP], diag[:, s, :], start=True, stop=True)
                    m.then_inc(sem("albc_ps"), 1)
        for j in range(PAIRS):
            pe.wait_ge(sem("v_out"), 2 * NT)
            if j >= 4:
                pe.wait_ge(sem("KV_out"), 4 * (j - 3))
            c = slice(j * P, (j + 1) * P)
            for t in range(NT):
                MM(PS[j % 4][:, 0:P], kk[:, t, c], vv[:, t, c], start=(t == 0), stop=(t == NT - 1))
            for t in range(NT):
                m = MM(PS[j % 4][:, P:P + HD], kk[:, t, c], ones[0:TP, 0:HD], start=(t == 0), stop=(t == NT - 1))
            m.then_inc(sem("KV_ps"), 1)
        pe.wait_ge(sem("ez_used"), NT)
        Cf = C[:].rearrange("p t c two -> p t (c two)")
        pe.wait_ge(sem("KV_out"), 4 * PAIRS)
        for t in range(NT):
            for dt in range(NT):
                m = MM(PS[4][0:TP, t:t + 1], Cf[:, dt, t * TP:(t + 1) * TP], ones[0:TP, 0:1],
                       start=(dt == 0), stop=(dt == NT - 1))
        m.then_inc(sem("rowsum_ps"), 1)
        for j in range(2 * NT):
            t, half = divmod(j, 2)
            if j >= 4:
                pe.wait_ge(sem("fe_used"), 2 * NT + j - 3)
            for dt in range(NT):
                m = MM(PS[j % 4][0:TP, :], Cf[:, dt, t * TP:(t + 1) * TP], h[:, dt, half * HALF:(half + 1) * HALF],
                       start=(dt == 0), stop=(dt == NT - 1))
            m.then_inc(sem("agg_ps"), 1)
        nf = 4 * NT
        pe.wait_ge(sem("fe_used"), nf)
        for j in range(PAIRS):
            if j % 4 == 0:
                turn(4 + j // 4)
                pe.wait_ge(sem("wT_out"), (5 + j // 4) * KT)
            if j:
                pe.wait_ge(sem("num_used"), 2 * j)
            for hf, (o, w) in enumerate(((0, 313), (313, 312))):
                for k in range(KT):
                    m = MM(PS[hf][:, 0:w], wT[:, k, (j % 4) * P:(j % 4 + 1) * P], xnT[:, k, o:o + w],
                           start=(k == 0), stop=(k == KT - 1))
                m.then_inc(sem("q_ps"), 1)
            for hf, (o, w) in enumerate(((0, 313), (313, 312))):
                pe.wait_ge(sem("fe_used"), nf + 2 * j + hf + 1)
                MM(PS[(2, 4)[hf]][:, 0:w], KV[:, j, :], qT[j % 2][:, o:o + w], start=True, stop=True)
                m = MM(PS[(3, 1)[hf]][:, 0:w], KS[:, j, :], qT[j % 2][:, o:o + w], start=True, stop=True)
                m.then_inc(sem("num_ps"), 1)
        for gp in (6, 7):
            turn(gp)
            pe.wait_ge(sem("wT_out"), (gp + 1) * KT)
            pe.wait_ge(sem("num_used"), 2 * PAIRS)
            for t in range(NT):
                if gp == 7:
                    pe.wait_ge(sem("o_out"), t + 1)
                project(t, outT, "o_ps")
        for j in range(2 * NT):
            t, half = divmod(j, 2)
            pe.wait_ge(sem("y_done"), t + 1)
            if j >= 3:
                pe.wait_ge(sem("yT_lo"), j - 2)
            for k in range(4):
                c = (4 * half + k) * P
                m = TR(PS[TB[j % 3]][:, k * TP:(k + 1) * TP], y[:, t, c:c + P], ident[0:TP, 0:TP])
            m.then_inc(sem("yT_ps"), 1)
        pe.wait_ge(sem("yT_lo"), 2 * NT)
        pe.wait_ge(sem("o_out"), 2 * NT)
        for t in range(NT):
            n = 0
            for k in range(KT):
                for ly in (yT_hi, yT_lo):
                    for lw in (rwT_hi, rwT_lo):
                        m = MM(PS[4][0:TP, t * E:(t + 1) * E], ly[:, k, t * TP:(t + 1) * TP], lw[:, k, :],
                               start=(n == 0), stop=(n == 4 * KT - 1))
                        n += 1
        m.then_inc(sem("lg_ps"), 1)
        pe.wait_ge(sem("mask_done"), 1)
        for t in range(NT):
            for s in range(t + 1):
                m = MM(PS[5][0:TP, t * E:(t + 1) * E], (tri if s == t else ones)[0:TP, 0:TP], rt["mask"][:, s, :],
                       start=(s == 0), stop=(s == t))
        m.then_inc(sem("rank_ps"), 1)
        pe.wait_ge(sem("S_done"), NT * E)
        for e in range(E):
            for t in range(NT):
                m = MM(PS[6][0:CAP, e:e + 1], S[:, t, e, :], rr["tok"][:, t:t + 1], start=(t == 0), stop=(t == NT - 1))
        m.then_inc(sem("tok_ps"), 1)
        for e in range(E):
            pe.wait_ge(sem(f"xg_in{e % 4}"), 16 * (e // 4 + 1))
            for half in range(2):
                if 2 * e + half >= 4:
                    pe.wait_ge(sem("st_lo_done"), 2 * e + half - 3)
                for k in range(4):
                    c = (4 * half + k) * P
                    m = TR(PS[(2 * e + half) % 4][:, k * CAP:(k + 1) * CAP], xg[e % 4][:, c:c + P],
                           ident[0:CAP, 0:CAP])
                m.then_inc(sem("xgT_ps"), 1)

        pe.wait_ge(sem("rd_clear"), 2)
        pe.sem_inc(sem("unit_used"), USED0)

        with pe.Fori(0, E) as e:
            with pe.Fori(0, Q) as q:
                it = pe.snap(e * Q + q)

                def split(u):
                    pe.wait_ge(sem("lo_done"), it * U + (U + u + 1))

                def three(out_, l_hi, l_lo, r_hi, r_lo, first, last):
                    MM(out_, l_hi, r_hi, start=first, stop=False)
                    MM(out_, l_hi, r_lo, start=False, stop=False)
                    return MM(out_, l_lo, r_hi, start=False, stop=last)

                def routed_up(b):
                    for i, bank in enumerate((GATE, UP)):
                        for k in range(KT):
                            u = UNITS_GATE[b] + 4 * i + k // 2
                            if k % 2 == 0:
                                split(u)
                            c = slice((k % 2) * HALF, (k % 2 + 1) * HALF)
                            xs = slice(k * CAP, (k + 1) * CAP)
                            m = three(PS[bank][0:CAP, :], xgT_hi[:, xs], xgT_lo[:, xs],
                                      c_hi[u % RING][:, c], c_lo[u % RING][:, c], k == 0, k == KT - 1)
                            if k % 2:
                                m.then_inc(sem("unit_used"), 1)

                def shared_up(n):
                    j, hf = divmod(n, 2)
                    o, w = HALVES[hf]
                    for i in range(2):
                        u = UNIT_S + 2 * j + i
                        split(u)
                        for k in range(KT):
                            c = slice(k * P, (k + 1) * P)
                            m = three(PS[X0 + 2 * hf + i][:, 0:w], c_hi[u % RING][:, c], c_lo[u % RING][:, c],
                                      yT_hi[:, k, o:o + w], yT_lo[:, k, o:o + w], k == 0, k == KT - 1)
                        if hf:
                            m.then_inc(sem("unit_used"), 1)
                    if not hf:
                        m.then_inc(sem("s_half"), 1)

                def turn_inner(b):
                    for k in range(4):
                        m = TR(PS[T_BANK[b]][:, k * CAP:(k + 1) * CAP], r_h[b][:, k * P:(k + 1) * P],
                               ident[0:CAP, 0:CAP])
                        if b == 1 and k == 0:
                            m.then_inc(sem("unit_used"), 1)
                    m.then_inc(sem("t_done"), 1)

                pe.wait_ge(sem("xgT_in"), e * 32 + 32)
                pe.wait_ge(sem("tlo_done"), it * 2 + ONE)
                pe.wait_ge(sem("h_done"), it * 2 + ONE)
                routed_up(0)
                pe.wait_ge(sem("sd_added"), it * (2 * NT) + ONE)
                shared_up(0)
                shared_up(1)
                for n in (2, 3):
                    pe.wait_ge(sem("sh_mult"), it * 4 + (n - 1) + ONE)
                    shared_up(n)
                pe.wait_ge(sem("h_done"), it * 2 + 1 + ONE)
                pe.wait_ge(sem("rd_added"), it * 2 + 2)
                turn_inner(0)
                routed_up(1)
                pe.wait_ge(sem("sh_ready"), it * 4 + 4)
                split(UNIT_SD)
                split(UNIT_SD + 1)
                for n in range(2 * NT):
                    t, half = divmod(n, 2)
                    if n >= 4:
                        pe.wait_ge(sem("sd_added"), it * (2 * NT) + (n - 3) + ONE)
                    c = slice(half * HALF, (half + 1) * HALF)
                    for j in range(2):
                        u = UNIT_SD + j
                        ts = slice(t * TP, (t + 1) * TP)
                        m = three(PS[X0 + n % 4][0:TP, :], sh_hi[:, j, ts], sh_lo[:, j, ts],
                                  c_hi[u % RING][:, c], c_lo[u % RING][:, c], j == 0, j == 1)
                        if n == 2 * NT - 1 and j == 0:
                            m.then_inc(sem("unit_used"), 1)
                    m.then_inc(sem("sd_done"), 1)
                pe.wait_ge(sem("h_done"), it * 2 + 2 + ONE)
                turn_inner(1)
                for k in range(8):
                    u = UNIT_RD + k
                    if k % 4 == 0:
                        pe.wait_ge(sem("tlo_done"), it * 2 + (k // 4 + 1) + ONE)
                    split(u)
                    xs = slice(k * CAP, (k + 1) * CAP)
                    for half in range(2):
                        c = slice(half * HALF, (half + 1) * HALF)
                        m = three(PS[R0 + half][0:CAP, :], hT_hi[:, xs], hT_lo[:, xs],
                                  c_hi[u % RING][:, c], c_lo[u % RING][:, c], k == 0, k == 7)
                    m.then_inc(sem("unit_used"), 1)

    ctx.close()


_INS = ["x", "src", "dst", "L0_gnn_W", "L0_gnn_a", "L0_mix_w_qkv", "L0_mix_w_out", "L0_mix_b_out",
        "L0_ffn_router_w", "L0_ffn_rg", "L0_ffn_ru", "L0_ffn_rd", "L0_ffn_sg", "L0_ffn_su", "L0_ffn_sd"]


def kernel(**inputs):
    import numpy as _np
    import concourse.bacc as _bacc
    from concourse import mybir as _mybir
    from concourse.bass_utils import run_bass_kernel_spmd as _run

    nc = _bacc.Bacc("TRN2", target_bir_lowering=False, num_devices=1)
    arrays, args = {}, []
    for name in _INS:
        v = _np.ascontiguousarray(inputs[name])
        arrays[f"in_{name}"] = v
        args.append(nc.dram_tensor(f"in_{name}", v.shape, _mybir.dt.from_np(v.dtype), kind="ExternalInput").ap())
    res = nc.dram_tensor("out_0", (N, D), _mybir.dt.float32, kind="ExternalOutput").ap()
    build(nc, *args, res)
    r = _run(nc, [arrays], core_ids=[0])
    return r.results[0]["out_0"]
```

```python
from contextlib import ExitStack

import numpy as np

import concourse.bass as bass
from concourse import mybir

F32 = mybir.dt.float32
F32R = mybir.dt.float32r
BF16 = mybir.dt.bfloat16
F16 = mybir.dt.float16
I32 = mybir.dt.int32
U32 = mybir.dt.uint32
ALU = mybir.AluOpType
ACT = mybir.ActivationFunctionType
AXX = mybir.AxisListType.X

P = 128
N = 625
TP = 125
NT = N // TP
D = 1024
KT = D // P
HALF = 512
E = 8
CAP = int(1.25 * N / E)
IR = 4 * D
IS = 8 * D
NE = 20625
EC = NE // TP
EG = 28
NG = 6
ECP = EG * NG
DIGIT = 4096.0
SC = (N + 1) // 2
NP2 = 626
HALVES = ((0, 314), (314, 312))
HEADS = 16
HD = 64
PAIRS = HEADS // 2
EPS = 1e-5
RMS_EPS = float(np.finfo(np.float32).eps)
FMAX = float(np.finfo(np.float32).max)
SLOPE = 0.1
Q = 4
U = 30
RING = 10
RAW = 3
BLK = 15
STEPS = E * Q
USED0 = RING + 1
ONE = 1
UNITS_GATE = (0, 12)
UNIT_S = 8
UNIT_SD = 20
UNIT_RD = 22
A_END = (8, 20)
S_END = (10, 12)
GATE, UP, X0, R0 = 0, 1, 2, 6
S_BANK = (X0, X0 + 2, R0, X0)
T_BANK = (X0 + 2, GATE)


TB = (5, 6)
GW = 256
G_K, G_V, G_Q, G_OUT = 4, 8, 12, 16
ACT_CHUNKS = tuple(range(3, EG, 3))
DVE_ONEHOTS = 2 * EG - len(ACT_CHUNKS)
VW = P + 2
FE_Q = 4 * NT
TRIPLES = ((0, 3), (3, 3), (6, 2))
AGG_BANK = (7, 0, 1, 2)
V_BANK = (3, 4, 1, 2, 0)
KV_BANK = (3, 4, 1)
Q_BANK = (7, 2, 0, 3, 4, 1)
ATT_BANK = ((4, 1, 7), (2, 0, 3))


def unit_source(u):
    def rows(half):
        return lambda t: t[:, half * 1024:(half + 1) * 1024]

    def columns(j):
        return lambda t: t[:].rearrange("p (k n) -> p k n", k=KT)[:, :, j * P:(j + 1) * P]

    if u < UNIT_S:
        return u // 2, rows(u % 2)
    if u < UNITS_GATE[1]:
        return 4 + u % 2, columns((u - UNIT_S) // 2)
    return u // 2, rows(u % 2)


def unit_view(t, u):
    if UNIT_S <= u < UNITS_GATE[1]:
        return t[:].rearrange("p (k n) -> p k n", k=KT)
    return t[:]


SOURCE = [unit_source(u) for u in range(U)]
LAST_UNIT = [max(u for u in range(U) if SOURCE[u][0] == b) for b in range(BLK)]


def build(nc, x, src, dst, W, a, w_qkv, w_out, b_out, router_w, rg, ru, rd, sg, su, sd, out):
    ctx = ExitStack()
    sems = {}

    def sem(name):
        if name not in sems:
            sems[name] = ctx.enter_context(nc.semaphore(name))
        return sems[name]

    cursor = [16512]

    def place(name, shape, dt, at=None):
        size = int(np.prod(shape[1:])) * mybir.dt.size(dt)
        size = (size + 31) // 32 * 32
        off = cursor[0] if at is None else at
        if at is None:
            cursor[0] += size
        return nc.alloc_sbuf_tensor_at(name, shape, dt, offset=off)

    def here():
        return cursor[0]

    resid = place("resid", [TP, NT, D], F32)
    ident = place("ident", [P, P], F32)
    ones = place("ones", [P, P], F32)
    tri = place("tri", [P, P], F32)
    pos_u = place("pos_u", [TP, 2, 8], U32)
    wts = place("wts", [TP, 2, 8], F32)
    tok_u = place("tok_u", [CAP, E], U32)
    raw_at = here()
    raw = [place(f"raw{r}", [P, 2048], F32) for r in range(RAW)]
    shared_at = here()
    yT_hi = place("yT_hi", [P, KT, NP2], F32R)
    yT_lo = place("yT_lo", [P, KT, NP2], F32R)
    conv_at = here()
    c_hi = [place(f"c_hi{s}", [P, 1024], F32R) for s in range(RING)]
    c_lo = [place(f"c_lo{s}", [P, 1024], F32R) for s in range(RING)]
    xgT_hi = place("xgT_hi", [P, KT * CAP], F32R)
    xgT_lo = place("xgT_lo", [P, KT * CAP], F32R)
    sh_at = here()
    sh_hi = place("sh_hi", [P, 2, NP2], F32R)
    sh_lo = place("sh_lo", [P, 2, NP2], F32R)
    s_silu = [place(f"s_silu{i}", [P, 314], F32) for i in range(2)]
    s_h = [place(f"s_h{i}", [P, 314], F32) for i in range(2)]
    r_silu = place("r_silu", [CAP, HALF], F32)
    r_h = [place(f"r_h{i}", [CAP, HALF], F32) for i in range(2)]
    hT_hi = place("hT_hi", [P, 8 * CAP], F32R)
    hT_lo = place("hT_lo", [P, 8 * CAP], F32R)
    eout = place("eout", [CAP, D], F32)
    eout_st = place("eout_st", [CAP, D], F32)
    eout_end = here()
    assert here() <= 229344, here()
    cursor[0] = raw_at
    C = place("C", [TP, NT, SC, 2], F32)
    a_at = here()
    a_bc = place("a_bc", [TP, 2 * D], F32)
    albc = place("albc", [TP, N], F32)
    assert here() <= shared_at, (here(), shared_at)
    cursor[0] = a_at
    fm = [place(f"fm{i}", [P, HALF], F32) for i in range(2)]
    fe = [place(f"fe{i}", [P, HALF], F32) for i in range(2)]
    assert here() <= a_at + 2 * D * 4
    wl = [place(f"wl{i}", [P, 4 * D], F32, at=shared_at + i * 16384) for i in range(2)]
    cursor[0] = shared_at + 2 * 16384
    al = place("al", [TP, NT, 2], F32)
    rinv = place("rinv", [TP, NT], F32)
    diag = place("diag", [TP, NT, TP], F32)
    rw_at = here()
    rw_in = place("rw_in", [E, D], F32)
    b_bc = place("b_bc", [TP, D], F32, at=rw_at)
    assert here() <= conv_at
    cursor[0] = conv_at
    xnT_hi = place("xnT_hi", [P, KT, NP2], F32R)
    outT_hi = place("outT_hi", [P, KT, NP2], F32R, at=conv_at)
    lo_at = here()
    xnT_lo = place("xnT_lo", [P, KT, NP2], F32R)
    outT_lo = place("outT_lo", [P, KT, NP2], F32R, at=lo_at)
    wT_at = here()
    wT_hi, wT_lo = [], []
    buf_at = []
    for i in range(2):
        buf_at.append(here())
        wT_hi.append(place(f"wT_hi{i}", [P, KT, GW], F32R))
        wT_lo.append(place(f"wT_lo{i}", [P, KT, GW], F32R))
    h_at = here()
    vv = place("vv", [TP, NT, PAIRS, VW], F32)
    h = place("h", [TP, NT, D], F32, at=h_at)
    xn = place("xn", [TP, NT, D], F32, at=h_at)
    att = [place(f"att{i}", [TP, D], F32, at=h_at + i * 4 * D) for i in range(2)]
    sq = place("sq", [TP, D], F32, at=h_at + 2 * 4 * D)
    k_at = here()
    kk = place("kk", [TP, NT, D], F32)
    qT = place("qT", [P, PAIRS, NP2], F32, at=k_at)
    y = place("y", [TP, NT, D], F32, at=k_at)
    scr = place("scr", [TP, D], F32, at=k_at)
    tail_at = here()
    zt = [place(f"zt{i}", [TP, N], F32) for i in range(2)]
    KV = place("KV", [P, PAIRS, VW], F32)
    gscr = [place(f"gscr{i}", [TP, HALF], F32, at=tail_at + i * 2048) for i in range(2)]
    dn = place("dn", [TP, PAIRS, 2], F32, at=tail_at + 2 * 2048)
    dr = place("dr", [TP, PAIRS, 2], F32, at=tail_at + 2 * 2048 + 64)
    late_at = max(here(), eout_end)
    late_end = 229344
    cursor[0] = late_at
    rwT = place("rwT", [P, KT * 2 * E + P], F32R)
    lgT = place("lgT", [2 * E, NP2], F32, at=conv_at)
    mv = place("mv", [TP, NT, 2], F32)
    st6 = place("st6", [TP, NT, 2, 6], F32)
    rstd = place("rstd", [TP, NT], F32)
    rr = {n: place("rr_" + n, [TP, 8], F32) for n in
          ("ms", "r", "mx", "sum", "den", "k1", "k2", "p1", "p2")}
    tok_b = place("tok_b", [TP, NT, 2], BF16)
    iota8 = place("iota8", [TP, E], F32)
    iotaslot = place("iotaslot", [TP, E], F32)
    iotacap = place("iotacap", [TP, CAP], F32)
    assert here() <= late_end, here()
    cursor[0] = k_at
    oh_d = [place(f"oh_d{i}", [TP, 640], BF16) for i in range(4)]
    oh_s = [place(f"oh_s{i}", [TP, 320], BF16) for i in range(4)]
    iota_h = place("iota_h", [TP, 640], F16)
    src_i = place("src_i", [TP, ECP], I32)
    dst_i = place("dst_i", [TP, ECP], I32)
    src_f = place("src_f", [TP, ECP], F32)
    dst_f = place("dst_f", [TP, ECP], F32)
    dig_f = place("dig_f", [TP, ECP], F32)
    src_n = place("src_n", [TP, ECP], F32)
    dig_n = place("dig_n", [TP, ECP], F32)
    tmp_i = place("tmp_i", [TP, ECP], I32)
    sq_s = [place(f"sq_s{i}", [TP, 320], F32) for i in range(2)]
    assert here() <= tail_at
    v_int = place("v_int", [TP, NT, SC], I32, at=buf_at[1])
    v_lo = place("v_lo", [TP, NT, SC], I32, at=buf_at[1] + 6272)
    assert buf_at[1] + 2 * 6272 <= h_at
    cursor[0] = sh_at
    S = place("S", [TP, NT, E, CAP], BF16, at=wT_at)
    xg = [place(f"xg{i}", [CAP, D], F32) for i in range(4)]
    st_hi = [place(f"st_hi{i}", [P, KT * CAP], F32R) for i in range(2)]
    st_lo = [place(f"st_lo{i}", [P, KT * CAP], F32R) for i in range(2)]
    assert here() <= late_at
    cursor[0] = h_at
    rt = {n: place("rt_" + n, [TP, NT, E], F32) for n in
          ("lg", "pr", "v8", "if8", "oh1", "oh2", "mask", "rank", "keep", "slot", "t1", "t2")}
    i8 = place("rt_i8", [TP, NT, E], U32)
    slot_tok = place("slot_tok", [CAP, E], F32)
    assert here() <= sh_at - 2 * KT * CAP * 4
    cursor[0] = conv_at
    got = [[place(f"got{c}_{t}", [TP, D], F32) for t in range(NT)] for c in range(2)]

    def rw_half(i):
        return rwT[:, 0:KT * 2 * E].rearrange("p (k two n) -> p k two n", k=KT, two=2)[:, :, i, :]

    PS = [ctx.enter_context(nc.psum_tensor(f"ps{b}", [P, HALF], F32)) for b in range(8)]

    y_rows = nc.dram_tensor("y_rows", [N, D], F32).ap()
    xgT_hi_d = nc.dram_tensor("xgT_hi_d", [E, P, KT * CAP], F32).ap()
    xgT_lo_d = nc.dram_tensor("xgT_lo_d", [E, P, KT * CAP], F32).ap()
    eout_d = nc.dram_tensor("eout_d", [(E + 1) * CAP, D], F32).ap()

    x_t = x.rearrange("(t p) d -> t p d", p=TP)
    out_t = out.rearrange("(t p) d -> t p d", p=TP)
    y_rows_t = y_rows.rearrange("(t p) d -> t p d", p=TP)
    rg_v = rg.rearrange("e (k p) (q n) -> e q p k n", p=P, n=HALF)
    ru_v = ru.rearrange("e (k p) (q n) -> e q p k n", p=P, n=HALF)
    rd_v = rd.rearrange("e (q k p) n -> e q p k n", k=8, p=P)
    sg_v = sg.rearrange("(k p) (i n) -> i p k n", p=P, n=256)
    su_v = su.rearrange("(k p) (i n) -> i p k n", p=P, n=256)
    sd_v = sd.rearrange("(i k p) n -> i p k n", k=2, p=P)
    W_v = W.rearrange("(k p) (c n) -> c p k n", p=P, n=HALF)
    wq_v = w_qkv.rearrange("(c s p) k -> c p s k", s=4, p=P)
    wo_v = w_out.rearrange("(c s p) k -> c p s k", s=4, p=P)
    loads = [W_v[0], W_v[1], wq_v[2], wq_v[3], wq_v[4], wq_v[5], wq_v[0], wq_v[1], wo_v[0], wo_v[1]]

    def proj_n(g, t):
        return NT * (g if g < G_Q else g - (G_OUT - G_Q)) + t + 1

    OUT0 = 2 * NT + 4 * (G_OUT + 2 - G_K)
    YT0 = OUT0 + 2 * NT + 4 * 2

    def fill_w(g, i):
        return 2 * NT + 4 * (g - G_K) + i if g < G_OUT + 2 else OUT0 + 2 * NT + 4 * (g - G_OUT - 2) + i

    def fill_bank(n):
        return PS[TB[n % 2]]

    def tokens_part(hi, lo, n, j):
        t, half = divmod(j, 2)
        s = (slice(None), slice(4 * half, 4 * half + 4), slice(t * TP, (t + 1) * TP))
        return hi[s], lo[s], fill_bank(n)[:, 0:4 * TP].rearrange("p (k n) -> p k n", k=4)

    def weights_part(g, i):
        ks = slice(2 * i, 2 * i + 2)
        return (wT_hi[g % 2][:, ks, :], wT_lo[g % 2][:, ks, :],
                fill_bank(fill_w(g, i))[:, 0:2 * GW].rearrange("p (k n) -> p k n", k=2))

    def quarter(g):
        return wl[g // 2][:].rearrange("p (k n) -> p k n", k=KT)[:, :, (g % 2) * GW:(g % 2 + 1) * GW]

    block = ctx.enter_context(nc.Block())
    @block.sync
    def _(sp):
        sp.dma_start(src_i[:, 0:EC], src.rearrange("(p c) -> p c", p=TP)).then_inc(sem("src_in"), 16)
        sp.dma_start(dst_i[:, 0:EC], dst.rearrange("(p c) -> p c", p=TP)).then_inc(sem("dst_in"), 16)
        for t in range(NT):
            sp.dma_start(resid[:, t, :], x_t[t]).then_inc(sem("x_in"), 16)
        for n, v in enumerate(loads):
            if n in (2, 3):
                sp.wait_ge(sem("w_lo"), 2 * (n - 1))
            elif n >= 4:
                sp.wait_ge(sem("turned"), fill_w(2 * n - 3, 3) + 1)
            d = wl[n % 2][:].rearrange("p (k n) -> p k n", k=v.shape[1])
            sp.dma_start(d, v).then_inc(sem(f"wl_in{n % 2}"), 16)
        for t in range(NT):
            sp.wait_ge(sem("y_done"), t + 1)
            sp.dma_start(y_rows_t[t], y[:, t, :]).then_inc(sem("y_stored"), 16)
        sp.wait_ge(sem("fe_used"), FE_Q + 2 * PAIRS)
        with sp.Fori(0, E) as e:
            with sp.Fori(0, Q) as q:
                it = sp.snap(e * Q + q)
                blocks = [rg_v[e, q * 2][:, 0:4, :], rg_v[e, q * 2][:, 4:8, :],
                          ru_v[e, q * 2][:, 0:4, :], ru_v[e, q * 2][:, 4:8, :],
                          sg_v[it], su_v[it],
                          rg_v[e, q * 2 + 1][:, 0:4, :], rg_v[e, q * 2 + 1][:, 4:8, :],
                          ru_v[e, q * 2 + 1][:, 0:4, :], ru_v[e, q * 2 + 1][:, 4:8, :],
                          sd_v[it]] + [rd_v[e, q][:, 2 * r:2 * r + 2, :] for r in range(4)]
                for b, v in enumerate(blocks):
                    if b >= RAW:
                        sp.wait_ge(sem("lo_done"), it * U + (U + LAST_UNIT[b - RAW] + 1))
                    else:
                        sp.wait_ge(sem("lo_done"), it * U + (LAST_UNIT[b - RAW + BLK] + 1))
                    sp.dma_start(raw[b % RAW][:].rearrange("p (k n) -> p k n", k=v.shape[1]),
                                 v).then_inc(sem(f"raw_in{b % RAW}"), 16)
        for t in range(NT):
            sp.wait_ge(sem("out_done"), t + 1)
            sp.dma_start(out_t[t], resid[:, t, :]).then_inc(sem("out_stored"), 16)
        sp.wait_ge(sem("out_stored"), 16 * NT)

    @block.gpsimd
    def _(pool):
        chain = [0]

        def link(ins):
            chain[0] += 1
            ins.then_inc(sem("pool_chain"), 1)
            pool.wait_ge(sem("pool_chain"), chain[0])

        link(nc.gpsimd.iota(iota_h[:], [[1, 640]], base=0, channel_multiplier=0,
                            allow_small_or_imprecise_dtypes=True))
        link(nc.gpsimd.memset(src_i[:, EC:ECP], -2))
        nc.gpsimd.memset(dst_i[:, EC:ECP], -2).then_inc(sem("iota_done"), 1)
        pool.dma_start(a_bc[:], a[0, :].partition_broadcast(TP)).then_inc(sem("a_in"), 16)
        pool.dma_start(rw_in[:], router_w).then_inc(sem("rw_in"), 16)
        link(nc.gpsimd.memset(C[:], 0.0))
        pool.sem_inc(sem("counted"), 2)
        link(nc.gpsimd.memset(ones[:], 1.0))
        link(nc.gpsimd.affine_select(out=ident[:], in_=ones[:], pattern=[[-1, P]], compare_op=ALU.is_equal,
                                     fill=0.0, base=0, channel_multiplier=1))
        link(nc.gpsimd.affine_select(out=tri[:], in_=ones[:], pattern=[[1, P]], compare_op=ALU.is_gt,
                                     fill=0.0, base=0, channel_multiplier=-1))
        link(nc.gpsimd.memset(KV[:], 0.0))
        link(nc.gpsimd.iota(iota8[:], [[1, E]], base=0, channel_multiplier=0, allow_small_or_imprecise_dtypes=True))
        link(nc.gpsimd.iota(iotaslot[:], [[CAP, E]], base=CAP, channel_multiplier=0,
                            allow_small_or_imprecise_dtypes=True))
        link(nc.gpsimd.iota(iotacap[:], [[1, CAP]], base=0, channel_multiplier=0,
                            allow_small_or_imprecise_dtypes=True))
        link(nc.gpsimd.iota(tok_b[:, :, 0], [[0, NT]], base=0, channel_multiplier=1,
                            allow_small_or_imprecise_dtypes=True))
        link(nc.gpsimd.iota(tok_b[:, :, 1], [[1, NT]], base=0, channel_multiplier=0,
                            allow_small_or_imprecise_dtypes=True))
        nc.gpsimd.memset(rwT[:].bitcast(F32), 0.0).then_inc(sem("const_done"), 1)
        Ci = C[:].bitcast(I32)
        with pool.Fori(0, NG) as gr:
            pool.wait_ge(sem("digits"), gr * 2 + 2)
            nc.gpsimd.tensor_tensor(Ci[:, :, :, 0], Ci[:, :, :, 0], v_lo[:], ALU.add).then_inc(sem("counted"), 1)
            nc.gpsimd.tensor_tensor(Ci[:, :, :, 1], Ci[:, :, :, 1], v_int[:], ALU.add).then_inc(sem("counted"), 1)
        pool.wait_ge(sem("rwT_ps"), 1)
        pool.dma_start(b_bc[:], b_out.partition_broadcast(TP)).then_inc(sem("b_in"), 16)
        pool.wait_ge(sem("b_in"), 16)
        pool.wait_ge(sem("xn_done"), NT)
        for t in range(NT):
            nc.gpsimd.tensor_tensor(resid[:, t, :], resid[:, t, :], b_bc[:], ALU.add).then_inc(sem("biased"), 1)
        pool.wait_ge(sem("agg_ps"), 2 * NT)
        nc.gpsimd.memset(vv[:, :, :, P:VW], 1.0).then_inc(sem("v_ones"), 1)
        pool.wait_ge(sem("y_stored"), 16 * NT)
        pool.wait_ge(sem("tok_done"), 1)
        for e in range(E + 3):
            if 4 <= e < E:
                pool.wait_ge(sem("xgT_ps"), 2 * (e - 3))
            if e < E:
                nc.gpsimd.indirect_dma_start(
                    out=xg[e % 4][:], out_offset=None, in_=y_rows,
                    in_offset=bass.IndirectOffsetOnAxis(ap=tok_u[:, e:e + 1], axis=0)).then_inc(
                        sem(f"xg_in{e % 4}"), 16)
            if e >= 4:
                s = e - 3
                pool.wait_ge(sem("st_lo_done"), 2 * (s + 1))
                pool.dma_start(xgT_hi_d[s], st_hi[s % 2][:].bitcast(F32)).then_inc(sem(f"st_stored{s % 2}"), 16)
                pool.dma_start(xgT_lo_d[s], st_lo[s % 2][:].bitcast(F32)).then_inc(sem(f"st_stored{s % 2}"), 16)
        for i in range(2):
            pool.wait_ge(sem(f"st_stored{i}"), 2 * 16 * ((E - 1 + i) // 2))
        link(nc.gpsimd.memset(eout[:], 0.0))
        nc.gpsimd.memset(eout_st[:], 0.0).then_inc(sem("eout_clear"), 1)

        def turn_over(e):
            pool.wait_ge(sem("rd_added"), e * (2 * Q) + 2)
            pool.sem_inc(sem("turns"), 1)
            nc.gpsimd.tensor_copy(eout_st[:], eout[:]).then_inc(sem("eout_copied"), 1)
            pool.wait_ge(sem("eout_copied"), e + 1)
            pool.sem_inc(sem("turns"), 1)
            nc.gpsimd.memset(eout[:], 0.0).then_inc(sem("eout_clear"), 1)
            pool.dma_start(eout_d[bass.ds(e * CAP, CAP), :], eout_st[:]).then_inc(sem("eout_stored"), 16)
            pool.wait_ge(sem("eout_stored"), e * 16 + 16)

        with pool.Fori(0, E - 1) as e:
            turn_over(e)
            pool.wait_ge(sem("unit_used"), e * (Q * U) + ((Q - 1) * U + A_END[1] + USED0))
            pool.dma_start(xgT_hi[:].bitcast(F32), xgT_hi_d[e + 1]).then_inc(sem("xgT_in"), 16)
            pool.dma_start(xgT_lo[:].bitcast(F32), xgT_lo_d[e + 1]).then_inc(sem("xgT_in"), 16)
            pool.wait_ge(sem("xgT_in"), e * 32 + 32)
            pool.sem_inc(sem("xgT_ready"), 1)
        turn_over(E - 1)
        pool.wait_ge(sem("rd_added"), 2 * Q * E + 2)
        pool.dma_start(eout_d[E * CAP:(E + 1) * CAP, :], eout[:]).then_inc(sem("eout_stored"), 16)
        pool.wait_ge(sem("eout_stored"), 16 * (E + 1))
        pool.wait_ge(sem("sd_added"), 2 * NT * Q * E + ONE)
        for t in range(NT):
            for c in range(2):
                nc.gpsimd.indirect_dma_start(
                    out=got[c][t][:], out_offset=None, in_=eout_d,
                    in_offset=bass.IndirectOffsetOnAxis(ap=pos_u[:, c, t:t + 1], axis=0)).then_inc(
                        sem(f"g_in{c}_{t}"), 16)

    @block.scalar
    def _(act):
        def count_group(gr, extra):
            for i, c in enumerate(ACT_CHUNKS):
                col = gr * EG + c
                if c >= 4:
                    act.wait_ge(sem("onehot_used"), gr * (EG - 1) + (c - 3))
                if i >= 2:
                    act.wait_ge(sem("onehot_act"), gr * len(ACT_CHUNKS) + i - 1)
                elif i == 0 and not (isinstance(gr, int) and gr == 0):
                    act.wait_ge(sem("onehot_act"), gr * len(ACT_CHUNKS))
                nc.scalar.activation(sq_s[i % 2][:, 0:314], iota_h[:, 0:314], ACT.Square,
                                     bias=src_n[:, bass.ds(col, 1)]).then_inc(sem("sq_s"), 1)
                act.wait_ge(sem("sq_s"), gr * len(ACT_CHUNKS) + i + 1)
                nc.scalar.activation(oh_s[c % 4][:, 0:314], sq_s[i % 2][:, 0:314], ACT.Relu, scale=dig_n[:, bass.ds(col, 1)],
                                     bias=dig_f[:, bass.ds(col, 1)]).then_inc(sem("onehot_act"), 1)
                if i == len(ACT_CHUNKS) // 2:
                    extra()
            for dt in range(NT):
                act.wait_ge(sem("count_done"), gr * NT + dt + 1)
                if dt == 0:
                    act.wait_ge(sem("counted"), gr * 2 + 2)
                nc.scalar.copy(v_int[:, dt, :], PS[dt][0:TP, 0:SC]).then_inc(sem("count_out"), 1)

        def w_hi(g):
            if g % 2 == 0:
                act.wait_ge(sem(f"wl_in{g // 2}"), 16)
            if g == 1:
                act.wait_ge(sem("counted"), 2 * NG + 2)
            if g >= 2:
                act.wait_ge(sem("proj"), proj_n(g - 2, NT - 1))
            nc.scalar.copy(wT_hi[g % 2][:], quarter(g)).then_inc(sem("w_hi"), 1)

        def std(tile):
            def f():
                act.wait_ge(sem("var_done"), tile)
                nc.scalar.activation(rstd[:, 0:1], mv[:, 0, 1:2], ACT.Sqrt).then_inc(sem("std_done"), 1)
            return f

        def split_hi(n, part):
            act.wait_ge(sem("turned"), n + 1)
            nc.scalar.copy(part[0], part[2]).then_inc(sem("turned_hi"), 1)

        def w_part(g, i):
            split_hi(fill_w(g, i), weights_part(g, i))

        def feature_exp(n, parts, cols):
            act.wait_ge(sem("fm_done"), n + 1)
            if n >= 2:
                act.wait_ge(sem("fe_used"), n - 1)
            nc.scalar.activation(fe[n % 2][0:parts, 0:cols], fm[n % 2][0:parts, 0:cols],
                                 ACT.Exp).then_inc(sem("fe_done"), 1)

        act.wait_ge(sem("indices"), 1)
        count_group(0, lambda: w_hi(0))
        with act.Fori(1, NG) as gr:
            count_group(gr, std(gr))
        for j in range(2 * NT):
            split_hi(j, tokens_part(xnT_hi, xnT_lo, j, j))
        act.wait_ge(sem("rwT_ps"), 1)
        act.wait_ge(sem("const_done"), 1)
        nc.scalar.copy(rw_half(0), PS[7][:, 0:KT * E].rearrange("p (k n) -> p k n", k=KT)).then_inc(sem("rwT_hi"), 1)
        w_hi(1)
        w_hi(2)
        for half in range(2):
            for t in range(NT):
                act.wait_ge(sem("proj"), proj_n(2 * half + 1, t))
                nc.scalar.copy(h[:, t, half * HALF:(half + 1) * HALF], PS[t][0:TP, :]).then_inc(sem("h_out"), 1)
                if half == 1 and t < 4:
                    w_part(G_K, t)
            if half == 0:
                w_hi(3)
        for i in range(4):
            w_part(G_K + 1, i)
        for t in range(NT):
            feature_exp(t, TP, HALF)
            if t < 4:
                w_part(G_K + 2, t)
        for dt in range(NT):
            if dt < 4:
                w_part(G_K + 3, dt)
            act.wait_ge(sem("z_done"), dt + 1)
            nc.scalar.activation(zt[dt % 2][:], zt[dt % 2][:], ACT.Exp, scale=-1.0).then_inc(sem("ez_done"), 1)
        for t in range(NT):
            feature_exp(NT + t, TP, HALF)
            if t < 4:
                w_part(G_V, t)
        for j in range(2 * NT):
            feature_exp(2 * NT + j, TP, HALF)
        for half in range(2):
            for i in range(4):
                w_part(G_V + 2 * half + 1, i)
            for t in range(NT):
                act.wait_ge(sem("proj"), proj_n(G_V + 2 * half + 1, t))
                nc.scalar.copy(vv[:, t, half * 4:half * 4 + 4, 0:P],
                               PS[V_BANK[t]][0:TP, :].rearrange("p (j m) -> p j m", j=4)).then_inc(sem("v_out"), 1)
                if t < 4:
                    w_part(G_V + 2 * half + 2, t)
        for n in range(2 * PAIRS):
            g, i = divmod(n, 4)
            if n == 0:
                w_part(G_Q + 1, 0)
                w_part(G_Q + 1, 1)
            feature_exp(FE_Q + n, P, HALVES[n % 2][1])
            if n >= 2:
                w_part(G_Q + g + 1, i)
        for i in range(4):
            w_part(G_OUT + 1, i)
        for j in range(2 * NT):
            split_hi(OUT0 + j, tokens_part(outT_hi, outT_lo, OUT0 + j, j))
        for g in (G_OUT + 2, G_OUT + 3):
            for i in range(4):
                w_part(g, i)
        for t in range(NT):
            act.wait_ge(sem("var_done"), NT + t + 1)
            nc.scalar.activation(rstd[:, t:t + 1], mv[:, t, 1:2], ACT.Sqrt).then_inc(sem("std_done"), 1)
        for t in range(NT):
            act.wait_ge(sem("y_done"), t + 1)
            if t:
                act.wait_ge(sem("ms_done"), t)
            nc.scalar.activation(sq[:], y[:, t, :], ACT.Square,
                                 accum_out=rr["ms"][:, t:t + 1]).then_inc(sem("ms_done"), 1)
            for j in (2 * t, 2 * t + 1):
                split_hi(YT0 + j, tokens_part(yT_hi, yT_lo, YT0 + j, j))
        act.wait_ge(sem("rms_done"), 1)
        nc.scalar.activation(rr["r"][:, 0:NT], rr["ms"][:, 0:NT], ACT.Sqrt).then_inc(sem("rms_sqrt"), 1)
        act.wait_ge(sem("lgT_ps"), 1)
        nc.scalar.copy(lgT[:, 0:HALVES[0][1]], PS[0][0:2 * E, 0:HALVES[0][1]]).then_inc(sem("lgT_out"), 1)
        act.wait_ge(sem("lgT_ps"), 2)
        nc.scalar.copy(lgT[:, HALVES[1][0]:NP2], PS[1][0:2 * E, 0:HALVES[1][1]]).then_inc(sem("lgT_out"), 1)
        act.wait_ge(sem("lg_done"), 1)
        nc.scalar.activation(rt["pr"][:], rt["lg"][:], ACT.Exp).then_inc(sem("pr_done"), 1)
        for e in range(E):
            if e >= 3:
                act.wait_ge(sem(f"st_stored{e % 2}"), 2 * 16 * ((e - 1) // 2))
            for half in range(2):
                act.wait_ge(sem("xgT_ps"), 2 * e + half + 1)
                nc.scalar.copy((xgT_hi if e == 0 else st_hi[e % 2])[:, half * 4 * CAP:(half + 1) * 4 * CAP],
                               PS[(2 * e + half) % 4][:, 0:4 * CAP]).then_inc(sem("st_hi_done"), 1)

        with act.Fori(0, E) as e:
            with act.Fori(0, Q) as q:
                it = act.snap(e * Q + q)

                def hi(u):
                    r, part = SOURCE[u]
                    act.wait_ge(sem(f"raw_in{r % RAW}"), (it * (BLK // RAW) + r // RAW + 1) * 16)
                    act.wait_ge(sem("unit_used"), it * U + (u + 1 - RING + USED0))
                    nc.scalar.copy(unit_view(c_hi[u % RING], u), part(raw[r % RAW])).then_inc(sem("hi_done"), 1)

                def silu_routed(b):
                    act.wait_ge(sem("unit_used"), it * U + (A_END[b] + USED0))
                    act.wait_ge(sem("h_done"), it * 2 + b + ONE)
                    nc.scalar.activation(r_silu[:], PS[GATE][0:CAP, :], ACT.Silu).then_inc(sem("silu_done"), 1)

                def silu_shared(n):
                    if n % 2 == 0:
                        act.wait_ge(sem("s_half"), it * 2 + (n // 2 + 1))
                    else:
                        act.wait_ge(sem("unit_used"), it * U + (S_END[n // 2] + USED0))
                    act.wait_ge(sem("sh_mult"), it * 4 + max(n - 1, 0) + ONE)
                    w = HALVES[n % 2][1]
                    nc.scalar.activation(s_silu[n % 2][:, 0:w], PS[S_BANK[n]][:, 0:w],
                                         ACT.Silu).then_inc(sem("silu_done"), 1)

                def turned_hi(b):
                    act.wait_ge(sem("t_done"), it * 2 + b + 1)
                    nc.scalar.copy(hT_hi[:, b * 4 * CAP:(b + 1) * 4 * CAP],
                                   PS[T_BANK[b]][:, 0:4 * CAP]).then_inc(sem("thi_done"), 1)

                for u in range(18):
                    hi(u)
                silu_routed(0)
                silu_shared(0)
                silu_shared(1)
                hi(18)
                hi(19)
                silu_shared(2)
                silu_shared(3)
                hi(20)
                hi(21)
                turned_hi(0)
                for u in range(22, 30):
                    hi(u)
                silu_routed(1)
                turned_hi(1)

    @block.vector
    def _(dve):
        chain = [0]

        def link(ins):
            chain[0] += 1
            ins.then_inc(sem("dve_chain"), 1)
            dve.wait_ge(sem("dve_chain"), chain[0])

        V = nc.vector
        dve.wait_ge(sem("src_in"), 16)
        dve.wait_ge(sem("dst_in"), 16)
        dve.wait_ge(sem("iota_done"), 1)
        V.tensor_copy(dst_f[:], dst_i[:]).then_inc(sem("idx"), 1)
        link(V.tensor_scalar(tmp_i[:], src_i[:], 1, None, ALU.arith_shift_right))
        link(V.tensor_copy(src_f[:], tmp_i[:]))
        link(V.tensor_scalar(tmp_i[:], src_i[:], 1, None, ALU.bitwise_and))
        link(V.tensor_copy(dig_f[:], tmp_i[:]))
        link(V.tensor_scalar(dig_f[:], dig_f[:], DIGIT - 1.0, 1.0, ALU.mult, ALU.add))
        V.tensor_scalar(src_n[:], src_f[:], -1.0, None, ALU.mult).then_inc(sem("idx"), 1)
        V.tensor_scalar(dig_n[:], dig_f[:], -1.0, None, ALU.mult).then_inc(sem("indices"), 1)
        dve.wait_ge(sem("idx"), 2)

        xf = resid[:].rearrange("p t d -> p (t d)")
        xnf = xn[:].rearrange("p t d -> p (t d)")

        def digits(gr):
            dve.wait_ge(sem("count_out"), gr * NT + NT)
            dve.wait_ge(sem("counted"), gr * 2 + 2)
            V.tensor_scalar(v_lo[:], v_int[:], int(DIGIT) - 1, None, ALU.bitwise_and).then_inc(sem("digits"), 1)
            dve.wait_ge(sem("digits"), gr * 2 + 1)
            V.tensor_scalar(v_int[:], v_int[:], 12, None, ALU.arith_shift_right).then_inc(sem("digits"), 1)

        def w_lo(g):
            dve.wait_ge(sem("w_hi"), g + 1)
            V.tensor_tensor(wT_lo[g % 2][:], quarter(g), wT_hi[g % 2][:].bitcast(F32),
                            ALU.subtract).then_inc(sem("w_lo"), 1)

        def count_group(gr, first, between):
            for c in range(EG):
                col = gr * EG + c
                if c >= 4:
                    dve.wait_ge(sem("onehot_used"), gr * (EG - 1) + (c - 3))
                elif not first and c < 3:
                    dve.wait_ge(sem("onehot_used"), gr * (EG - 1) + (c - 2))
                elif not first:
                    dve.wait_ge(sem("count_done"), gr * NT)
                V.tensor_scalar(oh_d[c % 4][:, 0:626], iota_h[:, 0:626], dst_f[:, bass.ds(col, 1)], None,
                                ALU.is_equal).then_inc(sem("onehot"), 1)
                if c not in ACT_CHUNKS:
                    V.tensor_scalar(oh_s[c % 4][:, 0:314], iota_h[:, 0:314], src_f[:, bass.ds(col, 1)],
                                    dig_f[:, bass.ds(col, 1)], ALU.is_equal, ALU.mult).then_inc(sem("onehot"), 1)
                if c in between:
                    between[c]()

        def first_layernorm(gr):
            def stats():
                for half in range(2):
                    V.bn_stats(st6[:, 0, half, :],
                               xf[:, bass.ds((gr - 1) * D + half * HALF, HALF)]).then_inc(sem("ln"), 1)
                dve.wait_ge(sem("ln"), gr * 4 - 2)
                dve.sem_inc(sem("dve_turns"), 1)
                V.bn_aggr(mv[:, 0, :], st6[:, 0, :, :]).then_inc(sem("ln"), 1)
                dve.wait_ge(sem("ln"), gr * 4 - 1)
                V.tensor_scalar(mv[:, 0, 1:2], mv[:, 0, 1:2], EPS, None, ALU.add).then_inc(sem("var_done"), 1)

            def apply():
                dve.wait_ge(sem("std_done"), gr)
                V.reciprocal(rstd[:, 0:1], rstd[:, 0:1]).then_inc(sem("ln"), 1)
                dve.wait_ge(sem("ln"), gr * 4)
                V.tensor_scalar(xnf[:, bass.ds((gr - 1) * D, D)], xf[:, bass.ds((gr - 1) * D, D)], mv[:, 0, 0:1],
                                rstd[:, 0:1], ALU.subtract, ALU.mult).then_inc(sem("xn_done"), 1)
            return stats, apply

        count_group(0, True, {20: lambda: w_lo(0)})
        dve.wait_ge(sem("x_in"), 16 * NT)
        with dve.Fori(1, NG) as gr:
            stats, apply = first_layernorm(gr)
            count_group(gr, False, {9: lambda: digits(gr - 1), 13: stats, 20: apply})
        V.memset(xnT_hi[:, :, N:NP2].bitcast(F32), 0.0).then_inc(sem("pad"), 1)
        V.memset(xnT_lo[:, :, N:NP2].bitcast(F32), 0.0).then_inc(sem("pad"), 1)

        def split_lo(n, part):
            dve.wait_ge(sem("turned_hi"), n + 1)
            V.tensor_tensor(part[1], part[2], part[0].bitcast(F32), ALU.subtract).then_inc(sem("turned_lo"), 1)

        def w_part(g, i):
            split_lo(fill_w(g, i), weights_part(g, i))

        digits(NG - 1)
        for j in range(2 * NT):
            split_lo(j, tokens_part(xnT_hi, xnT_lo, j, j))
        dve.wait_ge(sem("rwT_hi"), 1)
        V.tensor_tensor(rw_half(1), PS[7][:, 0:KT * E].rearrange("p (k n) -> p k n", k=KT),
                        rw_half(0).bitcast(F32), ALU.subtract).then_inc(sem("rwT_lo"), 1)
        for g in range(1, G_K):
            w_lo(g)
        for i in range(4):
            w_part(G_K, i)
        dve.wait_ge(sem("a_in"), 16)
        for t in range(NT):
            dve.wait_ge(sem("h_out"), NT + t + 1)
            for c in range(2):
                link(V.tensor_tensor_reduce(out=scr[:], in0=h[:, t, :], in1=a_bc[:, c * D:(c + 1) * D], scale=1.0,
                                            scalar=0.0, op0=ALU.mult, op1=ALU.add, accum_out=al[:, t, c:c + 1]))
            V.tensor_scalar(diag[:, t, :], ident[0:TP, 0:TP], al[:, t, 0:1], None,
                            ALU.mult).then_inc(sem("diag_done"), 1)
            if t < 4:
                w_part(G_K + 1, t)

        def feature_min(n, ps, parts, cols, scale=None):
            if n >= 2:
                dve.wait_ge(sem("fe_done"), n - 1)
            if scale is None:
                V.tensor_scalar(fm[n % 2][0:parts, 0:cols], ps, 0.0, None, ALU.min).then_inc(sem("fm_done"), 1)
            else:
                V.tensor_scalar(fm[n % 2][0:parts, 0:cols], ps, scale, 0.0, ALU.mult,
                                ALU.min).then_inc(sem("fm_done"), 1)

        def feature_map(n, ps, parts, cols, dest):
            dve.wait_ge(sem("fe_done"), n + 1)
            V.scalar_tensor_tensor(out=dest, in0=ps, scalar=0.0, in1=fe[n % 2][0:parts, 0:cols], op0=ALU.max,
                                   op1=ALU.add).then_inc(sem("fe_used"), 1)

        def k_map(half, t, g, between=None):
            dve.wait_ge(sem("proj"), proj_n(G_K + 2 * half + 1, t))
            ps = PS[t][0:TP, :]
            feature_min(half * NT + t, ps, TP, HALF)
            if between:
                between()
            feature_map(half * NT + t, ps, TP, HALF, kk[:, t, half * HALF:(half + 1) * HALF])
            if t < 4:
                w_part(g, t)

        def albc_copy(part):
            dve.wait_ge(sem("albc_ps"), part + 1)
            cols = slice(0, 4 * TP) if part == 0 else slice(4 * TP, N)
            V.tensor_copy(albc[:, cols], PS[7][0:TP, 0:cols.stop - cols.start]).then_inc(sem("albc_out"), 1)

        dve.wait_ge(sem("diag_done"), NT)
        for t in range(NT):
            k_map(0, t, G_K + 2, {0: lambda: albc_copy(0), 1: lambda: albc_copy(1)}.get(t))
        dve.wait_ge(sem("albc_out"), 2)
        dve.wait_ge(sem("counted"), 2 * NG + 2)
        Cf = C[:].rearrange("p t c two -> p t (c two)")
        Ci = C[:].bitcast(I32).rearrange("p t c two -> p t (c two)")

        def edge_weights(dt):
            dve.wait_ge(sem("ez_done"), dt + 1)
            V.scalar_tensor_tensor(out=Cf[:, dt, 0:N], in0=zt[dt % 2][:], scalar=FMAX, in1=Ci[:, dt, 0:N],
                                   op0=ALU.min, op1=ALU.mult).then_inc(sem("ez_used"), 1)

        for dt in range(NT):
            if dt >= 2:
                edge_weights(dt - 2)
                dve.wait_ge(sem("ez_used"), dt - 1)
            link(V.tensor_scalar(zt[dt % 2][:], albc[:], al[:, dt, 1:2], None, ALU.add))
            V.scalar_tensor_tensor(out=zt[dt % 2][:], in0=zt[dt % 2][:], scalar=SLOPE, in1=zt[dt % 2][:],
                                   op0=ALU.mult, op1=ALU.max).then_inc(sem("z_done"), 1)
            if dt < 4:
                w_part(G_K + 3, dt)
        edge_weights(NT - 2)
        edge_weights(NT - 1)
        for t in range(NT):
            k_map(1, t, G_V)
        dve.wait_ge(sem("ez_used"), NT)
        dve.wait_ge(sem("rowsum_ps"), 1)
        link(V.tensor_scalar(rinv[:], PS[3][0:TP, 0:NT], EPS, None, ALU.add))
        link(V.reciprocal(rinv[:], rinv[:]))
        dve.wait_ge(sem("biased"), NT)
        for j in range(2 * NT):
            t, half = divmod(j, 2)
            nf = 2 * NT + j
            dve.wait_ge(sem("agg_ps"), j + 1)
            ps = PS[AGG_BANK[j % 4]][0:TP, :]
            feature_min(nf, ps, TP, HALF, scale=rinv[:, t:t + 1])
            r = resid[:, t, half * HALF:(half + 1) * HALF]
            V.tensor_scalar(gscr[j % 2][:], ps, rinv[:, t:t + 1], 0.0, ALU.mult, ALU.max).then_inc(sem("agg_used"), 1)
            dve.wait_ge(sem("agg_used"), j + 1)
            V.tensor_tensor(r, r, gscr[j % 2][:], ALU.add).then_inc(sem("agg_out"), 1)
            dve.wait_ge(sem("agg_out"), j + 1)
            dve.wait_ge(sem("fe_done"), nf + 1)
            V.scalar_tensor_tensor(out=r, in0=fe[nf % 2][0:TP, :], scalar=-1.0, in1=r, op0=ALU.add,
                                   op1=ALU.add).then_inc(sem("fe_used"), 1)
        for g in range(G_V + 1, G_Q + 1):
            for i in range(4):
                w_part(g, i)
        w_part(G_Q + 1, 0)
        w_part(G_Q + 1, 1)
        for b, (j0, cnt) in enumerate(TRIPLES):
            dve.wait_ge(sem("KV_ps"), b + 1)
            ps = PS[KV_BANK[b]][:, 0:cnt * VW].rearrange("p (j c) -> p j c", j=cnt)
            for i in range(2):
                o = slice(i * HD, (i + 1) * HD)
                V.tensor_copy(KV[o, j0:j0 + cnt, o], ps[o, :, o]).then_inc(sem("KV_out"), 1)
                V.tensor_copy(KV[o, j0:j0 + cnt, P + i:P + i + 1], ps[o, :, P:P + 1]).then_inc(sem("KV_out"), 1)
        for n in range(2 * PAIRS):
            j, hf = divmod(n, 2)
            o, w = HALVES[hf]
            dve.wait_ge(sem("q_ps"), n + 1)
            ps = PS[Q_BANK[n % 6]][:, 0:w]
            feature_min(FE_Q + n, ps, P, w)
            feature_map(FE_Q + n, ps, P, w, qT[:, j, o:o + w])
            if n >= 2:
                w_part(G_Q + n // 4 + 1, n % 4)
        for i in range(4):
            w_part(G_OUT + 1, i)
        for t in range(NT + 1):
            if t < NT:
                dve.wait_ge(sem("att_ps"), t + 1)
                banks = [PS[b][0:TP, 0:cnt * VW].rearrange("p (j c) -> p j c", j=cnt)
                         for b, (j0, cnt) in zip(ATT_BANK[t % 2], TRIPLES)]
                for ps, (j0, cnt) in zip(banks, TRIPLES):
                    V.tensor_scalar(dn[:, j0:j0 + cnt, :], ps[:, :, P:VW], 1e-6, None, ALU.add).then_inc(sem("dn"), 1)
                dve.wait_ge(sem("dn"), 3 * (t + 1))
                link(V.reciprocal(dr[:], dn[:]))
                if t >= 2:
                    dve.wait_ge(sem("turned"), OUT0 + 2 * (t - 1))
                for ps, (j0, cnt) in zip(banks, TRIPLES):
                    ins = V.tensor_tensor(
                        att[t % 2][:, j0 * P:(j0 + cnt) * P].rearrange("p (j two m) -> p j two m", j=cnt, two=2),
                        ps[:, :, 0:P].rearrange("p j (two m) -> p j two m", two=2),
                        dr[:, j0:j0 + cnt, :].unsqueeze(3).to_broadcast([TP, cnt, 2, HD]), ALU.mult)
                ins.then_inc(sem("att_done"), 1)
            if t >= 1:
                for j in (2 * t - 2, 2 * t - 1):
                    split_lo(OUT0 + j, tokens_part(outT_hi, outT_lo, OUT0 + j, j))
        def residual_add(half, t):
            dve.wait_ge(sem("proj"), proj_n(G_OUT + 2 * half + 1, t))
            r = resid[:, t, half * HALF:(half + 1) * HALF]
            V.tensor_tensor(r, PS[t][0:TP, :], r, ALU.add).then_inc(sem("o_out"), 1)
            dve.wait_ge(sem("o_out"), half * NT + t + 1)
            link(V.bn_stats(st6[:, t, half, :], r))

        def normalize(t):
            dve.wait_ge(sem("std_done"), NT + t + 1)
            link(V.reciprocal(rstd[:, t:t + 1], rstd[:, t:t + 1]))
            V.tensor_scalar(y[:, t, :], resid[:, t, :], mv[:, t, 0:1], rstd[:, t:t + 1], ALU.subtract,
                            ALU.mult).then_inc(sem("y_done"), 1)

        for t in range(NT):
            if t < 4:
                w_part(G_OUT + 2, t)
            residual_add(0, t)
        for i in range(4):
            w_part(G_OUT + 3, i)
        V.memset(yT_hi[:, :, N:NP2].bitcast(F32), 0.0).then_inc(sem("pad"), 1)
        V.memset(yT_lo[:, :, N:NP2].bitcast(F32), 0.0).then_inc(sem("pad"), 1)
        for t in range(NT):
            residual_add(1, t)
            link(V.bn_aggr(mv[:, t, :], st6[:, t, :, :]))
            V.tensor_scalar(mv[:, t, 1:2], mv[:, t, 1:2], EPS, None, ALU.add).then_inc(sem("var_done"), 1)
            if t:
                normalize(t - 1)
        normalize(NT - 1)
        for j in range(2 * NT):
            split_lo(YT0 + j, tokens_part(yT_hi, yT_lo, YT0 + j, j))
        T = rt
        bc = [TP, NT, E]

        def wide(v):
            return v[:, 0:NT].unsqueeze(2).to_broadcast(bc)

        dve.wait_ge(sem("ms_done"), NT)
        V.tensor_scalar(rr["ms"][:, 0:NT], rr["ms"][:, 0:NT], 1.0 / D, RMS_EPS, ALU.mult,
                        ALU.add).then_inc(sem("rms_done"), 1)
        dve.wait_ge(sem("rms_sqrt"), 1)
        link(V.reciprocal(rr["r"][:, 0:NT], rr["r"][:, 0:NT]))
        dve.wait_ge(sem("lg_ps"), 1)
        lgs = PS[4][0:TP, 0:NT * 2 * E].rearrange("p (t two e) -> p t two e", t=NT, two=2)
        link(V.tensor_copy(T["lg"][:], lgs[:, :, 0, :]))
        link(V.tensor_tensor(T["lg"][:], T["lg"][:], lgs[:, :, 1, :], ALU.add))
        link(V.tensor_tensor(T["lg"][:], T["lg"][:], wide(rr["r"]), ALU.mult))
        link(V.tensor_reduce(rr["mx"][:, 0:NT], T["lg"][:], AXX, ALU.max))
        V.tensor_tensor(T["lg"][:], T["lg"][:], wide(rr["mx"]), ALU.subtract).then_inc(sem("lg_done"), 1)
        dve.wait_ge(sem("pr_done"), 1)
        link(V.tensor_reduce(rr["sum"][:, 0:NT], T["pr"][:], AXX, ALU.add))
        link(V.reciprocal(rr["sum"][:, 0:NT], rr["sum"][:, 0:NT]))
        link(V.tensor_tensor(T["pr"][:], T["pr"][:], wide(rr["sum"]), ALU.mult))
        dve.wait_ge(sem("const_done"), 1)
        for t in range(NT):
            V.max(T["v8"][:, t, :], T["pr"][:, t, :]).then_inc(sem("top"), 1)
        dve.wait_ge(sem("top"), NT)
        for t in range(NT):
            V.max_index(i8[:, t, :], T["v8"][:, t, :], T["pr"][:, t, :]).then_inc(sem("top"), 1)
        dve.wait_ge(sem("top"), 2 * NT)
        link(V.tensor_copy(T["if8"][:], i8[:]))
        for c, oh in enumerate(("oh1", "oh2")):
            link(V.tensor_tensor(T[oh][:], iota8[:].unsqueeze(1).to_broadcast(bc),
                                 T["if8"][:, :, c:c + 1].to_broadcast(bc), ALU.is_equal))
        V.tensor_tensor(T["mask"][:], T["oh1"][:], T["oh2"][:], ALU.add).then_inc(sem("mask_done"), 1)
        link(V.tensor_tensor(rr["den"][:, 0:NT], T["v8"][:, :, 0], T["v8"][:, :, 1], ALU.add))
        link(V.reciprocal(rr["den"][:, 0:NT], rr["den"][:, 0:NT]))
        dve.wait_ge(sem("rank_ps"), 1)
        dve.wait_ge(sem("mask_done"), 1)
        link(V.tensor_copy(T["rank"][:], PS[7][0:TP, 0:NT * E].rearrange("p (t e) -> p t e", t=NT)))
        link(V.tensor_scalar(T["t1"][:], T["rank"][:], 1.0, None, ALU.add))
        link(V.tensor_tensor(T["t1"][:], T["t1"][:], T["mask"][:], ALU.mult))
        link(V.tensor_scalar(T["t1"][:], T["t1"][:], 1.0, None, ALU.subtract))
        te = T["t1"][:].rearrange("p t e -> p (t e)")
        V.tensor_tensor(S[:].rearrange("p t e c -> p (t e) c"), iotacap[:].unsqueeze(1).to_broadcast([TP, NT * E, CAP]),
                        te.unsqueeze(2).to_broadcast([TP, NT * E, CAP]), ALU.is_equal).then_inc(sem("S_done"), 1)
        dve.wait_ge(sem("tok_ps"), 1)
        link(V.tensor_copy(slot_tok[:], PS[5][0:CAP, 0:2 * E].rearrange("p (e two) -> p e two", two=2)[:, :, 0]))
        link(V.scalar_tensor_tensor(out=slot_tok[:], in0=PS[5][0:CAP, 0:2 * E].rearrange("p (e two) -> p e two", two=2)[:, :, 1],
                                    scalar=float(TP), in1=slot_tok[:], op0=ALU.mult, op1=ALU.add))
        V.tensor_copy(tok_u[:], slot_tok[:]).then_inc(sem("tok_done"), 1)
        dve.wait_ge(sem("S_done"), 1)
        link(V.tensor_scalar(T["keep"][:], T["rank"][:], float(CAP), None, ALU.is_lt))
        link(V.tensor_scalar(T["slot"][:], T["rank"][:], float(CAP - 1), None, ALU.min))
        link(V.tensor_tensor(T["slot"][:], T["slot"][:], iotaslot[:].unsqueeze(1).to_broadcast(bc), ALU.add))
        for c, (oh, kv_, ps_) in enumerate((("oh1", "k1", "p1"), ("oh2", "k2", "p2"))):
            link(V.tensor_tensor(T["t1"][:], T[oh][:], T["keep"][:], ALU.mult))
            link(V.tensor_reduce(rr[kv_][:, 0:NT], T["t1"][:], AXX, ALU.add))
            link(V.tensor_tensor(T["t2"][:], T[oh][:], T["slot"][:], ALU.mult))
            link(V.tensor_reduce(rr[ps_][:, 0:NT], T["t2"][:], AXX, ALU.add))
            link(V.tensor_copy(pos_u[:, c, 0:NT], rr[ps_][:, 0:NT]))
            link(V.tensor_tensor(rr[kv_][:, 0:NT], rr[kv_][:, 0:NT], rr["den"][:, 0:NT], ALU.mult))
            link(V.tensor_tensor(wts[:, c, 0:NT], rr[kv_][:, 0:NT], T["v8"][:, :, c], ALU.mult))
        for e in range(E):
            for half in range(2):
                s = slice(half * 4 * CAP, (half + 1) * 4 * CAP)
                dve.wait_ge(sem("st_hi_done"), 2 * e + half + 1)
                V.tensor_tensor((xgT_lo if e == 0 else st_lo[e % 2])[:, s], PS[(2 * e + half) % 4][:, 0:4 * CAP],
                                (xgT_hi if e == 0 else st_hi[e % 2])[:, s].bitcast(F32),
                                ALU.subtract).then_inc(sem("st_lo_done"), 1)
        V.memset(PS[R0][0:CAP, :], 0.0).then_inc(sem("rd_clear"), 1)
        V.memset(PS[R0 + 1][0:CAP, :], 0.0).then_inc(sem("rd_clear"), 1)
        dve.wait_ge(sem("rd_clear"), 2)

        def routed_add(step, cleared):
            dve.wait_ge(sem("unit_used"), step * U + USED0)
            dve.wait_ge(sem("eout_clear"), cleared)
            for half in range(2):
                r = eout[:, half * HALF:(half + 1) * HALF]
                V.tensor_tensor(r, PS[R0 + half][0:CAP, :], r, ALU.add).then_inc(sem("rd_added"), 1)

        dve.sem_inc(sem("lo_done"), U)
        dve.wait_ge(sem("st_lo_done"), 2)
        for name in ("h_done", "sh_mult", "tlo_done", "sd_added", "xgT_ready"):
            dve.sem_inc(sem(name), ONE)

        with dve.Fori(0, E) as e:
            with dve.Fori(0, Q) as q:
                it = dve.snap(e * Q + q)

                def lo(u):
                    r, part = SOURCE[u]
                    dve.wait_ge(sem("hi_done"), it * U + u + 1)
                    V.tensor_tensor(unit_view(c_lo[u % RING], u), part(raw[r % RAW]),
                                    unit_view(c_hi[u % RING], u).bitcast(F32),
                                    ALU.subtract).then_inc(sem("lo_done"), 1)

                def routed_inner(b):
                    dve.wait_ge(sem("silu_done"), it * 6 + (0, 5)[b] + 1)
                    V.tensor_tensor(r_h[b][:], PS[UP][0:CAP, :], r_silu[:], ALU.mult).then_inc(sem("h_done"), 1)

                def shared_inner(n):
                    j, hf = divmod(n, 2)
                    o, w = HALVES[hf]
                    dve.wait_ge(sem("silu_done"), it * 6 + n + 2)
                    V.tensor_tensor(s_h[hf][:, 0:w], PS[S_BANK[n] + 1][:, 0:w], s_silu[hf][:, 0:w],
                                    ALU.mult).then_inc(sem("sh_mult"), 1)
                    dve.wait_ge(sem("sh_mult"), it * 4 + n + 1 + ONE)
                    V.tensor_copy(sh_hi[:, j, o:o + w], s_h[hf][:, 0:w]).then_inc(sem("sh_hi_done"), 1)
                    dve.wait_ge(sem("sh_hi_done"), it * 4 + n + 1)
                    V.tensor_tensor(sh_lo[:, j, o:o + w], s_h[hf][:, 0:w], sh_hi[:, j, o:o + w].bitcast(F32),
                                    ALU.subtract).then_inc(sem("sh_ready"), 1)

                def turned_lo(b):
                    s = slice(b * 4 * CAP, (b + 1) * 4 * CAP)
                    dve.wait_ge(sem("thi_done"), it * 2 + b + 1)
                    V.tensor_tensor(hT_lo[:, s], PS[T_BANK[b]][:, 0:4 * CAP], hT_hi[:, s].bitcast(F32),
                                    ALU.subtract).then_inc(sem("tlo_done"), 1)

                def shared_add(n):
                    t, half = divmod(n, 2)
                    r = resid[:, t, half * HALF:(half + 1) * HALF]
                    dve.wait_ge(sem("sd_done"), it * (2 * NT) + n + 1)
                    V.tensor_tensor(r, PS[X0 + n % 4][0:TP, :], r, ALU.add).then_inc(sem("sd_added"), 1)

                for u in range(10):
                    lo(u)
                routed_add(it, ((it + (Q - 1)) >> 2) + 1)
                for u in range(10, 18):
                    lo(u)
                routed_inner(0)
                shared_inner(0)
                shared_inner(1)
                lo(18)
                lo(19)
                shared_inner(2)
                shared_inner(3)
                lo(20)
                lo(21)
                turned_lo(0)
                for u in range(22, 29):
                    lo(u)
                shared_add(0)
                lo(29)
                shared_add(1)
                routed_inner(1)
                for n in range(2, 2 * NT):
                    shared_add(n)
                turned_lo(1)
        routed_add(STEPS, E + 1)
        dve.wait_ge(sem("sd_added"), 2 * NT * Q * E + ONE)
        for t in range(NT):
            for c in range(2):
                dve.wait_ge(sem(f"g_in{c}_{t}"), 16)
                ins = V.scalar_tensor_tensor(out=resid[:, t, :], in0=got[c][t][:], scalar=wts[:, c, t:t + 1],
                                             in1=resid[:, t, :], op0=ALU.mult, op1=ALU.add)
                if c == 0:
                    link(ins)
            ins.then_inc(sem("out_done"), 1)

    @block.tensor
    def _(pe):
        MM = nc.tensor.matmul
        TR = nc.tensor.transpose

        def count_group(gr):
            for c in range(EG):
                pe.wait_ge(sem("onehot"), gr * DVE_ONEHOTS + 2 * (c + 1) - sum(a <= c for a in ACT_CHUNKS))
                if c in ACT_CHUNKS:
                    pe.wait_ge(sem("onehot_act"), gr * len(ACT_CHUNKS) + ACT_CHUNKS.index(c) + 1)
                for dt in range(NT):
                    if c == 0 and not (isinstance(gr, int) and gr == 0):
                        pe.wait_ge(sem("count_out"), gr * NT - (NT - 1 - dt))
                    m = MM(PS[dt][0:TP, 0:SC], oh_d[c % 4][:, dt * TP:(dt + 1) * TP], oh_s[c % 4][:, 0:SC],
                           start=(c == 0), stop=(c == EG - 1))
                    if c == EG - 1:
                        m.then_inc(sem("count_done"), 1)
                    elif dt == NT - 1:
                        m.then_inc(sem("onehot_used"), 1)
        count_group(0)
        with pe.Fori(1, NG) as gr:
            count_group(gr)

        def turn_tokens(n, src_, j):
            if n >= 2:
                pe.wait_ge(sem("turned_lo"), n - 1)
            for k in range(4):
                c = (4 * (j % 2) + k) * P
                m = TR(fill_bank(n)[:, k * TP:(k + 1) * TP], src_[:, c:c + P], ident[0:TP, 0:TP])
            m.then_inc(sem("turned"), 1)

        def turn(g, i):
            n = fill_w(g, i)
            ld = 2 + (g - G_K) // 2
            pe.wait_ge(sem(f"wl_in{ld % 2}"), 16 * (ld // 2 + 1))
            w = wl[ld % 2][:].rearrange("p (s k) -> p s k", s=4)
            pe.wait_ge(sem("turned_lo"), n - 1)
            for k in range(2):
                for s in range(2):
                    m = TR(fill_bank(n)[:, k * GW + s * P:k * GW + (s + 1) * P],
                           w[:, 2 * (g % 2) + s, (2 * i + k) * P:(2 * i + k + 1) * P], ident[:])
            m.then_inc(sem("turned"), 1)

        def group_ready(g):
            if g < G_K:
                pe.wait_ge(sem("w_lo"), g + 1)
            else:
                pe.wait_ge(sem("turned_lo"), fill_w(g, 3) + 1)

        def project(g, t, l_hi, l_lo, bank):
            ts = slice(t * TP, (t + 1) * TP)
            ps = PS[bank][0:TP, (g % 2) * GW:(g % 2 + 1) * GW]
            for k in range(KT):
                MM(ps, l_hi[:, k, ts], wT_hi[g % 2][:, k, :], start=(k == 0), stop=False)
                MM(ps, l_hi[:, k, ts], wT_lo[g % 2][:, k, :], start=False, stop=False)
                m = MM(ps, l_lo[:, k, ts], wT_hi[g % 2][:, k, :], start=False, stop=(k == KT - 1))
            m.then_inc(sem("proj"), 1)

        pe.wait_ge(sem("const_done"), 1)
        for j in range(2 * NT):
            pe.wait_ge(sem("xn_done"), j // 2 + 1)
            turn_tokens(j, xn[:, j // 2, :], j)
        pe.wait_ge(sem("rw_in"), 16)
        for k in range(KT):
            m = TR(PS[7][:, k * E:(k + 1) * E], rw_in[:, k * P:(k + 1) * P], ident[0:E, 0:E])
        m.then_inc(sem("rwT_ps"), 1)
        pe.wait_ge(sem("count_out"), NG * NT)
        for g in range(G_K):
            group_ready(g)
            for t in range(NT):
                if g == 0:
                    pe.wait_ge(sem("turned_lo"), 2 * t + 2)
                if g == 2:
                    pe.wait_ge(sem("h_out"), t + 1)
                project(g, t, xnT_hi, xnT_lo, t)
                if g == G_K - 1 and t < 4:
                    turn(G_K, t)
        for g in range(G_K, G_V):
            group_ready(g)
            for t in range(NT):
                if g == G_K:
                    pe.wait_ge(sem("h_out"), NT + t + 1)
                if g == G_K + 2:
                    pe.wait_ge(sem("fe_used"), t + 1)
                project(g, t, xnT_hi, xnT_lo, t)
                if g == G_K + 1 and t == 0:
                    pe.wait_ge(sem("diag_done"), NT)
                    pe.wait_ge(sem("rwT_lo"), 1)
                    for s in range(4):
                        m = MM(PS[7][0:TP, s * TP:(s + 1) * TP], ones[0:TP, 0:TP], diag[:, s, :], start=True, stop=True)
                    m.then_inc(sem("albc_ps"), 1)
                if g == G_K + 1 and t == 1:
                    pe.wait_ge(sem("albc_out"), 1)
                    MM(PS[7][0:TP, 0:TP], ones[0:TP, 0:TP], diag[:, 4, :], start=True,
                       stop=True).then_inc(sem("albc_ps"), 1)
                if t < 4:
                    turn(g + 1, t)
        pe.wait_ge(sem("ez_used"), NT)
        pe.wait_ge(sem("albc_out"), 2)
        Cf = C[:].rearrange("p t c two -> p t (c two)")
        for j in range(2 * NT):
            t, half = divmod(j, 2)
            if j == 1:
                pe.wait_ge(sem("fe_used"), 2 * NT)
            if j >= 4:
                pe.wait_ge(sem("agg_used"), j - 3)
            for dt in range(NT):
                m = MM(PS[AGG_BANK[j % 4]][0:TP, :], Cf[:, dt, t * TP:(t + 1) * TP],
                       h[:, dt, half * HALF:(half + 1) * HALF], start=(dt == 0), stop=(dt == NT - 1))
            m.then_inc(sem("agg_ps"), 1)
            if j == 0:
                pe.wait_ge(sem("fe_used"), 2 * NT - 1)
                for s in range(NT):
                    for dt in range(NT):
                        m = MM(PS[3][0:TP, s:s + 1], Cf[:, dt, s * TP:(s + 1) * TP], ones[0:TP, 0:1],
                               start=(dt == 0), stop=(dt == NT - 1))
                m.then_inc(sem("rowsum_ps"), 1)
        for g in range(G_V, G_Q):
            group_ready(g)
            for t in range(NT):
                if g == G_V:
                    pe.wait_ge(sem("agg_used"), (1, 1, 7, 8, 10)[t])
                if g == G_V + 2:
                    pe.wait_ge(sem("v_out"), t + 1)
                project(g, t, xnT_hi, xnT_lo, V_BANK[t])
                if t < 4:
                    turn(g + 1, t)
        for n in range(2 * PAIRS):
            g, i = G_Q + n // 4, n % 4
            if i == 0:
                group_ready(g)
            if n in (1, 2):
                pe.wait_ge(sem("v_out"), 2 * NT + n - 2)
            if n == 3:
                pe.wait_ge(sem("KV_out"), 4 * len(TRIPLES))
            if n >= 6:
                pe.wait_ge(sem("fe_used"), FE_Q + n - 5)
            o, w = HALVES[n % 2]
            c = slice((i // 2) * P, (i // 2 + 1) * P)
            ps = PS[Q_BANK[n % 6]][:, 0:w]
            for k in range(KT):
                MM(ps, wT_hi[g % 2][:, k, c], xnT_hi[:, k, o:o + w], start=(k == 0), stop=False)
                MM(ps, wT_hi[g % 2][:, k, c], xnT_lo[:, k, o:o + w], start=False, stop=False)
                m = MM(ps, wT_lo[g % 2][:, k, c], xnT_hi[:, k, o:o + w], start=False, stop=(k == KT - 1))
            m.then_inc(sem("q_ps"), 1)
            turn(g + 1, i)
            if n == 1:
                pe.wait_ge(sem("v_out"), 2 * NT)
                pe.wait_ge(sem("v_ones"), 1)
                for b, (j0, cnt) in enumerate(TRIPLES):
                    for j in range(j0, j0 + cnt):
                        for t in range(NT):
                            m = MM(PS[KV_BANK[b]][:, (j - j0) * VW:(j - j0 + 1) * VW], kk[:, t, j * P:(j + 1) * P],
                                   vv[:, t, j, :], start=(t == 0), stop=(t == NT - 1))
                    m.then_inc(sem("KV_ps"), 1)
        for i in range(4):
            turn(G_OUT + 1, i)
        pe.wait_ge(sem("fe_used"), FE_Q + 2 * PAIRS)
        for t in range(NT + 1):
            if t < NT:
                if t >= 2:
                    pe.wait_ge(sem("att_done"), t - 1)
                for b, (j0, cnt) in zip(ATT_BANK[t % 2], TRIPLES):
                    for j in range(j0, j0 + cnt):
                        m = MM(PS[b][0:TP, (j - j0) * VW:(j - j0 + 1) * VW], qT[:, j, t * TP:(t + 1) * TP], KV[:, j, :],
                               start=True, stop=True)
                m.then_inc(sem("att_ps"), 1)
            if t >= 1:
                pe.wait_ge(sem("att_done"), t)
                for j in (2 * t - 2, 2 * t - 1):
                    turn_tokens(OUT0 + j, att[(t - 1) % 2], j)
        for g in range(G_OUT, G_OUT + 4):
            group_ready(g)
            for t in range(NT):
                if g == G_OUT:
                    pe.wait_ge(sem("turned_lo"), OUT0 + 2 * t + 2)
                if g == G_OUT + 2:
                    pe.wait_ge(sem("o_out"), t + 1)
                project(g, t, outT_hi, outT_lo, t)
                if g in (G_OUT + 1, G_OUT + 2) and t < 4:
                    turn(g + 1, t)
        for j in range(2 * NT):
            pe.wait_ge(sem("y_done"), j // 2 + 1)
            turn_tokens(YT0 + j, y[:, j // 2, :], j)
        pe.wait_ge(sem("turned_lo"), YT0 + 2 * NT)
        pe.wait_ge(sem("o_out"), 2 * NT)
        pe.wait_ge(sem("const_done"), 1)
        for hf, (o, w) in enumerate(HALVES):
            for k in range(KT):
                lw = rwT[:, k * 2 * E:k * 2 * E + P]
                MM(PS[hf][:, 0:w], lw, yT_hi[:, k, o:o + w], start=(k == 0), stop=False)
                m = MM(PS[hf][:, 0:w], lw, yT_lo[:, k, o:o + w], start=False, stop=(k == KT - 1))
            m.then_inc(sem("lgT_ps"), 1)
        pe.wait_ge(sem("lgT_out"), 2)
        for t in range(NT):
            m = TR(PS[4][0:TP, t * 2 * E:(t + 1) * 2 * E], lgT[:, t * TP:(t + 1) * TP], ident[0:2 * E, 0:2 * E])
        m.then_inc(sem("lg_ps"), 1)
        pe.wait_ge(sem("mask_done"), 1)
        for t in range(NT):
            for s in range(t + 1):
                m = MM(PS[7][0:TP, t * E:(t + 1) * E], (tri if s == t else ones)[0:TP, 0:TP], rt["mask"][:, s, :],
                       start=(s == 0), stop=(s == t))
        m.then_inc(sem("rank_ps"), 1)
        pe.wait_ge(sem("S_done"), 1)
        for e in range(E):
            for t in range(NT):
                m = MM(PS[5][0:CAP, 2 * e:2 * e + 2], S[:, t, e, :], tok_b[:, t, :], start=(t == 0), stop=(t == NT - 1))
        m.then_inc(sem("tok_ps"), 1)
        for e in range(E):
            pe.wait_ge(sem(f"xg_in{e % 4}"), 16 * (e // 4 + 1))
            for half in range(2):
                if 2 * e + half >= 4:
                    pe.wait_ge(sem("st_lo_done"), 2 * e + half - 3)
                for k in range(4):
                    c = (4 * half + k) * P
                    m = TR(PS[(2 * e + half) % 4][:, k * CAP:(k + 1) * CAP], xg[e % 4][:, c:c + P],
                           ident[0:CAP, 0:CAP])
                m.then_inc(sem("xgT_ps"), 1)

        pe.wait_ge(sem("rd_clear"), 2)
        pe.sem_inc(sem("unit_used"), USED0)

        with pe.Fori(0, E) as e:
            with pe.Fori(0, Q) as q:
                it = pe.snap(e * Q + q)

                def split(u):
                    pe.wait_ge(sem("lo_done"), it * U + (U + u + 1))

                def three(out_, l_hi, l_lo, r_hi, r_lo, first, last):
                    MM(out_, l_hi, r_hi, start=first, stop=False)
                    MM(out_, l_hi, r_lo, start=False, stop=False)
                    return MM(out_, l_lo, r_hi, start=False, stop=last)

                def routed_up(b):
                    for i, bank in enumerate((GATE, UP)):
                        for k in range(KT):
                            u = UNITS_GATE[b] + 4 * i + k // 2
                            if k % 2 == 0:
                                split(u)
                            c = slice((k % 2) * HALF, (k % 2 + 1) * HALF)
                            xs = slice(k * CAP, (k + 1) * CAP)
                            m = three(PS[bank][0:CAP, :], xgT_hi[:, xs], xgT_lo[:, xs],
                                      c_hi[u % RING][:, c], c_lo[u % RING][:, c], k == 0, k == KT - 1)
                            if k % 2:
                                m.then_inc(sem("unit_used"), 1)

                def shared_up(n):
                    j, hf = divmod(n, 2)
                    o, w = HALVES[hf]
                    for i in range(2):
                        u = UNIT_S + 2 * j + i
                        split(u)
                        for k in range(KT):
                            c = slice(k * P, (k + 1) * P)
                            m = three(PS[S_BANK[n] + i][:, 0:w], c_hi[u % RING][:, c], c_lo[u % RING][:, c],
                                      yT_hi[:, k, o:o + w], yT_lo[:, k, o:o + w], k == 0, k == KT - 1)
                        if hf:
                            m.then_inc(sem("unit_used"), 1)
                    if not hf:
                        m.then_inc(sem("s_half"), 1)

                def turn_inner(b):
                    for k in range(4):
                        m = TR(PS[T_BANK[b]][:, k * CAP:(k + 1) * CAP], r_h[b][:, k * P:(k + 1) * P],
                               ident[0:CAP, 0:CAP])
                        if b == 1 and k == 0:
                            m.then_inc(sem("unit_used"), 1)
                    m.then_inc(sem("t_done"), 1)

                pe.wait_ge(sem("xgT_ready"), e + ONE)
                pe.wait_ge(sem("tlo_done"), it * 2 + ONE)
                pe.wait_ge(sem("h_done"), it * 2 + ONE)
                routed_up(0)
                pe.wait_ge(sem("sd_added"), it * (2 * NT) + ONE)
                shared_up(0)
                shared_up(1)
                pe.wait_ge(sem("rd_added"), it * 2 + 2)
                shared_up(2)
                pe.wait_ge(sem("sh_mult"), it * 4 + 1 + ONE)
                shared_up(3)
                pe.wait_ge(sem("h_done"), it * 2 + 1 + ONE)
                pe.wait_ge(sem("sh_mult"), it * 4 + 2 + ONE)
                turn_inner(0)
                routed_up(1)
                pe.wait_ge(sem("sh_ready"), it * 4 + 4)
                split(UNIT_SD)
                split(UNIT_SD + 1)
                for n in range(2 * NT):
                    t, half = divmod(n, 2)
                    if n == 2:
                        pe.wait_ge(sem("tlo_done"), it * 2 + 1 + ONE)
                    if n >= 4:
                        pe.wait_ge(sem("sd_added"), it * (2 * NT) + (n - 3) + ONE)
                    c = slice(half * HALF, (half + 1) * HALF)
                    for j in range(2):
                        u = UNIT_SD + j
                        ts = slice(t * TP, (t + 1) * TP)
                        m = three(PS[X0 + n % 4][0:TP, :], sh_hi[:, j, ts], sh_lo[:, j, ts],
                                  c_hi[u % RING][:, c], c_lo[u % RING][:, c], j == 0, j == 1)
                        if n == 2 * NT - 1 and j == 0:
                            m.then_inc(sem("unit_used"), 1)
                    m.then_inc(sem("sd_done"), 1)
                pe.wait_ge(sem("h_done"), it * 2 + 2 + ONE)
                turn_inner(1)
                for k in range(8):
                    u = UNIT_RD + k
                    if k % 4 == 0:
                        pe.wait_ge(sem("tlo_done"), it * 2 + (k // 4 + 1) + ONE)
                    split(u)
                    xs = slice(k * CAP, (k + 1) * CAP)
                    for half in range(2):
                        c = slice(half * HALF, (half + 1) * HALF)
                        m = three(PS[R0 + half][0:CAP, :], hT_hi[:, xs], hT_lo[:, xs],
                                  c_hi[u % RING][:, c], c_lo[u % RING][:, c], k == 0, k == 7)
                    m.then_inc(sem("unit_used"), 1)

    ctx.close()


_INS = ["x", "src", "dst", "L0_gnn_W", "L0_gnn_a", "L0_mix_w_qkv", "L0_mix_w_out", "L0_mix_b_out",
        "L0_ffn_router_w", "L0_ffn_rg", "L0_ffn_ru", "L0_ffn_rd", "L0_ffn_sg", "L0_ffn_su", "L0_ffn_sd"]


def kernel(**inputs):
    import numpy as _np
    import concourse.bacc as _bacc
    from concourse import mybir as _mybir
    from concourse.bass_utils import run_bass_kernel_spmd as _run

    nc = _bacc.Bacc("TRN2", target_bir_lowering=False, num_devices=1)
    arrays, args = {}, []
    for name in _INS:
        v = _np.ascontiguousarray(inputs[name])
        arrays[f"in_{name}"] = v
        args.append(nc.dram_tensor(f"in_{name}", v.shape, _mybir.dt.from_np(v.dtype), kind="ExternalInput").ap())
    res = nc.dram_tensor("out_0", (N, D), _mybir.dt.float32, kind="ExternalOutput").ap()
    build(nc, *args, res)
    r = _run(nc, [arrays], core_ids=[0])
    return r.results[0]["out_0"]
```

```python
from contextlib import ExitStack

import numpy as np

import concourse.bass as bass
from concourse import mybir

F32 = mybir.dt.float32
F32R = mybir.dt.float32r
BF16 = mybir.dt.bfloat16
F16 = mybir.dt.float16
I32 = mybir.dt.int32
U32 = mybir.dt.uint32
ALU = mybir.AluOpType
ACT = mybir.ActivationFunctionType
AXX = mybir.AxisListType.X

P = 128
N = 625
TP = 125
NT = N // TP
D = 1024
KT = D // P
HALF = 512
E = 8
CAP = int(1.25 * N / E)
IR = 4 * D
IS = 8 * D
NE = 20625
EC = NE // TP
EG = 28
NG = 6
ECP = EG * NG
DIGIT = 4096.0
SC = (N + 1) // 2
NP2 = 626
HALVES = ((0, 314), (314, 312))
HEADS = 16
HD = 64
PAIRS = HEADS // 2
EPS = 1e-5
RMS_EPS = float(np.finfo(np.float32).eps)
FMAX = float(np.finfo(np.float32).max)
SLOPE = 0.1
Q = 4
U = 30
TOGETHER = 2
RING = 10
RAW = 3
BLK = 15
STEPS = E * Q
USED0 = RING + 1
ONE = 1
A0, X0, R0 = 0, 2, 6
T_BANK = (A0 + 1, A0)


TB = (5, 6, 7)
GW = 256
G_K, G_V, G_Q, G_OUT = 4, 8, 12, 16
ACT_CHUNKS = (3, 5, 7, 9, 12, 14, 16, 18, 21, 23, 25, 27)
SLOTS = 7
DVE_ONEHOTS = 2 * EG - len(ACT_CHUNKS)
VW = P + 2
FE_Q = 4 * NT
TRIPLES = ((0, 3), (3, 3), (6, 2))
RANK_BANK, TOK_BANK = 0, 1
AGG_BANK = (7, 0, 1, 2)
V_BANK = (3, 4, 1, 2, 0)
KV_BANK = (3, 4, 1)
Q_PARTS = ((0, 1), (2,), (3,), ())
Q_BANK = (7, 2, 0, 3, 4, 1)
ATT_BANK = ((4, 1, 7), (2, 0, 3))


class Order:

    def __init__(self, s, gate, sd, rd, a_bank, s_bank):
        self.s, self.gate, self.sd, self.rd = s, gate, sd, rd
        self.a_bank = a_bank
        self.s_bank = s_bank
        self.s_end = (s + 2, s + 4)
        self.a_end = (gate[0] + 8, gate[1] + 8)
        self.silu_s, self.silu_r = (0, 4) if s < gate[0] else (2, 0)
        self.last_unit = [max(u for u in range(U) if self.source(u)[0] == b) for b in range(BLK)]

    def shared(self, u):
        return self.s <= u < self.s + 4

    def source(self, u):
        def rows(half):
            return lambda t: t[:, half * 1024:(half + 1) * 1024]

        def columns(j):
            return lambda t: t[:].rearrange("p (k n) -> p k n", k=KT)[:, :, j * P:(j + 1) * P]

        if self.shared(u):
            return (self.s + (u - self.s) % 2 * 2) // 2, columns((u - self.s) // 2)
        return u // 2, rows(u % 2)

    def view(self, t, u):
        return t[:].rearrange("p (k n) -> p k n", k=KT) if self.shared(u) else t[:]


def count(e, q, per_step, n):
    return e * (Q * per_step) + (q * per_step + n)


STEP = Order(s=0, gate=(4, 12), sd=20, rd=22, a_bank=(A0, R0), s_bank=(X0, X0 + 2, R0, X0))
LAST = Order(s=24, gate=(0, 8), sd=28, rd=16, a_bank=(A0, X0), s_bank=(X0, X0 + 2, R0, A0))


def build(nc, x, src, dst, W, a, w_qkv, w_out, b_out, router_w, rg, ru, rd, sg, su, sd, out):
    ctx = ExitStack()
    sems = {}

    def sem(name):
        if name not in sems:
            sems[name] = ctx.enter_context(nc.semaphore(name))
        return sems[name]

    cursor = [16512]

    def place(name, shape, dt, at=None):
        size = int(np.prod(shape[1:])) * mybir.dt.size(dt)
        size = (size + 31) // 32 * 32
        off = cursor[0] if at is None else at
        if at is None:
            cursor[0] += size
        return nc.alloc_sbuf_tensor_at(name, shape, dt, offset=off)

    def here():
        return cursor[0]

    resid = place("resid", [TP, NT, D], F32)
    ident = place("ident", [P, P], F32)
    ones = place("ones", [P, P], F32)
    tri = place("tri", [P, P], BF16)
    ones_b = place("ones_b", [P, P], BF16)
    pos_u = place("pos_u", [TP, 2, 8], U32)
    wts = place("wts", [TP, 2, 8], F32)
    tok_u = place("tok_u", [CAP, E], U32)
    tok_cur = place("tok_cur", [CAP, 1], U32)
    raw_at = here()
    raw = [place(f"raw{r}", [P, 2048], F32) for r in range(RAW)]
    shared_at = here()
    yT_hi = place("yT_hi", [P, KT, NP2], F32R)
    yT_lo = place("yT_lo", [P, KT, NP2], F32R)
    conv_at = here()
    c_hi = [place(f"c_hi{s}", [P, 1024], F32R) for s in range(RING)]
    c_lo = [place(f"c_lo{s}", [P, 1024], F32R) for s in range(RING)]
    xgT_hi = place("xgT_hi", [P, KT * CAP], F32R)
    xgT_lo = place("xgT_lo", [P, KT * CAP], F32R)
    sh_hi = place("sh_hi", [P, 2, NP2], F32R)
    sh_lo = place("sh_lo", [P, 2, NP2], F32R)
    s_silu = [place(f"s_silu{i}", [P, 314], F32) for i in range(2)]
    s_h = [place(f"s_h{i}", [P, 314], F32) for i in range(2)]
    r_silu = place("r_silu", [CAP, HALF], F32)
    r_h_at = here()
    r_h = [place(f"r_h{i}", [CAP, HALF], F32) for i in range(2)]
    hT_hi = place("hT_hi", [P, 8 * CAP], F32R)
    hT_lo = place("hT_lo", [P, 8 * CAP], F32R)
    eout = place("eout", [CAP, D], F32)
    out_at = here()
    eout_st = place("eout_st", [CAP, D], F32)
    xg = place("xg", [CAP, D], F32, at=out_at)
    eout_end = here()
    assert here() <= 229344, here()
    cursor[0] = raw_at
    C = place("C", [TP, NT, SC, 2], F32)
    a_at = here()
    a_bc = place("a_bc", [TP, 2 * D], F32)
    albc = place("albc", [TP, N], F32)
    assert here() <= shared_at, (here(), shared_at)
    cursor[0] = a_at
    fm = [place(f"fm{i}", [P, HALF], F32) for i in range(2)]
    fe = [place(f"fe{i}", [P, HALF], F32) for i in range(2)]
    assert here() <= a_at + 2 * D * 4
    wl = [place(f"wl{i}", [P, 4 * D], F32, at=shared_at + i * 16384) for i in range(2)]
    cursor[0] = shared_at + 2 * 16384
    al = place("al", [TP, NT, 2], F32)
    rinv = place("rinv", [TP, NT], F32)
    diag = place("diag", [TP, NT, TP], F32)
    rw_at = here()
    rw_in = place("rw_in", [E, D], F32)
    b_bc = place("b_bc", [TP, D], F32, at=rw_at)
    assert here() <= conv_at
    cursor[0] = conv_at
    xnT_hi = place("xnT_hi", [P, KT, NP2], F32R)
    outT_hi = place("outT_hi", [P, KT, NP2], F32R, at=conv_at)
    lo_at = here()
    xnT_lo = place("xnT_lo", [P, KT, NP2], F32R)
    outT_lo = place("outT_lo", [P, KT, NP2], F32R, at=lo_at)
    wT_at = here()
    wT_hi, wT_lo = [], []
    buf_at = []
    for i in range(2):
        buf_at.append(here())
        wT_hi.append(place(f"wT_hi{i}", [P, KT, GW], F32R))
        wT_lo.append(place(f"wT_lo{i}", [P, KT, GW], F32R))
    h_at = here()
    vv = place("vv", [TP, NT, PAIRS, VW], F32)
    h = place("h", [TP, NT, D], F32, at=h_at)
    xn = place("xn", [TP, NT, D], F32, at=h_at)
    att = [place(f"att{i}", [TP, D], F32, at=h_at + i * 4 * D) for i in range(2)]
    sq = place("sq", [TP, D], F32, at=h_at + 2 * 4 * D)
    k_at = here()
    kk = place("kk", [TP, NT, D], F32)
    qT = place("qT", [P, PAIRS, NP2], F32, at=k_at)
    y = place("y", [TP, NT, D], F32, at=k_at)
    scr = place("scr", [TP, D], F32, at=k_at)
    tail_at = here()
    zt = [place(f"zt{i}", [TP, N], F32) for i in range(2)]
    KV = place("KV", [P, PAIRS, VW], F32)
    gscr = [place(f"gscr{i}", [TP, HALF], F32, at=tail_at + i * 2048) for i in range(2)]
    dn = place("dn", [TP, PAIRS, 2], F32, at=tail_at + 2 * 2048)
    dr = place("dr", [TP, PAIRS, 2], F32, at=tail_at + 2 * 2048 + 64)
    late_at = max(here(), eout_end)
    late_end = 229344
    cursor[0] = late_at
    rwT = place("rwT", [P, KT * 2 * E + P], F32R)
    mv = place("mv", [TP, NT, 2], F32)
    st6 = place("st6", [TP, NT, 2, 6], F32)
    rstd = place("rstd", [TP, NT], F32)
    rr = {n: place("rr_" + n, [TP, 8], F32) for n in
          ("ms", "r")}
    tok_b = place("tok_b", [TP, NT, 2], BF16)
    iota8 = place("iota8", [TP, E], F32)
    iotaslot = place("iotaslot", [TP, E], F32)
    iotacap = place("iotacap", [TP, CAP], F32)
    assert here() <= late_end, here()
    cursor[0] = k_at
    oh_d = [place(f"oh_d{i}", [TP, 640], BF16) for i in range(SLOTS)]
    oh_s = [place(f"oh_s{i}", [TP, 320], BF16) for i in range(SLOTS)]
    iota_h = place("iota_h", [TP, 640], F16)
    src_f = place("src_f", [TP, ECP], F32)
    dst_f = place("dst_f", [TP, ECP], F32)
    dig_f = place("dig_f", [TP, ECP], F32)
    src_n = place("src_n", [TP, ECP], F32)
    dig_n = place("dig_n", [TP, ECP], F32)
    assert here() <= tail_at
    cursor[0] = tail_at
    src_i = place("src_i", [TP, ECP], I32)
    dst_i = place("dst_i", [TP, ECP], I32)
    tmp_i = place("tmp_i", [TP, ECP], I32)
    sq_s = [place(f"sq_s{i}", [TP, 320], F32) for i in range(2)]
    assert here() <= tail_at + 2 * 2528
    v_int = place("v_int", [TP, NT, SC], I32, at=buf_at[1])
    v_lo = place("v_lo", [TP, NT, SC], I32, at=buf_at[1] + 6272)
    assert buf_at[1] + 2 * 6272 <= h_at
    S = place("S", [TP, NT, E, CAP], BF16, at=conv_at + 4 * 4096)
    assert NT * E * CAP * 2 <= 2 * 4096
    cursor[0] = h_at
    rt = {n: place("rt_" + n, [TP, NT, E], F32) for n in
          ("lg", "pr", "v8", "if8", "oh1", "oh2", "rank", "keep", "slot", "t1", "t2")}
    i8 = place("rt_i8", [TP, NT, E], U32)
    mask = place("rt_mask", [TP, NT, E], BF16)
    slot_tok = place("slot_tok", [CAP, E], F32)
    rr.update({n: place("rr_" + n, [TP, 8], F32) for n in ("mx", "sum", "den", "k1", "k2", "p1", "p2")})
    lgT = place("lgT", [2 * E, NP2], F32)
    assert here() <= h_at + 2 * 4 * D
    cursor[0] = conv_at
    got_at = [conv_at + i * 4 * 1024 for i in (0, 1, 2, 3, RING, RING + 1, RING + 2, RING + 3)] + [out_at, r_h_at]
    got = [[place(f"got{c}_{t}", [TP, D], F32, at=got_at[2 * t + c]) for t in range(NT)] for c in range(2)]

    def rw_half(i):
        return rwT[:, 0:KT * 2 * E].rearrange("p (k two n) -> p k two n", k=KT, two=2)[:, :, i, :]

    PS = [ctx.enter_context(nc.psum_tensor(f"ps{b}", [P, HALF], F32)) for b in range(8)]

    y_rows = nc.dram_tensor("y_rows", [N, D], F32).ap()
    eout_d = nc.dram_tensor("eout_d", [(E + 1) * CAP, D], F32).ap()

    x_t = x.rearrange("(t p) d -> t p d", p=TP)
    out_t = out.rearrange("(t p) d -> t p d", p=TP)
    y_rows_t = y_rows.rearrange("(t p) d -> t p d", p=TP)
    rg_v = rg.rearrange("e (k p) (q n) -> e q p k n", p=P, n=HALF)
    ru_v = ru.rearrange("e (k p) (q n) -> e q p k n", p=P, n=HALF)
    rd_v = rd.rearrange("e (q k p) n -> e q p k n", k=8, p=P)
    sg_v = sg.rearrange("(k p) (i n) -> i p k n", p=P, n=256)
    su_v = su.rearrange("(k p) (i n) -> i p k n", p=P, n=256)
    sd_v = sd.rearrange("(i k p) n -> i p k n", k=2, p=P)
    W_v = W.rearrange("(k p) (c n) -> c p k n", p=P, n=HALF)
    wq_v = w_qkv.rearrange("(c s p) k -> c p s k", s=4, p=P)
    wo_v = w_out.rearrange("(c s p) k -> c p s k", s=4, p=P)
    loads = [W_v[0], W_v[1], wq_v[2], wq_v[3], wq_v[4], wq_v[5], wq_v[0], wq_v[1], wo_v[0], wo_v[1]]

    def proj_n(g, t):
        return NT * (g if g < G_Q else g - (G_OUT - G_Q)) + t + 1

    OUT0 = 2 * NT + 4 * (G_OUT + 2 - G_K)
    YT0 = OUT0 + 2 * NT + 4 * 2

    def fill_w(g, i):
        return 2 * NT + 4 * (g - G_K) + i if g < G_OUT + 2 else OUT0 + 2 * NT + 4 * (g - G_OUT - 2) + i

    def fill_banks(n):
        return TB if n < 2 * NT or n >= YT0 else TB[:2]

    def fill_bank(n):
        return PS[fill_banks(n)[n % len(fill_banks(n))]]

    def tokens_part(hi, lo, n, j):
        t, half = divmod(j, 2)
        s = (slice(None), slice(4 * half, 4 * half + 4), slice(t * TP, (t + 1) * TP))
        return hi[s], lo[s], fill_bank(n)[:, 0:4 * TP].rearrange("p (k n) -> p k n", k=4)

    def weights_part(g, i):
        ks = slice(2 * i, 2 * i + 2)
        return (wT_hi[g % 2][:, ks, :], wT_lo[g % 2][:, ks, :],
                fill_bank(fill_w(g, i))[:, 0:2 * GW].rearrange("p (k n) -> p k n", k=2))

    def quarter(g):
        return wl[g // 2][:].rearrange("p (k n) -> p k n", k=KT)[:, :, (g % 2) * GW:(g % 2 + 1) * GW]

    block = ctx.enter_context(nc.Block())
    @block.sync
    def _(sp):
        sp.dma_start(src_i[:, 0:EC], src.rearrange("(p c) -> p c", p=TP)).then_inc(sem("src_in"), 16)
        sp.dma_start(dst_i[:, 0:EC], dst.rearrange("(p c) -> p c", p=TP)).then_inc(sem("dst_in"), 16)
        for t in range(NT):
            sp.dma_start(resid[:, t, :], x_t[t]).then_inc(sem("x_in"), 16)
        for n, v in enumerate(loads):
            if n in (2, 3):
                sp.wait_ge(sem("w_lo"), 2 * (n - 1))
            elif n >= 4:
                sp.wait_ge(sem("turned"), fill_w(2 * n - 3, 3) + 1)
            d = wl[n % 2][:].rearrange("p (k n) -> p k n", k=v.shape[1])
            sp.dma_start(d, v).then_inc(sem(f"wl_in{n % 2}"), 16)
        for t in range(NT):
            sp.wait_ge(sem("y_done"), t + 1)
            sp.dma_start(y_rows_t[t], y[:, t, :]).then_inc(sem("y_stored"), 16)
        sp.wait_ge(sem("fe_used"), FE_Q + 2 * PAIRS)
        def step(e, q, order=STEP):
            shared = [sg_v[e * Q + q], su_v[e * Q + q]]
            inner = [v[e, q * 2 + b][:, 4 * i:4 * i + 4, :] for b in range(2) for v in (rg_v, ru_v) for i in range(2)]
            down = [rd_v[e, q][:, 2 * r:2 * r + 2, :] for r in range(4)]
            blocks = (shared + inner + [sd_v[e * Q + q]] + down if order is STEP else
                      inner + down + shared + [sd_v[e * Q + q]])
            for b, v in enumerate(blocks):
                if b >= RAW:
                    sp.wait_ge(sem("lo_done"), count(e, q, U, U + order.last_unit[b - RAW] + 1))
                else:
                    sp.wait_ge(sem("lo_done"), count(e, q, U, STEP.last_unit[b - RAW + BLK] + 1))
                sp.dma_start(raw[b % RAW][:].rearrange("p (k n) -> p k n", k=v.shape[1]),
                             v).then_inc(sem(f"raw_in{b % RAW}"), 16)

        with sp.Fori(0, E - 1) as e:
            for q in range(Q):
                step(e, q)
        for q in range(Q):
            step(E - 1, q, LAST if q == Q - 1 else STEP)
        for t in range(NT):
            sp.wait_ge(sem("sd_added"), count(E - 1, Q - 1, 2 * NT, 2 * t + 2 + ONE))
            sp.dma_start(out_t[t], resid[:, t, :]).then_inc(sem("out_stored"), 16)
        sp.wait_ge(sem("out_stored"), 16 * NT)

    @block.gpsimd
    def _(pool):
        chain = [0]

        def link(ins):
            chain[0] += 1
            ins.then_inc(sem("pool_chain"), 1)
            pool.wait_ge(sem("pool_chain"), chain[0])

        link(nc.gpsimd.iota(iota_h[:], [[1, 640]], base=0, channel_multiplier=0,
                            allow_small_or_imprecise_dtypes=True))
        link(nc.gpsimd.memset(src_i[:, EC:ECP], -2))
        nc.gpsimd.memset(dst_i[:, EC:ECP], -2).then_inc(sem("iota_done"), 1)
        pool.dma_start(a_bc[:], a[0, :].partition_broadcast(TP)).then_inc(sem("a_in"), 16)
        pool.dma_start(rw_in[:], router_w).then_inc(sem("rw_in"), 16)
        link(nc.gpsimd.memset(C[:], 0.0))
        pool.sem_inc(sem("counted"), 2)
        link(nc.gpsimd.memset(ones[:], 1.0))
        link(nc.gpsimd.affine_select(out=ident[:], in_=ones[:], pattern=[[-1, P]], compare_op=ALU.is_equal,
                                     fill=0.0, base=0, channel_multiplier=1))
        link(nc.gpsimd.memset(ones_b[:], 1.0))
        link(nc.gpsimd.affine_select(out=tri[:], in_=ones_b[:], pattern=[[1, P]], compare_op=ALU.is_gt,
                                     fill=0.0, base=0, channel_multiplier=-1))
        link(nc.gpsimd.memset(KV[:], 0.0))
        link(nc.gpsimd.iota(iota8[:], [[1, E]], base=0, channel_multiplier=0, allow_small_or_imprecise_dtypes=True))
        link(nc.gpsimd.iota(iotaslot[:], [[CAP, E]], base=CAP, channel_multiplier=0,
                            allow_small_or_imprecise_dtypes=True))
        link(nc.gpsimd.iota(iotacap[:], [[1, CAP]], base=0, channel_multiplier=0,
                            allow_small_or_imprecise_dtypes=True))
        link(nc.gpsimd.iota(tok_b[:, :, 0], [[0, NT]], base=0, channel_multiplier=1,
                            allow_small_or_imprecise_dtypes=True))
        link(nc.gpsimd.iota(tok_b[:, :, 1], [[1, NT]], base=0, channel_multiplier=0,
                            allow_small_or_imprecise_dtypes=True))
        nc.gpsimd.memset(rwT[:].bitcast(F32), 0.0).then_inc(sem("const_done"), 1)
        Ci = C[:].bitcast(I32)
        with pool.Fori(0, NG) as gr:
            pool.wait_ge(sem("digits"), gr * 2 + 2)
            nc.gpsimd.tensor_tensor(Ci[:, :, :, 0], Ci[:, :, :, 0], v_lo[:], ALU.add).then_inc(sem("counted"), 1)
            nc.gpsimd.tensor_tensor(Ci[:, :, :, 1], Ci[:, :, :, 1], v_int[:], ALU.add).then_inc(sem("counted"), 1)
        pool.wait_ge(sem("rwT_ps"), 1)
        pool.dma_start(b_bc[:], b_out.partition_broadcast(TP)).then_inc(sem("b_in"), 16)
        pool.wait_ge(sem("b_in"), 16)
        pool.wait_ge(sem("xn_done"), NT)
        for t in range(NT):
            nc.gpsimd.tensor_tensor(resid[:, t, :], resid[:, t, :], b_bc[:], ALU.add).then_inc(sem("biased"), 1)
        pool.wait_ge(sem("agg_ps"), 2 * NT)
        nc.gpsimd.memset(vv[:, :, :, P:VW], 1.0).then_inc(sem("v_ones"), 1)
        pool.wait_ge(sem("y_stored"), 16 * NT)
        link(nc.gpsimd.memset(eout[:], 0.0))
        pool.sem_inc(sem("eout_clear"), 1)
        pool.wait_ge(sem("tok_done"), 1)

        def gather():
            nc.gpsimd.indirect_dma_start(
                out=xg[:], out_offset=None, in_=y_rows,
                in_offset=bass.IndirectOffsetOnAxis(ap=tok_cur[:, 0:1], axis=0)).then_inc(sem("xg_in"), 16)

        link(nc.gpsimd.tensor_copy(tok_cur[:], tok_u[:, 0:1]))
        gather()

        def turn_over(e):
            pool.wait_ge(sem("rd_added"), e * (2 * Q) + 2)
            pool.wait_ge(sem("xgT_ps"), e * 2 + 2)
            pool.sem_inc(sem("turns"), 1)
            nc.gpsimd.tensor_copy(eout_st[:], eout[:]).then_inc(sem("eout_copied"), 1)
            pool.wait_ge(sem("eout_copied"), e + 1)
            pool.sem_inc(sem("turns"), 1)
            nc.gpsimd.memset(eout[:], 0.0).then_inc(sem("eout_clear"), 1)
            pool.dma_start(eout_d[bass.ds(e * CAP, CAP), :], eout_st[:]).then_inc(sem("eout_stored"), 16)
            pool.wait_ge(sem("eout_stored"), e * 16 + 16)

        with pool.Fori(0, E - 1) as e:
            turn_over(e)
            pool.sem_inc(sem("turns"), 1)
            nc.gpsimd.tensor_copy(tok_cur[:], tok_u[:, bass.ds(e + 1, 1)]).then_inc(sem("tok_copied"), 1)
            pool.wait_ge(sem("tok_copied"), e + 1)
            pool.sem_inc(sem("turns"), 1)
            gather()
        turn_over(E - 1)
        pool.wait_ge(sem("rd_added"), 2 * Q * E + 2)
        pool.dma_start(eout_d[E * CAP:(E + 1) * CAP, :], eout[:]).then_inc(sem("eout_stored"), 16)
        pool.wait_ge(sem("eout_stored"), 16 * (E + 1))
        for t in range(NT):
            for c in range(2):
                nc.gpsimd.indirect_dma_start(
                    out=got[c][t][:], out_offset=None, in_=eout_d,
                    in_offset=bass.IndirectOffsetOnAxis(ap=pos_u[:, c, t:t + 1], axis=0)).then_inc(
                        sem(f"g_in{c}_{t}"), 16)

    @block.scalar
    def _(act):
        def count_group(gr, extra):
            for i, c in enumerate(ACT_CHUNKS):
                col = gr * EG + c
                if c >= SLOTS:
                    act.wait_ge(sem("onehot_used"), gr * (EG - 1) + (c - SLOTS + 1))
                if i >= 2:
                    act.wait_ge(sem("onehot_act"), gr * len(ACT_CHUNKS) + i - 1)
                elif i == 0 and not (isinstance(gr, int) and gr == 0):
                    act.wait_ge(sem("onehot_act"), gr * len(ACT_CHUNKS))
                nc.scalar.activation(sq_s[i % 2][:, 0:314], iota_h[:, 0:314], ACT.Square,
                                     bias=src_n[:, bass.ds(col, 1)]).then_inc(sem("sq_s"), 1)
                act.wait_ge(sem("sq_s"), gr * len(ACT_CHUNKS) + i + 1)
                nc.scalar.activation(oh_s[c % SLOTS][:, 0:314], sq_s[i % 2][:, 0:314], ACT.Relu, scale=dig_n[:, bass.ds(col, 1)],
                                     bias=dig_f[:, bass.ds(col, 1)]).then_inc(sem("onehot_act"), 1)
                if i == len(ACT_CHUNKS) // 2:
                    extra()
            for dt in range(NT):
                act.wait_ge(sem("count_done"), gr * NT + dt + 1)
                if dt == 0:
                    act.wait_ge(sem("counted"), gr * 2 + 2)
                nc.scalar.copy(v_int[:, dt, :], PS[dt][0:TP, 0:SC]).then_inc(sem("count_out"), 1)

        def w_hi(g):
            if g % 2 == 0:
                act.wait_ge(sem(f"wl_in{g // 2}"), 16)
            if g == 1:
                act.wait_ge(sem("counted"), 2 * NG + 2)
            if g >= 2:
                act.wait_ge(sem("proj"), proj_n(g - 2, NT - 1))
            nc.scalar.copy(wT_hi[g % 2][:], quarter(g)).then_inc(sem("w_hi"), 1)

        def std(tile):
            def f():
                act.wait_ge(sem("var_done"), tile)
                nc.scalar.activation(rstd[:, 0:1], mv[:, 0, 1:2], ACT.Sqrt).then_inc(sem("std_done"), 1)
            return f

        def split_hi(n, part):
            act.wait_ge(sem("turned"), n + 1)
            nc.scalar.copy(part[0], part[2]).then_inc(sem("turned_hi"), 1)

        def w_part(g, i):
            split_hi(fill_w(g, i), weights_part(g, i))

        def feature_exp(n, parts, cols):
            act.wait_ge(sem("fm_done"), n + 1)
            if n >= 2:
                act.wait_ge(sem("fe_used"), n - 1)
            nc.scalar.activation(fe[n % 2][0:parts, 0:cols], fm[n % 2][0:parts, 0:cols],
                                 ACT.Exp).then_inc(sem("fe_done"), 1)

        act.wait_ge(sem("indices"), 1)
        count_group(0, lambda: w_hi(0))
        with act.Fori(1, NG) as gr:
            count_group(gr, std(gr))
        for j in range(2 * NT):
            split_hi(j, tokens_part(xnT_hi, xnT_lo, j, j))
        act.wait_ge(sem("rwT_ps"), 1)
        act.wait_ge(sem("const_done"), 1)
        nc.scalar.copy(rw_half(0), PS[7][:, 0:KT * E].rearrange("p (k n) -> p k n", k=KT)).then_inc(sem("rwT_hi"), 1)
        w_hi(1)
        w_hi(2)
        for half in range(2):
            for t in range(NT):
                act.wait_ge(sem("proj"), proj_n(2 * half + 1, t))
                nc.scalar.copy(h[:, t, half * HALF:(half + 1) * HALF], PS[t][0:TP, :]).then_inc(sem("h_out"), 1)
                if half == 1 and t < 4:
                    w_part(G_K, t)
            if half == 0:
                w_hi(3)
        for i in range(4):
            w_part(G_K + 1, i)
        for t in range(NT):
            feature_exp(t, TP, HALF)
            if t < 4:
                w_part(G_K + 2, t)
        for dt in range(NT):
            if dt < 4:
                w_part(G_K + 3, dt)
            act.wait_ge(sem("z_done"), dt + 1)
            nc.scalar.activation(zt[dt % 2][:], zt[dt % 2][:], ACT.Exp, scale=-1.0).then_inc(sem("ez_done"), 1)
        for t in range(NT):
            feature_exp(NT + t, TP, HALF)
            if t < 4:
                w_part(G_V, t)
        for j in range(2 * NT):
            feature_exp(2 * NT + j, TP, HALF)
        for half in range(2):
            for i in range(4):
                w_part(G_V + 2 * half + 1, i)
            for t in range(NT):
                act.wait_ge(sem("proj"), proj_n(G_V + 2 * half + 1, t))
                nc.scalar.copy(vv[:, t, half * 4:half * 4 + 4, 0:P],
                               PS[V_BANK[t]][0:TP, :].rearrange("p (j m) -> p j m", j=4)).then_inc(sem("v_out"), 1)
                if t < 4:
                    w_part(G_V + 2 * half + 2, t)
        for n in range(2 * PAIRS):
            g, i = divmod(n, 4)
            if n == 0:
                for part in Q_PARTS[0] + Q_PARTS[1]:
                    w_part(G_Q + 1, part)
            feature_exp(FE_Q + n, P, HALVES[n % 2][1])
            if n >= 2:
                for part in Q_PARTS[i]:
                    w_part(G_Q + g + 1, part)
        for i in range(4):
            w_part(G_OUT + 1, i)
        for j in range(2 * NT):
            split_hi(OUT0 + j, tokens_part(outT_hi, outT_lo, OUT0 + j, j))
        for g in (G_OUT + 2, G_OUT + 3):
            for i in range(4):
                w_part(g, i)
        for t in range(NT):
            act.wait_ge(sem("var_done"), NT + t + 1)
            nc.scalar.activation(rstd[:, t:t + 1], mv[:, t, 1:2], ACT.Sqrt).then_inc(sem("std_done"), 1)
        for t in range(NT):
            act.wait_ge(sem("y_done"), t + 1)
            for j in (2 * t, 2 * t + 1):
                split_hi(YT0 + j, tokens_part(yT_hi, yT_lo, YT0 + j, j))

        def squares(t0, t1):
            for t in range(t0, t1):
                if t:
                    act.wait_ge(sem("ms_done"), t)
                nc.scalar.activation(sq[:], y[:, t, :], ACT.Square,
                                     accum_out=rr["ms"][:, t:t + 1]).then_inc(sem("ms_done"), 1)

        def rms_root():
            act.wait_ge(sem("rms_done"), 1)
            nc.scalar.activation(rr["r"][:, 0:NT], rr["ms"][:, 0:NT], ACT.Sqrt).then_inc(sem("rms_sqrt"), 1)

        def logits_out(hf):
            act.wait_ge(sem("lgT_ps"), hf + 1)
            o, w = HALVES[hf]
            nc.scalar.copy(lgT[:, o:o + w], PS[hf][0:2 * E, 0:w]).then_inc(sem("lgT_out"), 1)

        def softmax_exp():
            act.wait_ge(sem("lg_done"), 1)
            nc.scalar.activation(rt["pr"][:], rt["lg"][:], ACT.Exp).then_inc(sem("pr_done"), 1)

        def step(e, q, order=STEP, routing=False):
            def hi(u):
                r, part = order.source(u)
                act.wait_ge(sem(f"raw_in{r % RAW}"), count(e, q, 16 * BLK // RAW, 16 * (r // RAW + 1)))
                act.wait_ge(sem("unit_used"), count(e, q, U, u + 1 - RING + USED0))
                nc.scalar.copy(order.view(c_hi[u % RING], u), part(raw[r % RAW])).then_inc(sem("hi_done"), 1)

            def silu_routed(b):
                act.wait_ge(sem("unit_used"), count(e, q, U, order.a_end[b] + USED0))
                act.wait_ge(sem("h_done"), count(e, q, 2, b + ONE))
                nc.scalar.activation(r_silu[:], PS[order.a_bank[b]][0:CAP, :], ACT.Silu).then_inc(sem("silu_done"), 1)

            def silu_shared(n):
                if n % 2 == 0:
                    act.wait_ge(sem("s_half"), count(e, q, 2, n // 2 + 1))
                else:
                    act.wait_ge(sem("unit_used"), count(e, q, U, order.s_end[n // 2] + USED0))
                act.wait_ge(sem("sh_mult"), count(e, q, 4, max(n - 1, 0) + ONE))
                w = HALVES[n % 2][1]
                nc.scalar.activation(s_silu[n % 2][:, 0:w], PS[order.s_bank[n]][:, 0:w],
                                     ACT.Silu).then_inc(sem("silu_done"), 1)

            def turned_hi(b):
                act.wait_ge(sem("t_done"), count(e, q, 2, b + 1))
                nc.scalar.copy(hT_hi[:, b * 4 * CAP:(b + 1) * 4 * CAP],
                               PS[T_BANK[b]][:, 0:4 * CAP]).then_inc(sem("thi_done"), 1)

            def tokens_hi(half):
                act.wait_ge(sem("xgT_ps"), e * 2 + (half + 1))
                nc.scalar.copy(xgT_hi[:, half * 4 * CAP:(half + 1) * 4 * CAP],
                               PS[A0 + half][:, 0:4 * CAP]).then_inc(sem("xg_hi"), 1)

            if order is LAST:
                for u in range(18):
                    hi(u)
                silu_routed(0)
                for u in range(18, 21):
                    hi(u)
                turned_hi(0)
                for u in range(21, 24):
                    hi(u)
                silu_routed(1)
                turned_hi(1)
                for u in range(24, 30):
                    hi(u)
                for n in range(4):
                    silu_shared(n)
                return
            if routing:
                hi(0)
                hi(1)
                squares(0, 2)
                logits_out(0)
                logits_out(1)
                squares(2, NT)
                rms_root()
                hi(2)
                softmax_exp()
                hi(3)
            else:
                for u in range(10):
                    hi(u)
            silu_shared(0)
            silu_shared(1)
            if routing:
                act.wait_ge(sem("tok_ps"), 1)
                for u in range(4, 10):
                    hi(u)
                silu_shared(2)
            if q == 0:
                tokens_hi(0)
                tokens_hi(1)
            hi(10)
            hi(11)
            if not routing:
                silu_shared(2)
            silu_shared(3)
            for u in range(12, 22):
                hi(u)
            silu_routed(0)
            for u in range(22, 28):
                hi(u)
            turned_hi(0)
            silu_routed(1)
            hi(28)
            hi(29)
            turned_hi(1)

        for q in range(Q):
            step(0, q, routing=(q == 0))
        with act.Fori(1, E - 1) as e:
            for q in range(Q):
                step(e, q)
        for q in range(Q):
            step(E - 1, q, LAST if q == Q - 1 else STEP)

    @block.vector
    def _(dve):
        chain = [0]

        def link(ins):
            chain[0] += 1
            ins.then_inc(sem("dve_chain"), 1)
            dve.wait_ge(sem("dve_chain"), chain[0])

        V = nc.vector
        dve.wait_ge(sem("src_in"), 16)
        dve.wait_ge(sem("dst_in"), 16)
        dve.wait_ge(sem("iota_done"), 1)
        V.tensor_copy(dst_f[:], dst_i[:]).then_inc(sem("idx"), 1)
        link(V.tensor_scalar(tmp_i[:], src_i[:], 1, None, ALU.arith_shift_right))
        link(V.tensor_copy(src_f[:], tmp_i[:]))
        link(V.tensor_scalar(tmp_i[:], src_i[:], 1, None, ALU.bitwise_and))
        link(V.tensor_copy(dig_f[:], tmp_i[:]))
        link(V.tensor_scalar(dig_f[:], dig_f[:], DIGIT - 1.0, 1.0, ALU.mult, ALU.add))
        V.tensor_scalar(src_n[:], src_f[:], -1.0, None, ALU.mult).then_inc(sem("idx"), 1)
        V.tensor_scalar(dig_n[:], dig_f[:], -1.0, None, ALU.mult).then_inc(sem("indices"), 1)
        dve.wait_ge(sem("idx"), 2)

        xf = resid[:].rearrange("p t d -> p (t d)")
        xnf = xn[:].rearrange("p t d -> p (t d)")

        def digits(gr):
            dve.wait_ge(sem("count_out"), gr * NT + NT)
            dve.wait_ge(sem("counted"), gr * 2 + 2)
            V.tensor_scalar(v_lo[:], v_int[:], int(DIGIT) - 1, None, ALU.bitwise_and).then_inc(sem("digits"), 1)
            dve.wait_ge(sem("digits"), gr * 2 + 1)
            V.tensor_scalar(v_int[:], v_int[:], 12, None, ALU.arith_shift_right).then_inc(sem("digits"), 1)

        def w_lo(g):
            dve.wait_ge(sem("w_hi"), g + 1)
            V.tensor_tensor(wT_lo[g % 2][:], quarter(g), wT_hi[g % 2][:].bitcast(F32),
                            ALU.subtract).then_inc(sem("w_lo"), 1)

        def count_group(gr, first, between):
            for c in range(EG):
                col = gr * EG + c
                if c >= SLOTS:
                    dve.wait_ge(sem("onehot_used"), gr * (EG - 1) + (c - SLOTS + 1))
                elif not first and c < SLOTS - 1:
                    dve.wait_ge(sem("onehot_used"), gr * (EG - 1) + (c - SLOTS + 2))
                elif not first:
                    dve.wait_ge(sem("count_done"), gr * NT)
                V.tensor_scalar(oh_d[c % SLOTS][:, 0:626], iota_h[:, 0:626], dst_f[:, bass.ds(col, 1)], None,
                                ALU.is_equal).then_inc(sem("onehot"), 1)
                if c not in ACT_CHUNKS:
                    V.tensor_scalar(oh_s[c % SLOTS][:, 0:314], iota_h[:, 0:314], src_f[:, bass.ds(col, 1)],
                                    dig_f[:, bass.ds(col, 1)], ALU.is_equal, ALU.mult).then_inc(sem("onehot"), 1)
                if c in between:
                    between[c]()

        def first_layernorm(gr):
            def stats():
                for half in range(2):
                    V.bn_stats(st6[:, 0, half, :],
                               xf[:, bass.ds((gr - 1) * D + half * HALF, HALF)]).then_inc(sem("ln"), 1)
                dve.wait_ge(sem("ln"), gr * 4 - 2)
                dve.sem_inc(sem("dve_turns"), 1)
                V.bn_aggr(mv[:, 0, :], st6[:, 0, :, :]).then_inc(sem("ln"), 1)
                dve.wait_ge(sem("ln"), gr * 4 - 1)
                V.tensor_scalar(mv[:, 0, 1:2], mv[:, 0, 1:2], EPS, None, ALU.add).then_inc(sem("var_done"), 1)

            def apply():
                dve.wait_ge(sem("std_done"), gr)
                V.reciprocal(rstd[:, 0:1], rstd[:, 0:1]).then_inc(sem("ln"), 1)
                dve.wait_ge(sem("ln"), gr * 4)
                V.tensor_scalar(xnf[:, bass.ds((gr - 1) * D, D)], xf[:, bass.ds((gr - 1) * D, D)], mv[:, 0, 0:1],
                                rstd[:, 0:1], ALU.subtract, ALU.mult).then_inc(sem("xn_done"), 1)
            return stats, apply

        count_group(0, True, {20: lambda: w_lo(0)})
        dve.wait_ge(sem("x_in"), 16 * NT)
        with dve.Fori(1, NG) as gr:
            stats, apply = first_layernorm(gr)
            count_group(gr, False, {9: lambda: digits(gr - 1), 13: stats, 20: apply})
        V.memset(xnT_hi[:, :, N:NP2].bitcast(F32), 0.0).then_inc(sem("pad"), 1)
        V.memset(xnT_lo[:, :, N:NP2].bitcast(F32), 0.0).then_inc(sem("pad"), 1)

        def split_lo(n, part):
            dve.wait_ge(sem("turned_hi"), n + 1)
            V.tensor_tensor(part[1], part[2], part[0].bitcast(F32), ALU.subtract).then_inc(sem("turned_lo"), 1)

        def w_part(g, i):
            split_lo(fill_w(g, i), weights_part(g, i))

        for j in range(2 * NT):
            split_lo(j, tokens_part(xnT_hi, xnT_lo, j, j))
        digits(NG - 1)
        dve.wait_ge(sem("rwT_hi"), 1)
        V.tensor_tensor(rw_half(1), PS[7][:, 0:KT * E].rearrange("p (k n) -> p k n", k=KT),
                        rw_half(0).bitcast(F32), ALU.subtract).then_inc(sem("rwT_lo"), 1)
        for g in range(1, G_K):
            w_lo(g)
        for i in range(4):
            w_part(G_K, i)
        dve.wait_ge(sem("a_in"), 16)
        for t in range(NT):
            dve.wait_ge(sem("h_out"), NT + t + 1)
            for c in range(2):
                link(V.tensor_tensor_reduce(out=scr[:], in0=h[:, t, :], in1=a_bc[:, c * D:(c + 1) * D], scale=1.0,
                                            scalar=0.0, op0=ALU.mult, op1=ALU.add, accum_out=al[:, t, c:c + 1]))
            V.tensor_scalar(diag[:, t, :], ident[0:TP, 0:TP], al[:, t, 0:1], None,
                            ALU.mult).then_inc(sem("diag_done"), 1)
            if t < 4:
                w_part(G_K + 1, t)

        def feature_min(n, ps, parts, cols, scale=None):
            if n >= 2:
                dve.wait_ge(sem("fe_done"), n - 1)
            if scale is None:
                V.tensor_scalar(fm[n % 2][0:parts, 0:cols], ps, 0.0, None, ALU.min).then_inc(sem("fm_done"), 1)
            else:
                V.tensor_scalar(fm[n % 2][0:parts, 0:cols], ps, scale, 0.0, ALU.mult,
                                ALU.min).then_inc(sem("fm_done"), 1)

        def feature_map(n, ps, parts, cols, dest):
            dve.wait_ge(sem("fe_done"), n + 1)
            V.scalar_tensor_tensor(out=dest, in0=ps, scalar=0.0, in1=fe[n % 2][0:parts, 0:cols], op0=ALU.max,
                                   op1=ALU.add).then_inc(sem("fe_used"), 1)

        def k_map(half, t, g, between=None):
            dve.wait_ge(sem("proj"), proj_n(G_K + 2 * half + 1, t))
            ps = PS[t][0:TP, :]
            feature_min(half * NT + t, ps, TP, HALF)
            if between:
                between()
            feature_map(half * NT + t, ps, TP, HALF, kk[:, t, half * HALF:(half + 1) * HALF])
            if t < 4:
                w_part(g, t)

        def albc_copy(part):
            dve.wait_ge(sem("albc_ps"), part + 1)
            cols = slice(0, 4 * TP) if part == 0 else slice(4 * TP, N)
            V.tensor_copy(albc[:, cols], PS[7][0:TP, 0:cols.stop - cols.start]).then_inc(sem("albc_out"), 1)

        dve.wait_ge(sem("diag_done"), NT)
        for t in range(NT):
            k_map(0, t, G_K + 2, {0: lambda: albc_copy(0), 1: lambda: albc_copy(1)}.get(t))
        dve.wait_ge(sem("albc_out"), 2)
        dve.wait_ge(sem("counted"), 2 * NG + 2)
        Cf = C[:].rearrange("p t c two -> p t (c two)")
        Ci = C[:].bitcast(I32).rearrange("p t c two -> p t (c two)")

        def edge_weights(dt):
            dve.wait_ge(sem("ez_done"), dt + 1)
            V.scalar_tensor_tensor(out=Cf[:, dt, 0:N], in0=zt[dt % 2][:], scalar=FMAX, in1=Ci[:, dt, 0:N],
                                   op0=ALU.min, op1=ALU.mult).then_inc(sem("ez_used"), 1)

        for dt in range(NT):
            if dt >= 2:
                edge_weights(dt - 2)
                dve.wait_ge(sem("ez_used"), dt - 1)
            link(V.tensor_scalar(zt[dt % 2][:], albc[:], al[:, dt, 1:2], None, ALU.add))
            V.scalar_tensor_tensor(out=zt[dt % 2][:], in0=zt[dt % 2][:], scalar=SLOPE, in1=zt[dt % 2][:],
                                   op0=ALU.mult, op1=ALU.max).then_inc(sem("z_done"), 1)
            if dt < 4:
                w_part(G_K + 3, dt)
        edge_weights(NT - 2)
        edge_weights(NT - 1)
        for t in range(NT):
            k_map(1, t, G_V)
        dve.wait_ge(sem("ez_used"), NT)
        dve.wait_ge(sem("rowsum_ps"), 1)
        link(V.tensor_scalar(rinv[:], PS[3][0:TP, 0:NT], EPS, None, ALU.add))
        link(V.reciprocal(rinv[:], rinv[:]))
        dve.wait_ge(sem("biased"), NT)
        for j in range(2 * NT):
            t, half = divmod(j, 2)
            nf = 2 * NT + j
            dve.wait_ge(sem("agg_ps"), j + 1)
            ps = PS[AGG_BANK[j % 4]][0:TP, :]
            feature_min(nf, ps, TP, HALF, scale=rinv[:, t:t + 1])
            r = resid[:, t, half * HALF:(half + 1) * HALF]
            V.tensor_scalar(gscr[j % 2][:], ps, rinv[:, t:t + 1], 0.0, ALU.mult, ALU.max).then_inc(sem("agg_used"), 1)
            dve.wait_ge(sem("agg_used"), j + 1)
            V.tensor_tensor(r, r, gscr[j % 2][:], ALU.add).then_inc(sem("agg_out"), 1)
            dve.wait_ge(sem("agg_out"), j + 1)
            dve.wait_ge(sem("fe_done"), nf + 1)
            V.scalar_tensor_tensor(out=r, in0=fe[nf % 2][0:TP, :], scalar=-1.0, in1=r, op0=ALU.add,
                                   op1=ALU.add).then_inc(sem("fe_used"), 1)
        for g in range(G_V + 1, G_Q + 1):
            for i in range(4):
                w_part(g, i)
        for part in Q_PARTS[0] + Q_PARTS[1]:
            w_part(G_Q + 1, part)
        for b, (j0, cnt) in enumerate(TRIPLES):
            dve.wait_ge(sem("KV_ps"), b + 1)
            ps = PS[KV_BANK[b]][:, 0:cnt * VW].rearrange("p (j c) -> p j c", j=cnt)
            for i in range(2):
                o = slice(i * HD, (i + 1) * HD)
                V.tensor_copy(KV[o, j0:j0 + cnt, o], ps[o, :, o]).then_inc(sem("KV_out"), 1)
                V.tensor_copy(KV[o, j0:j0 + cnt, P + i:P + i + 1], ps[o, :, P:P + 1]).then_inc(sem("KV_out"), 1)
        for n in range(2 * PAIRS):
            j, hf = divmod(n, 2)
            o, w = HALVES[hf]
            dve.wait_ge(sem("q_ps"), n + 1)
            ps = PS[Q_BANK[n % 6]][:, 0:w]
            feature_min(FE_Q + n, ps, P, w)
            feature_map(FE_Q + n, ps, P, w, qT[:, j, o:o + w])
            if n >= 2:
                for part in Q_PARTS[n % 4]:
                    w_part(G_Q + n // 4 + 1, part)
        dve.sem_inc(sem("lo_done"), U)
        for i in range(4):
            w_part(G_OUT + 1, i)
        for t in range(NT + 1):
            if t < NT:
                dve.wait_ge(sem("att_ps"), t + 1)
                banks = [PS[b][0:TP, 0:cnt * VW].rearrange("p (j c) -> p j c", j=cnt)
                         for b, (j0, cnt) in zip(ATT_BANK[t % 2], TRIPLES)]
                for ps, (j0, cnt) in zip(banks, TRIPLES):
                    V.tensor_scalar(dn[:, j0:j0 + cnt, :], ps[:, :, P:VW], 1e-6, None, ALU.add).then_inc(sem("dn"), 1)
                dve.wait_ge(sem("dn"), 3 * (t + 1))
                link(V.reciprocal(dr[:], dn[:]))
                if t >= 2:
                    dve.wait_ge(sem("turned"), OUT0 + 2 * (t - 1))
                for ps, (j0, cnt) in zip(banks, TRIPLES):
                    ins = V.tensor_tensor(
                        att[t % 2][:, j0 * P:(j0 + cnt) * P].rearrange("p (j two m) -> p j two m", j=cnt, two=2),
                        ps[:, :, 0:P].rearrange("p j (two m) -> p j two m", two=2),
                        dr[:, j0:j0 + cnt, :].unsqueeze(3).to_broadcast([TP, cnt, 2, HD]), ALU.mult)
                ins.then_inc(sem("att_done"), 1)
            if t >= 1:
                for j in (2 * t - 2, 2 * t - 1):
                    split_lo(OUT0 + j, tokens_part(outT_hi, outT_lo, OUT0 + j, j))
        def residual_add(half, t):
            dve.wait_ge(sem("proj"), proj_n(G_OUT + 2 * half + 1, t))
            r = resid[:, t, half * HALF:(half + 1) * HALF]
            V.tensor_tensor(r, PS[t][0:TP, :], r, ALU.add).then_inc(sem("o_out"), 1)
            dve.wait_ge(sem("o_out"), half * NT + t + 1)
            link(V.bn_stats(st6[:, t, half, :], r))

        def normalize(t):
            dve.wait_ge(sem("std_done"), NT + t + 1)
            link(V.reciprocal(rstd[:, t:t + 1], rstd[:, t:t + 1]))
            V.tensor_scalar(y[:, t, :], resid[:, t, :], mv[:, t, 0:1], rstd[:, t:t + 1], ALU.subtract,
                            ALU.mult).then_inc(sem("y_done"), 1)

        for t in range(NT):
            if t < 4:
                w_part(G_OUT + 2, t)
            residual_add(0, t)
        for i in range(4):
            w_part(G_OUT + 3, i)
        V.memset(yT_hi[:, :, N:NP2].bitcast(F32), 0.0).then_inc(sem("pad"), 1)
        V.memset(yT_lo[:, :, N:NP2].bitcast(F32), 0.0).then_inc(sem("pad"), 1)
        for t in range(NT):
            residual_add(1, t)
            link(V.bn_aggr(mv[:, t, :], st6[:, t, :, :]))
            V.tensor_scalar(mv[:, t, 1:2], mv[:, t, 1:2], EPS, None, ALU.add).then_inc(sem("var_done"), 1)
            if t:
                normalize(t - 1)
        normalize(NT - 1)
        for j in range(2 * NT):
            split_lo(YT0 + j, tokens_part(yT_hi, yT_lo, YT0 + j, j))
        T = rt
        bc = [TP, NT, E]

        def wide(v):
            return v[:, 0:NT].unsqueeze(2).to_broadcast(bc)

        def rsqrt_squares():
            dve.wait_ge(sem("ms_done"), NT)
            V.tensor_scalar(rr["ms"][:, 0:NT], rr["ms"][:, 0:NT], 1.0 / D, RMS_EPS, ALU.mult,
                            ALU.add).then_inc(sem("rms_done"), 1)
            dve.wait_ge(sem("rms_sqrt"), 1)
            link(V.reciprocal(rr["r"][:, 0:NT], rr["r"][:, 0:NT]))

        def choose():
            dve.wait_ge(sem("lg_ps"), 1)
            lgs = PS[4][0:TP, 0:NT * 2 * E].rearrange("p (t two e) -> p t two e", t=NT, two=2)
            link(V.tensor_copy(T["lg"][:], lgs[:, :, 0, :]))
            link(V.tensor_tensor(T["lg"][:], T["lg"][:], lgs[:, :, 1, :], ALU.add))
            link(V.tensor_tensor(T["lg"][:], T["lg"][:], wide(rr["r"]), ALU.mult))
            link(V.tensor_reduce(rr["mx"][:, 0:NT], T["lg"][:], AXX, ALU.max))
            V.tensor_tensor(T["lg"][:], T["lg"][:], wide(rr["mx"]), ALU.subtract).then_inc(sem("lg_done"), 1)
            dve.wait_ge(sem("pr_done"), 1)
            link(V.tensor_reduce(rr["sum"][:, 0:NT], T["pr"][:], AXX, ALU.add))
            link(V.reciprocal(rr["sum"][:, 0:NT], rr["sum"][:, 0:NT]))
            link(V.tensor_tensor(T["pr"][:], T["pr"][:], wide(rr["sum"]), ALU.mult))
            dve.wait_ge(sem("const_done"), 1)
            for t in range(NT):
                V.max(T["v8"][:, t, :], T["pr"][:, t, :]).then_inc(sem("top"), 1)
            dve.wait_ge(sem("top"), NT)
            for t in range(NT):
                V.max_index(i8[:, t, :], T["v8"][:, t, :], T["pr"][:, t, :]).then_inc(sem("top"), 1)
            dve.wait_ge(sem("top"), 2 * NT)
            link(V.tensor_copy(T["if8"][:], i8[:]))
            for c, oh in enumerate(("oh1", "oh2")):
                link(V.tensor_tensor(T[oh][:], iota8[:].unsqueeze(1).to_broadcast(bc),
                                     T["if8"][:, :, c:c + 1].to_broadcast(bc), ALU.is_equal))
            V.tensor_tensor(mask[:], T["oh1"][:], T["oh2"][:], ALU.add).then_inc(sem("mask_done"), 1)
            link(V.tensor_tensor(rr["den"][:, 0:NT], T["v8"][:, :, 0], T["v8"][:, :, 1], ALU.add))
            link(V.reciprocal(rr["den"][:, 0:NT], rr["den"][:, 0:NT]))

        def slots():
            dve.wait_ge(sem("rank_ps"), 1)
            dve.wait_ge(sem("mask_done"), 1)
            link(V.tensor_copy(T["rank"][:], PS[RANK_BANK][0:TP, 0:NT * E].rearrange("p (t e) -> p t e", t=NT)))
            link(V.tensor_scalar(T["t1"][:], T["rank"][:], 1.0, None, ALU.add))
            link(V.tensor_tensor(T["t1"][:], T["t1"][:], mask[:], ALU.mult))
            link(V.tensor_scalar(T["t1"][:], T["t1"][:], 1.0, None, ALU.subtract))
            te = T["t1"][:].rearrange("p t e -> p (t e)")
            V.tensor_tensor(S[:].rearrange("p t e c -> p (t e) c"), iotacap[:].unsqueeze(1).to_broadcast([TP, NT * E, CAP]),
                            te.unsqueeze(2).to_broadcast([TP, NT * E, CAP]), ALU.is_equal).then_inc(sem("S_done"), 1)

        def slot_tokens():
            dve.wait_ge(sem("tok_ps"), 1)
            link(V.tensor_copy(slot_tok[:], PS[TOK_BANK][0:CAP, 0:2 * E].rearrange("p (e two) -> p e two", two=2)[:, :, 0]))
            link(V.scalar_tensor_tensor(out=slot_tok[:], in0=PS[TOK_BANK][0:CAP, 0:2 * E].rearrange("p (e two) -> p e two", two=2)[:, :, 1],
                                        scalar=float(TP), in1=slot_tok[:], op0=ALU.mult, op1=ALU.add))
            V.tensor_copy(tok_u[:], slot_tok[:]).then_inc(sem("tok_done"), 1)

        def choice_rows():
            dve.wait_ge(sem("S_done"), 1)
            link(V.tensor_scalar(T["keep"][:], T["rank"][:], float(CAP), None, ALU.is_lt))
            link(V.tensor_scalar(T["slot"][:], T["rank"][:], float(CAP - 1), None, ALU.min))
            link(V.tensor_tensor(T["slot"][:], T["slot"][:], iotaslot[:].unsqueeze(1).to_broadcast(bc), ALU.add))
            for c, (oh, kv_, ps_) in enumerate((("oh1", "k1", "p1"), ("oh2", "k2", "p2"))):
                link(V.tensor_tensor(T["t1"][:], T[oh][:], T["keep"][:], ALU.mult))
                link(V.tensor_reduce(rr[kv_][:, 0:NT], T["t1"][:], AXX, ALU.add))
                link(V.tensor_tensor(T["t2"][:], T[oh][:], T["slot"][:], ALU.mult))
                link(V.tensor_reduce(rr[ps_][:, 0:NT], T["t2"][:], AXX, ALU.add))
                link(V.tensor_copy(pos_u[:, c, 0:NT], rr[ps_][:, 0:NT]))
                link(V.tensor_tensor(rr[kv_][:, 0:NT], rr[kv_][:, 0:NT], rr["den"][:, 0:NT], ALU.mult))
                link(V.tensor_tensor(wts[:, c, 0:NT], rr[kv_][:, 0:NT], T["v8"][:, :, c], ALU.mult))

        dve.wait_ge(sem("turned_lo"), YT0 + 2 * NT)
        V.memset(PS[R0][0:CAP, :], 0.0).then_inc(sem("rd_clear"), 1)
        V.memset(PS[R0 + 1][0:CAP, :], 0.0).then_inc(sem("rd_clear"), 1)
        dve.wait_ge(sem("rd_clear"), 2)

        def routed_add(used, cleared):
            dve.wait_ge(sem("unit_used"), used)
            dve.wait_ge(sem("eout_clear"), cleared)
            for half in range(2):
                r = eout[:, half * HALF:(half + 1) * HALF]
                V.tensor_tensor(r, PS[R0 + half][0:CAP, :], r, ALU.add).then_inc(sem("rd_added"), 1)

        def choices_add(t0, t1):
            for t in range(t0, t1):
                for c in range(2):
                    dve.wait_ge(sem(f"g_in{c}_{t}"), 16)
                    link(V.scalar_tensor_tensor(out=resid[:, t, :], in0=got[c][t][:], scalar=wts[:, c, t:t + 1],
                                                in1=resid[:, t, :], op0=ALU.mult, op1=ALU.add))

        def step(e, q, order=STEP, routing=False):
            def lo(u):
                r, part = order.source(u)
                dve.wait_ge(sem("hi_done"), count(e, q, U, u + 1))
                V.tensor_tensor(order.view(c_lo[u % RING], u), part(raw[r % RAW]),
                                order.view(c_hi[u % RING], u).bitcast(F32), ALU.subtract).then_inc(sem("lo_done"), 1)

            def routed_inner(b):
                dve.wait_ge(sem("silu_done"), count(e, q, 6, order.silu_r + b + 1))
                V.tensor_tensor(r_h[b][:], PS[order.a_bank[b] + 1][0:CAP, :], r_silu[:], ALU.mult).then_inc(sem("h_done"), 1)

            def shared_inner(n):
                j, hf = divmod(n, 2)
                o, w = HALVES[hf]
                dve.wait_ge(sem("silu_done"), count(e, q, 6, order.silu_s + n + 1))
                V.tensor_tensor(s_h[hf][:, 0:w], PS[order.s_bank[n] + 1][:, 0:w], s_silu[hf][:, 0:w],
                                ALU.mult).then_inc(sem("sh_mult"), 1)
                dve.wait_ge(sem("sh_mult"), count(e, q, 4, n + 1 + ONE))
                V.tensor_copy(sh_hi[:, j, o:o + w], s_h[hf][:, 0:w]).then_inc(sem("sh_hi_done"), 1)
                dve.wait_ge(sem("sh_hi_done"), count(e, q, 4, n + 1))
                V.tensor_tensor(sh_lo[:, j, o:o + w], s_h[hf][:, 0:w], sh_hi[:, j, o:o + w].bitcast(F32),
                                ALU.subtract).then_inc(sem("sh_ready"), 1)

            def turned_lo(b):
                s = slice(b * 4 * CAP, (b + 1) * 4 * CAP)
                dve.wait_ge(sem("thi_done"), count(e, q, 2, b + 1))
                V.tensor_tensor(hT_lo[:, s], PS[T_BANK[b]][:, 0:4 * CAP], hT_hi[:, s].bitcast(F32),
                                ALU.subtract).then_inc(sem("tlo_done"), 1)

            def tokens_lo(half):
                s = slice(half * 4 * CAP, (half + 1) * 4 * CAP)
                dve.wait_ge(sem("xg_hi"), e * 2 + (half + 1))
                V.tensor_tensor(xgT_lo[:, s], PS[A0 + half][:, 0:4 * CAP], xgT_hi[:, s].bitcast(F32),
                                ALU.subtract).then_inc(sem("xgT_ready"), 1)

            def shared_add(n):
                t, half = divmod(n, 2)
                r = resid[:, t, half * HALF:(half + 1) * HALF]
                dve.wait_ge(sem("sd_done"), count(e, q, 2 * NT, n + 1))
                V.tensor_tensor(r, PS[X0 + n % 4][0:TP, :], r, ALU.add).then_inc(sem("sd_added"), 1)

            cleared = e + (1 if q == 0 else 2)
            if order is LAST:
                for u in range(10):
                    lo(u)
                for u in range(10, 16):
                    lo(u)
                routed_inner(0)
                for u in range(16, 21):
                    lo(u)
                turned_lo(0)
                routed_add(count(e, q, U, USED0), cleared)
                for u in range(21, 23):
                    lo(u)
                routed_inner(1)
                lo(23)
                turned_lo(1)
                for u in range(24, 30):
                    lo(u)
                routed_add(count(e, q, U, order.rd + 8 + USED0), cleared)
                shared_inner(0)
                shared_inner(1)
                choices_add(0, 2)
                shared_inner(2)
                choices_add(2, 3)
                shared_inner(3)
                for n in range(2 * NT):
                    if n >= 4 and n % 2 == 0 and n // 2 + 1 < NT:
                        choices_add(n // 2 + 1, n // 2 + 2)
                    shared_add(n)
                return
            if routing:
                lo(0)
                lo(1)
                routed_add(count(e, q, U, USED0), cleared)
                rsqrt_squares()
                choose()
                lo(2)
                lo(3)
                slots()
                shared_inner(0)
                slot_tokens()
                shared_inner(1)
                choice_rows()
                for u in range(4, 10):
                    lo(u)
                shared_inner(2)
            else:
                for u in range(10):
                    lo(u)
                routed_add(count(e, q, U, USED0), cleared)
                shared_inner(0)
                shared_inner(1)
            if q == 0:
                tokens_lo(0)
                tokens_lo(1)
            lo(10)
            lo(11)
            if not routing:
                shared_inner(2)
            shared_inner(3)
            for u in range(12, 22):
                lo(u)
            routed_inner(0)
            for u in range(22, 27):
                lo(u)
            shared_add(0)
            lo(27)
            turned_lo(0)
            shared_add(1)
            routed_inner(1)
            shared_add(2)
            lo(28)
            shared_add(3)
            lo(29)
            for n in range(4, 2 * NT):
                shared_add(n)
            turned_lo(1)

        for name in ("h_done", "sh_mult", "tlo_done", "sd_added"):
            dve.sem_inc(sem(name), ONE)

        for q in range(Q):
            step(0, q, routing=(q == 0))
        with dve.Fori(1, E - 1) as e:
            for q in range(Q):
                step(e, q)
        for q in range(Q):
            step(E - 1, q, LAST if q == Q - 1 else STEP)

    @block.tensor
    def _(pe):
        MM = nc.tensor.matmul
        TR = nc.tensor.transpose

        def count_group(gr):
            def chunk_ready(c):
                pe.wait_ge(sem("onehot"), gr * DVE_ONEHOTS + 2 * (c + 1) - sum(a <= c for a in ACT_CHUNKS))
                if c in ACT_CHUNKS:
                    pe.wait_ge(sem("onehot_act"), gr * len(ACT_CHUNKS) + ACT_CHUNKS.index(c) + 1)

            def count_chunk(c, dt):
                m = MM(PS[dt][0:TP, 0:SC], oh_d[c % SLOTS][:, dt * TP:(dt + 1) * TP], oh_s[c % SLOTS][:, 0:SC],
                       start=(c == 0), stop=(c == EG - 1))
                if c == EG - 1:
                    m.then_inc(sem("count_done"), 1)
                elif dt == NT - 1:
                    m.then_inc(sem("onehot_used"), 1)

            for c in range(EG - TOGETHER):
                chunk_ready(c)
                for dt in range(NT):
                    if c == 0 and not (isinstance(gr, int) and gr == 0):
                        pe.wait_ge(sem("count_out"), gr * NT - (NT - 1 - dt))
                    count_chunk(c, dt)
            for c in range(EG - TOGETHER, EG):
                chunk_ready(c)
            for dt in range(NT):
                for c in range(EG - TOGETHER, EG):
                    count_chunk(c, dt)
        count_group(0)
        with pe.Fori(1, NG) as gr:
            count_group(gr)

        def turn_tokens(n, src_, j):
            if n >= len(fill_banks(n)):
                pe.wait_ge(sem("turned_lo"), n + 1 - len(fill_banks(n)))
            for k in range(4):
                c = (4 * (j % 2) + k) * P
                m = TR(fill_bank(n)[:, k * TP:(k + 1) * TP], src_[:, c:c + P], ident[0:TP, 0:TP])
            m.then_inc(sem("turned"), 1)

        def turn(g, i):
            n = fill_w(g, i)
            ld = 2 + (g - G_K) // 2
            pe.wait_ge(sem(f"wl_in{ld % 2}"), 16 * (ld // 2 + 1))
            w = wl[ld % 2][:].rearrange("p (s k) -> p s k", s=4)
            pe.wait_ge(sem("turned_lo"), max(n - 1, 2 * NT))
            for k in range(2):
                for s in range(2):
                    m = TR(fill_bank(n)[:, k * GW + s * P:k * GW + (s + 1) * P],
                           w[:, 2 * (g % 2) + s, (2 * i + k) * P:(2 * i + k + 1) * P], ident[:])
            m.then_inc(sem("turned"), 1)

        def group_ready(g):
            if g < G_K:
                pe.wait_ge(sem("w_lo"), g + 1)
            else:
                pe.wait_ge(sem("turned_lo"), fill_w(g, 3) + 1)

        def project(g, t, l_hi, l_lo, bank):
            ts = slice(t * TP, (t + 1) * TP)
            ps = PS[bank][0:TP, (g % 2) * GW:(g % 2 + 1) * GW]
            for k in range(KT):
                MM(ps, l_hi[:, k, ts], wT_hi[g % 2][:, k, :], start=(k == 0), stop=False)
                MM(ps, l_hi[:, k, ts], wT_lo[g % 2][:, k, :], start=False, stop=False)
                m = MM(ps, l_lo[:, k, ts], wT_hi[g % 2][:, k, :], start=False, stop=(k == KT - 1))
            m.then_inc(sem("proj"), 1)

        pe.wait_ge(sem("const_done"), 1)
        for j in range(2 * NT):
            pe.wait_ge(sem("xn_done"), j // 2 + 1)
            turn_tokens(j, xn[:, j // 2, :], j)
        pe.wait_ge(sem("rw_in"), 16)
        pe.wait_ge(sem("turned_lo"), 2 * NT)
        for k in range(KT):
            m = TR(PS[7][:, k * E:(k + 1) * E], rw_in[:, k * P:(k + 1) * P], ident[0:E, 0:E])
        m.then_inc(sem("rwT_ps"), 1)
        pe.wait_ge(sem("count_out"), NG * NT)
        for g in range(G_K):
            group_ready(g)
            for t in range(NT):
                if g == 0:
                    pe.wait_ge(sem("turned_lo"), 2 * t + 2)
                if g == 2:
                    pe.wait_ge(sem("h_out"), t + 1)
                project(g, t, xnT_hi, xnT_lo, t)
                if g == G_K - 1 and t < 4:
                    turn(G_K, t)
        for g in range(G_K, G_V):
            group_ready(g)
            for t in range(NT):
                if g == G_K:
                    pe.wait_ge(sem("h_out"), NT + t + 1)
                if g == G_K + 2:
                    pe.wait_ge(sem("fe_used"), t + 1)
                project(g, t, xnT_hi, xnT_lo, t)
                if g == G_K + 1 and t == 0:
                    pe.wait_ge(sem("diag_done"), NT)
                    pe.wait_ge(sem("rwT_lo"), 1)
                    for s in range(4):
                        m = MM(PS[7][0:TP, s * TP:(s + 1) * TP], ones[0:TP, 0:TP], diag[:, s, :], start=True, stop=True)
                    m.then_inc(sem("albc_ps"), 1)
                if g == G_K + 1 and t == 1:
                    pe.wait_ge(sem("albc_out"), 1)
                    MM(PS[7][0:TP, 0:TP], ones[0:TP, 0:TP], diag[:, 4, :], start=True,
                       stop=True).then_inc(sem("albc_ps"), 1)
                if t < 4:
                    turn(g + 1, t)
        pe.wait_ge(sem("ez_used"), NT)
        pe.wait_ge(sem("albc_out"), 2)
        Cf = C[:].rearrange("p t c two -> p t (c two)")
        for j in range(2 * NT):
            t, half = divmod(j, 2)
            if j == 1:
                pe.wait_ge(sem("fe_used"), 2 * NT)
            if j >= 4:
                pe.wait_ge(sem("agg_used"), j - 3)
            for dt in range(NT):
                m = MM(PS[AGG_BANK[j % 4]][0:TP, :], Cf[:, dt, t * TP:(t + 1) * TP],
                       h[:, dt, half * HALF:(half + 1) * HALF], start=(dt == 0), stop=(dt == NT - 1))
            m.then_inc(sem("agg_ps"), 1)
            if j == 0:
                pe.wait_ge(sem("fe_used"), 2 * NT - 1)
                for s in range(NT):
                    for dt in range(NT):
                        m = MM(PS[3][0:TP, s:s + 1], Cf[:, dt, s * TP:(s + 1) * TP], ones[0:TP, 0:1],
                               start=(dt == 0), stop=(dt == NT - 1))
                m.then_inc(sem("rowsum_ps"), 1)
        for g in range(G_V, G_Q):
            group_ready(g)
            for t in range(NT):
                if g == G_V:
                    pe.wait_ge(sem("agg_used"), (1, 1, 7, 8, 10)[t])
                if g == G_V + 2:
                    pe.wait_ge(sem("v_out"), t + 1)
                project(g, t, xnT_hi, xnT_lo, V_BANK[t])
                if t < 4:
                    turn(g + 1, t)
        for n in range(2 * PAIRS):
            g, i = G_Q + n // 4, n % 4
            if i == 0:
                group_ready(g)
            if n in (1, 2):
                pe.wait_ge(sem("v_out"), 2 * NT + n - 2)
            if n == 3:
                pe.wait_ge(sem("KV_out"), 4 * len(TRIPLES))
            if n >= 6:
                pe.wait_ge(sem("fe_used"), FE_Q + n - 5)
            o, w = HALVES[n % 2]
            c = slice((i // 2) * P, (i // 2 + 1) * P)
            ps = PS[Q_BANK[n % 6]][:, 0:w]
            for k in range(KT):
                MM(ps, wT_hi[g % 2][:, k, c], xnT_hi[:, k, o:o + w], start=(k == 0), stop=False)
                MM(ps, wT_hi[g % 2][:, k, c], xnT_lo[:, k, o:o + w], start=False, stop=False)
                m = MM(ps, wT_lo[g % 2][:, k, c], xnT_hi[:, k, o:o + w], start=False, stop=(k == KT - 1))
            m.then_inc(sem("q_ps"), 1)
            for part in Q_PARTS[i]:
                turn(g + 1, part)
            if n == 1:
                pe.wait_ge(sem("v_out"), 2 * NT)
                pe.wait_ge(sem("v_ones"), 1)
                for b, (j0, cnt) in enumerate(TRIPLES):
                    for j in range(j0, j0 + cnt):
                        for t in range(NT):
                            m = MM(PS[KV_BANK[b]][:, (j - j0) * VW:(j - j0 + 1) * VW], kk[:, t, j * P:(j + 1) * P],
                                   vv[:, t, j, :], start=(t == 0), stop=(t == NT - 1))
                    m.then_inc(sem("KV_ps"), 1)
        for i in range(4):
            turn(G_OUT + 1, i)
        pe.wait_ge(sem("fe_used"), FE_Q + 2 * PAIRS)
        for t in range(NT + 1):
            if t < NT:
                if t >= 2:
                    pe.wait_ge(sem("att_done"), t - 1)
                for b, (j0, cnt) in zip(ATT_BANK[t % 2], TRIPLES):
                    for j in range(j0, j0 + cnt):
                        m = MM(PS[b][0:TP, (j - j0) * VW:(j - j0 + 1) * VW], qT[:, j, t * TP:(t + 1) * TP], KV[:, j, :],
                               start=True, stop=True)
                m.then_inc(sem("att_ps"), 1)
            if t >= 1:
                pe.wait_ge(sem("att_done"), t)
                for j in (2 * t - 2, 2 * t - 1):
                    turn_tokens(OUT0 + j, att[(t - 1) % 2], j)
        for g in range(G_OUT, G_OUT + 4):
            group_ready(g)
            for t in range(NT):
                if g == G_OUT:
                    pe.wait_ge(sem("turned_lo"), OUT0 + 2 * t + 2)
                if g == G_OUT + 2:
                    pe.wait_ge(sem("o_out"), t + 1)
                project(g, t, outT_hi, outT_lo, t)
                if g in (G_OUT + 1, G_OUT + 2) and t < 4:
                    turn(g + 1, t)
        for j in range(2 * NT):
            pe.wait_ge(sem("y_done"), j // 2 + 1)
            turn_tokens(YT0 + j, y[:, j // 2, :], j)
            if j == NT:
                pe.wait_ge(sem("o_out"), 2 * NT)
                pe.sem_inc(sem("unit_used"), USED0)
        pe.wait_ge(sem("turned_lo"), YT0 + 2 * NT)
        pe.wait_ge(sem("o_out"), 2 * NT)
        pe.wait_ge(sem("const_done"), 1)
        for hf, (o, w) in enumerate(HALVES):
            for k in range(KT):
                lw = rwT[:, k * 2 * E:k * 2 * E + P]
                MM(PS[hf][:, 0:w], lw, yT_hi[:, k, o:o + w], start=(k == 0), stop=False)
                m = MM(PS[hf][:, 0:w], lw, yT_lo[:, k, o:o + w], start=False, stop=(k == KT - 1))
            m.then_inc(sem("lgT_ps"), 1)
        pe.wait_ge(sem("lgT_out"), 2)
        for t in range(NT):
            m = TR(PS[4][0:TP, t * 2 * E:(t + 1) * 2 * E], lgT[:, t * TP:(t + 1) * TP], ident[0:2 * E, 0:2 * E])
        m.then_inc(sem("lg_ps"), 1)
        def ranks():
            pe.wait_ge(sem("mask_done"), 1)
            for t in range(NT):
                for s in range(t + 1):
                    m = MM(PS[RANK_BANK][0:TP, t * E:(t + 1) * E], (tri if s == t else ones_b)[0:TP, 0:TP], mask[:, s, :],
                           start=(s == 0), stop=(s == t))
            m.then_inc(sem("rank_ps"), 1)

        def slot_tokens():
            pe.wait_ge(sem("S_done"), 1)
            for e in range(E):
                for t in range(NT):
                    m = MM(PS[TOK_BANK][0:CAP, 2 * e:2 * e + 2], S[:, t, e, :], tok_b[:, t, :],
                           start=(t == 0), stop=(t == NT - 1))
            m.then_inc(sem("tok_ps"), 1)

        def step(e, q, order=STEP, routing=False):
            def split(u):
                pe.wait_ge(sem("lo_done"), count(e, q, U, U + u + 1))

            def three(out_, l_hi, l_lo, r_hi, r_lo, first, last):
                MM(out_, l_hi, r_hi, start=first, stop=False)
                MM(out_, l_hi, r_lo, start=False, stop=False)
                return MM(out_, l_lo, r_hi, start=False, stop=last)

            def routed_up(b, parts=(0, 1)):
                for i in parts:
                    for k in range(KT):
                        u = order.gate[b] + 4 * i + k // 2
                        if k % 2 == 0:
                            split(u)
                        c = slice((k % 2) * HALF, (k % 2 + 1) * HALF)
                        xs = slice(k * CAP, (k + 1) * CAP)
                        m = three(PS[order.a_bank[b] + i][0:CAP, :], xgT_hi[:, xs], xgT_lo[:, xs],
                                  c_hi[u % RING][:, c], c_lo[u % RING][:, c], k == 0, k == KT - 1)
                        if k % 2:
                            m.then_inc(sem("unit_used"), 1)

            def shared_up(n):
                j, hf = divmod(n, 2)
                o, w = HALVES[hf]
                for i in range(2):
                    u = order.s + 2 * j + i
                    split(u)
                    for k in range(KT):
                        c = slice(k * P, (k + 1) * P)
                        m = three(PS[order.s_bank[n] + i][:, 0:w], c_hi[u % RING][:, c], c_lo[u % RING][:, c],
                                  yT_hi[:, k, o:o + w], yT_lo[:, k, o:o + w], k == 0, k == KT - 1)
                    if hf:
                        m.then_inc(sem("unit_used"), 1)
                if not hf:
                    m.then_inc(sem("s_half"), 1)

            def turn_inner(b):
                for k in range(4):
                    m = TR(PS[T_BANK[b]][:, k * CAP:(k + 1) * CAP], r_h[b][:, k * P:(k + 1) * P],
                           ident[0:CAP, 0:CAP])
                    if b == 1 and k == 0 and order is STEP:
                        m.then_inc(sem("unit_used"), 1)
                m.then_inc(sem("t_done"), 1)

            def turn_expert():
                pe.wait_ge(sem("xg_in"), e * 16 + 16)
                pe.wait_ge(sem("tlo_done"), count(e, q, 2, ONE))
                for half in range(2):
                    for k in range(4):
                        c = (4 * half + k) * P
                        m = TR(PS[A0 + half][:, k * CAP:(k + 1) * CAP], xg[:, c:c + P], ident[0:CAP, 0:CAP])
                    m.then_inc(sem("xgT_ps"), 1)

            def shared_down(n, tiles=(0, 1)):
                t, half = divmod(n, 2)
                if n >= 4:
                    pe.wait_ge(sem("sd_added"), count(e, q, 2 * NT, n - 3 + ONE))
                c = slice(half * HALF, (half + 1) * HALF)
                for j in tiles:
                    u = order.sd + j
                    split(u)
                    ts = slice(t * TP, (t + 1) * TP)
                    m = three(PS[X0 + n % 4][0:TP, :], sh_hi[:, j, ts], sh_lo[:, j, ts],
                              c_hi[u % RING][:, c], c_lo[u % RING][:, c], j == 0, j == 1)
                    if n == 2 * NT - 1 and j == 0:
                        m.then_inc(sem("unit_used"), 1)
                if 1 in tiles:
                    m.then_inc(sem("sd_done"), 1)

            def routed_down(k0, k1):
                for k in range(k0, k1):
                    u = order.rd + k
                    if k % 4 == 0:
                        pe.wait_ge(sem("tlo_done"), count(e, q, 2, k // 4 + 1 + ONE))
                    split(u)
                    xs = slice(k * CAP, (k + 1) * CAP)
                    for half in range(2):
                        c = slice(half * HALF, (half + 1) * HALF)
                        m = three(PS[R0 + half][0:CAP, :], hT_hi[:, xs], hT_lo[:, xs],
                                  c_hi[u % RING][:, c], c_lo[u % RING][:, c], k == 0, k == 7)
                    m.then_inc(sem("unit_used"), 1)

            if order is LAST:
                pe.wait_ge(sem("tlo_done"), count(e, q, 2, ONE))
                routed_up(0)
                pe.wait_ge(sem("sd_added"), count(e, q, 2 * NT, ONE))
                routed_up(1, (0,))
                pe.wait_ge(sem("h_done"), count(e, q, 2, 1 + ONE))
                turn_inner(0)
                routed_up(1, (1,))
                pe.wait_ge(sem("rd_added"), count(e, q, 2, 2))
                routed_down(0, 2)
                pe.wait_ge(sem("h_done"), count(e, q, 2, 2 + ONE))
                turn_inner(1)
                routed_down(2, 8)
                shared_up(0)
                shared_up(1)
                pe.wait_ge(sem("rd_added"), count(e, q, 2, 4))
                shared_up(2)
                shared_up(3)
                pe.wait_ge(sem("sh_ready"), count(e, q, 4, 2))
                for n in range(4):
                    shared_down(n, (0,))
                pe.wait_ge(sem("sh_ready"), count(e, q, 4, 4))
                for n in range(2 * NT):
                    shared_down(n, (1,) if n < 4 else (0, 1))
                return
            pe.wait_ge(sem("sd_added"), count(e, q, 2 * NT, ONE))
            shared_up(0)
            if routing:
                ranks()
            shared_up(1)
            if routing:
                slot_tokens()
            elif q == 0:
                turn_expert()
            pe.wait_ge(sem("rd_added"), count(e, q, 2, 2))
            shared_up(2)
            if routing:
                turn_expert()
            pe.wait_ge(sem("sh_mult"), count(e, q, 4, 1 + ONE))
            shared_up(3)
            pe.wait_ge(sem("xgT_ready"), e * 2 + 2)
            pe.wait_ge(sem("tlo_done"), count(e, q, 2, ONE))
            routed_up(0)
            pe.wait_ge(sem("sh_mult"), count(e, q, 4, 3 + ONE))
            routed_up(1)
            pe.wait_ge(sem("h_done"), count(e, q, 2, 1 + ONE))
            turn_inner(0)
            pe.wait_ge(sem("sh_ready"), count(e, q, 4, 4))
            for n in range(2 * NT):
                shared_down(n)
            pe.wait_ge(sem("h_done"), count(e, q, 2, 2 + ONE))
            turn_inner(1)
            routed_down(0, 8)

        for q in range(Q):
            step(0, q, routing=(q == 0))
        with pe.Fori(1, E - 1) as e:
            for q in range(Q):
                step(e, q)
        for q in range(Q):
            step(E - 1, q, LAST if q == Q - 1 else STEP)
    ctx.close()


_INS = ["x", "src", "dst", "L0_gnn_W", "L0_gnn_a", "L0_mix_w_qkv", "L0_mix_w_out", "L0_mix_b_out",
        "L0_ffn_router_w", "L0_ffn_rg", "L0_ffn_ru", "L0_ffn_rd", "L0_ffn_sg", "L0_ffn_su", "L0_ffn_sd"]


def kernel(**inputs):
    import numpy as _np
    import concourse.bacc as _bacc
    from concourse import mybir as _mybir
    from concourse.bass_utils import run_bass_kernel_spmd as _run

    nc = _bacc.Bacc("TRN2", target_bir_lowering=False, num_devices=1)
    arrays, args = {}, []
    for name in _INS:
        v = _np.ascontiguousarray(inputs[name])
        arrays[f"in_{name}"] = v
        args.append(nc.dram_tensor(f"in_{name}", v.shape, _mybir.dt.from_np(v.dtype), kind="ExternalInput").ap())
    res = nc.dram_tensor("out_0", (N, D), _mybir.dt.float32, kind="ExternalOutput").ap()
    build(nc, *args, res)
    r = _run(nc, [arrays], core_ids=[0])
    return r.results[0]["out_0"]
```
